# Optimizing a Trainium2 kernel written in Bass

```python
import numpy as np
import jax
import jax.numpy as jnp

def _softmax(x, axis=-1):
    return jax.nn.softmax(x, axis=axis)

def _gelu(x):
    return jax.nn.gelu(x, approximate=True)

def _silu(x):
    return jax.nn.silu(x)

def _sigmoid(x):
    return jax.nn.sigmoid(x)

def _layernorm(x, axis=-1, eps=1e-05):
    m = jnp.mean(x, axis=axis, keepdims=True)
    v = jnp.var(x, axis=axis, keepdims=True)
    return (x - m) / jnp.sqrt(v + eps)

def _scatter_add(tgt, idx, src, axis=0):
    return tgt.at[idx].add(src)

def _segment_sum(src, seg, n):
    return jax.ops.segment_sum(src, seg, n)
kernel_name = 'mk_prb_d4_jaxref_r8_5912fc'

def setup_inputs(seed: int=0):
    np.random.seed(seed)
    _w = jnp.asarray

    def _L0_attn_setup():
        import jax, jax.numpy as jnp
        import numpy as np
        B, L, D = (4, 512, 128)
        EPS_NORM = 1e-06
        EPS_PHAZOR = 1e-05
        key = jax.random.key(seed)
        ks = jax.random.split(key, 8)
        gain = 0.01 * np.sqrt(2.0 / (D + D))
        inp = {'x': jax.random.normal(ks[0], (B, L, D), dtype=jnp.float32), 'Wz': jax.random.normal(ks[1], (D, D), dtype=jnp.float32) * gain, 'bz': jnp.zeros((D,), jnp.float32), 'Wza': jax.random.normal(ks[2], (D, D), dtype=jnp.float32) * gain, 'bza': jnp.zeros((D,), jnp.float32), 'Wy': jax.random.normal(ks[3], (D, D), dtype=jnp.float32) * gain, 'by': jnp.zeros((D,), jnp.float32), 'Wya': jax.random.normal(ks[4], (D, D), dtype=jnp.float32) * gain, 'bya': jnp.zeros((D,), jnp.float32), 'norm_w': jnp.ones((D,), jnp.float32), 'lc_re': jax.random.normal(ks[5], (D,), dtype=jnp.float32), 'lc_im': jax.random.normal(ks[6], (D,), dtype=jnp.float32)}
        return inp
    _L0_attn_in = _L0_attn_setup()

    def _L0_ffn_setup():
        import jax, jax.numpy as jnp
        import numpy as np
        B, S, H = (4, 256, 128)
        E, K = (8, 2)
        I_R, I_S = (4 * H, 8 * H)
        CAP_FACTOR = 1.25
        SCALE = 1.0
        key = jax.random.key(seed)
        ks = jax.random.split(key, 9)
        std = 0.02
        return {'x': jax.random.normal(ks[0], (B, S, H), jnp.float32), 'router_w': std * jax.random.normal(ks[1], (E, H), jnp.float32), 'rg': std * jax.random.normal(ks[2], (E, H, I_R), jnp.float32), 'ru': std * jax.random.normal(ks[3], (E, H, I_R), jnp.float32), 'rd': std * jax.random.normal(ks[4], (E, I_R, H), jnp.float32), 'sg': std * jax.random.normal(ks[5], (H, I_S), jnp.float32), 'su': std * jax.random.normal(ks[6], (H, I_S), jnp.float32), 'sd': std * jax.random.normal(ks[7], (I_S, H), jnp.float32)}
    _L0_ffn_in = _L0_ffn_setup()

    def _L1_attn_setup():
        import jax, jax.numpy as jnp
        import numpy as np
        import math
        N_EMBD = 128
        N_HEAD = 16
        HEAD_DIM = N_EMBD // N_HEAD
        BLOCK_SIZE = 256
        ROPE_BASE = 10000.0
        B, T = (4, 256)

        def _rope_cache(n_pos):
            theta = 1.0 / ROPE_BASE ** (jnp.arange(0, HEAD_DIM, 2, dtype=jnp.float32) / HEAD_DIM)
            idx_theta = jnp.arange(n_pos, dtype=jnp.float32)[:, None] * theta[None, :]
            return (jnp.cos(idx_theta), jnp.sin(idx_theta))

        def _apply_rope(x):
            cos, sin = _rope_cache(x.shape[1])
            cos = cos[None, :, None, :]
            sin = sin[None, :, None, :]
            xs = x.reshape(*x.shape[:-1], HEAD_DIM // 2, 2)
            x0, x1 = (xs[..., 0], xs[..., 1])
            out = jnp.stack([x0 * cos - x1 * sin, x1 * cos + x0 * sin], axis=-1)
            return out.reshape(x.shape)
        key = jax.random.key(seed)
        ks = jax.random.split(key, 5)
        x = jax.random.normal(ks[0], (B, T, N_EMBD), dtype=jnp.float32)
        s1 = 1.0 / math.sqrt(N_EMBD)
        W_attn = jax.random.uniform(ks[1], (N_EMBD, 3 * N_EMBD), jnp.float32, -s1, s1)
        b_attn = jax.random.uniform(ks[2], (3 * N_EMBD,), jnp.float32, -s1, s1)
        W_proj = jax.random.uniform(ks[3], (N_EMBD, N_EMBD), jnp.float32, -s1, s1)
        b_proj = jax.random.uniform(ks[4], (N_EMBD,), jnp.float32, -s1, s1)
        return {'x': x, 'W_attn': W_attn, 'b_attn': b_attn, 'W_proj': W_proj, 'b_proj': b_proj}
    _L1_attn_in = _L1_attn_setup()

    def _L1_ffn_setup():
        import jax, jax.numpy as jnp
        import numpy as np
        D_IN, D_HID = (128, 512)

        def _ternary(key, shape):
            return jax.random.randint(key, shape, -1, 2).astype(jnp.float32)

        def _tlin(x, w, s):
            return jnp.einsum('bsi,oi->bso', x, w) * s
        key = jax.random.key(seed)
        ks = jax.random.split(key, 12)
        inv = lambda fan: 1.0 / np.sqrt(fan).astype(np.float32)
        return {'x': jax.random.normal(ks[0], (4, 256, D_IN), dtype=jnp.float32), 'w1_w': _ternary(ks[1], (D_HID, D_IN)), 'w1_s': jax.random.uniform(ks[2], (D_HID,), dtype=jnp.float32) * inv(D_IN), 'w2_w': _ternary(ks[3], (D_HID, D_IN)), 'w2_s': jax.random.uniform(ks[4], (D_HID,), dtype=jnp.float32) * inv(D_IN), 'h1_w': _ternary(ks[5], (D_HID, D_HID)), 'h1_s': jax.random.uniform(ks[6], (D_HID,), dtype=jnp.float32) * inv(D_HID), 'h2_w': _ternary(ks[7], (D_HID, D_HID)), 'h2_s': jax.random.uniform(ks[8], (D_HID,), dtype=jnp.float32) * inv(D_HID), 'w3_w': _ternary(ks[9], (D_IN, D_HID)), 'w3_s': jax.random.uniform(ks[10], (D_IN,), dtype=jnp.float32) * inv(D_HID)}
    _L1_ffn_in = _L1_ffn_setup()

    def _L2_attn_setup():
        import jax, jax.numpy as jnp
        import numpy as np
        D = 128
        H = 16
        N = D // H
        B = 4
        T = 256
        NLAYERS = 12
        LAYER_ID = 6
        EPS = 1e-05 * 64

        def _forward(x, w_r, w_k, w_v, w_g, w_o, time_maa_k, time_maa_v, time_maa_r, time_maa_g, time_decay, time_faaaa, ln_g, ln_b):
            Bs, Ts, C = x.shape
            if Ts % 32 == 0:
                Q = 32
            elif Ts % 128 == 0:
                Q = 128
            else:
                Q = Ts
            nC = Ts // Q
            xs = jnp.pad(x, ((0, 0), (1, 0), (0, 0)))[:, :-1]
            xx = xs - x
            xk = x + xx * time_maa_k
            xv = x + xx * time_maa_v
            xr = x + xx * time_maa_r
            xg = x + xx * time_maa_g
            r = (xr @ w_r.T).reshape(Bs, Ts, H, N).transpose(0, 2, 1, 3)
            k = (xk @ w_k.T).reshape(Bs, Ts, H, N).transpose(0, 2, 3, 1)
            v = (xv @ w_v.T).reshape(Bs, Ts, H, N).transpose(0, 2, 1, 3)
            g = jax.nn.silu(xg @ w_g.T)
            w = jnp.exp(-jnp.exp(time_decay))
            u = time_faaaa
            ws = (w ** Q)[None, :, None, None]
            q = jnp.arange(Q)
            wk = (w[:, None] ** (Q - 1 - q)[None, :])[None, :, None, :]
            wb = (w[:, None] ** q[None, :])[None, :, :, None]
            ii = q[:, None]
            jj = q[None, :]
            e = jnp.maximum(ii - jj - 1, 0)
            Wmat = jnp.where((jj < ii)[None], w[:, None, None] ** e[None], 0.0)
            Wmat = Wmat + jnp.eye(Q, dtype=x.dtype)[None] * u[:, None, None]
            Wmat = Wmat[None]
            rC = r.reshape(Bs, H, nC, Q, N).transpose(2, 0, 1, 3, 4)
            kC = k.reshape(Bs, H, N, nC, Q).transpose(3, 0, 1, 2, 4)
            vC = v.reshape(Bs, H, nC, Q, N).transpose(2, 0, 1, 3, 4)

            def step(state, inp):
                rr, kk, vv = inp
                y = rr @ kk * Wmat @ vv + rr @ state * wb
                state = ws * state + kk * wk @ vv
                return (state, y)
            state0 = jnp.zeros((Bs, H, N, N), x.dtype)
            _, yC = jax.lax.scan(step, state0, (rC, kC, vC))
            y = yC.transpose(1, 2, 0, 3, 4).reshape(Bs, H, Ts, N)
            y = y.transpose(0, 2, 1, 3).reshape(Bs * Ts, H, N)
            mu = y.mean(-1, keepdims=True)
            var = y.var(-1, keepdims=True)
            y = (y - mu) / jnp.sqrt(var + EPS)
            y = y.reshape(Bs, Ts, C) * ln_g + ln_b
            y = y * g
            return y @ w_o.T
        key = jax.random.key(seed)
        ks = jax.random.split(key, 6)
        r01 = LAYER_ID / (NLAYERS - 1)
        r10 = 1.0 - LAYER_ID / NLAYERS
        ddd = np.arange(D, dtype=np.float64) / D
        maa_k = (1.0 - ddd ** r10).astype(np.float32)
        maa_v = (1.0 - (ddd ** r10 + 0.3 * r01)).astype(np.float32)
        maa_r = (1.0 - ddd ** (0.5 * r10)).astype(np.float32)
        maa_g = maa_r.copy()
        hh = np.arange(H, dtype=np.float64)
        decay = (-6.0 + 5.0 * (hh / (H - 1)) ** (0.7 + 1.3 * r01)).astype(np.float32)
        faaaa = (r01 * (1.0 - hh / (H - 1))).astype(np.float32)
        s = 0.02
        return {'x': jax.random.normal(ks[0], (B, T, D), jnp.float32), 'w_r': jax.random.normal(ks[1], (D, D), jnp.float32) * s, 'w_k': jax.random.normal(ks[2], (D, D), jnp.float32) * s, 'w_v': jax.random.normal(ks[3], (D, D), jnp.float32) * s, 'w_g': jax.random.normal(ks[4], (D, D), jnp.float32) * s, 'w_o': jax.random.normal(ks[5], (D, D), jnp.float32) * s, 'time_maa_k': jnp.asarray(maa_k), 'time_maa_v': jnp.asarray(maa_v), 'time_maa_r': jnp.asarray(maa_r), 'time_maa_g': jnp.asarray(maa_g), 'time_decay': jnp.asarray(decay), 'time_faaaa': jnpp if False else jnp.asarray(faaaa), 'ln_g': jnp.ones((D,), jnp.float32), 'ln_b': jnp.zeros((D,), jnp.float32)}
    _L2_attn_in = _L2_attn_setup()

    def _L2_ffn_setup():
        import jax, jax.numpy as jnp
        import numpy as np
        NUM_EXPERTS = 8
        IN_FEATURES = 128
        HIDDEN_FEATURES = 512
        GATE_DIM = 16
        EPS = 0.0001
        key = jax.random.key(seed)
        ks = jax.random.split(key, 7)
        hidden_states = jax.random.normal(ks[0], (1, 256, IN_FEATURES), dtype=jnp.float32)
        wg_red = jax.random.normal(ks[1], (GATE_DIM, IN_FEATURES), dtype=jnp.float32) * 0.02
        wg = jax.random.normal(ks[2], (NUM_EXPERTS, GATE_DIM), dtype=jnp.float32)
        w1 = jax.random.uniform(ks[3], (NUM_EXPERTS, IN_FEATURES, HIDDEN_FEATURES), dtype=jnp.float32)
        b1 = jax.random.uniform(ks[4], (NUM_EXPERTS, HIDDEN_FEATURES), dtype=jnp.float32)
        w2 = jax.random.uniform(ks[5], (NUM_EXPERTS, HIDDEN_FEATURES, IN_FEATURES), dtype=jnp.float32)
        b2 = jax.random.uniform(ks[6], (NUM_EXPERTS, IN_FEATURES), dtype=jnp.float32)
        return {'hidden_states': hidden_states, 'wg_red': wg_red, 'wg': wg, 'w1': w1, 'b1': b1, 'w2': w2, 'b2': b2}
    _L2_ffn_in = _L2_ffn_setup()

    def _L3_attn_setup():
        import jax, jax.numpy as jnp
        import numpy as np
        KEY_DIM = 128
        EMBED_DIM = 128
        key = jax.random.key(seed)
        kx, kw = jax.random.split(key)
        x = jax.random.normal(kx, (4, 256, EMBED_DIM), dtype=jnp.float32)
        W = jax.random.normal(kw, (EMBED_DIM, 3 * KEY_DIM), dtype=jnp.float32)
        return {'x': x, 'W': W}
    _L3_attn_in = _L3_attn_setup()

    def _L3_ffn_setup():
        import jax, jax.numpy as jnp
        import numpy as np
        B, S, D = (4, 256, 128)
        E, H, TOP_K = (8, 256, 2)
        key = jax.random.key(seed)
        k_x, k_g, k_w1, k_w2, k_w3 = jax.random.split(key, 5)
        s_d = 1.0 / np.sqrt(D)
        s_h = 1.0 / np.sqrt(H)
        return {'x': jax.random.normal(k_x, (B, S, D), dtype=jnp.float32), 'w_gate': jax.random.normal(k_g, (D, E), dtype=jnp.float32) * s_d, 'w1': jax.random.normal(k_w1, (E, D, H), dtype=jnp.float32) * s_d, 'w3': jax.random.normal(k_w3, (E, D, H), dtype=jnp.float32) * s_d, 'w2': jax.random.normal(k_w2, (E, H, D), dtype=jnp.float32) * s_h}
    _L3_ffn_in = _L3_ffn_setup()
    _d = {'L0_attn_x': _L0_attn_in['x'], 'L0_attn_Wz': _L0_attn_in['Wz'], 'L0_attn_bz': _L0_attn_in['bz'], 'L0_attn_Wza': _L0_attn_in['Wza'], 'L0_attn_bza': _L0_attn_in['bza'], 'L0_attn_Wy': _L0_attn_in['Wy'], 'L0_attn_by': _L0_attn_in['by'], 'L0_attn_Wya': _L0_attn_in['Wya'], 'L0_attn_bya': _L0_attn_in['bya'], 'L0_attn_norm_w': _L0_attn_in['norm_w'], 'L0_attn_lc_re': _L0_attn_in['lc_re'], 'L0_attn_lc_im': _L0_attn_in['lc_im'], 'L0_ffn_router_w': _L0_ffn_in['router_w'], 'L0_ffn_rg': _L0_ffn_in['rg'], 'L0_ffn_ru': _L0_ffn_in['ru'], 'L0_ffn_rd': _L0_ffn_in['rd'], 'L0_ffn_sg': _L0_ffn_in['sg'], 'L0_ffn_su': _L0_ffn_in['su'], 'L0_ffn_sd': _L0_ffn_in['sd'], 'L1_attn_W_attn': _L1_attn_in['W_attn'], 'L1_attn_b_attn': _L1_attn_in['b_attn'], 'L1_attn_W_proj': _L1_attn_in['W_proj'], 'L1_attn_b_proj': _L1_attn_in['b_proj'], 'L1_ffn_w1_w': _L1_ffn_in['w1_w'], 'L1_ffn_w1_s': _L1_ffn_in['w1_s'], 'L1_ffn_w2_w': _L1_ffn_in['w2_w'], 'L1_ffn_w2_s': _L1_ffn_in['w2_s'], 'L1_ffn_h1_w': _L1_ffn_in['h1_w'], 'L1_ffn_h1_s': _L1_ffn_in['h1_s'], 'L1_ffn_h2_w': _L1_ffn_in['h2_w'], 'L1_ffn_h2_s': _L1_ffn_in['h2_s'], 'L1_ffn_w3_w': _L1_ffn_in['w3_w'], 'L1_ffn_w3_s': _L1_ffn_in['w3_s'], 'L2_attn_w_r': _L2_attn_in['w_r'], 'L2_attn_w_k': _L2_attn_in['w_k'], 'L2_attn_w_v': _L2_attn_in['w_v'], 'L2_attn_w_g': _L2_attn_in['w_g'], 'L2_attn_w_o': _L2_attn_in['w_o'], 'L2_attn_time_maa_k': _L2_attn_in['time_maa_k'], 'L2_attn_time_maa_v': _L2_attn_in['time_maa_v'], 'L2_attn_time_maa_r': _L2_attn_in['time_maa_r'], 'L2_attn_time_maa_g': _L2_attn_in['time_maa_g'], 'L2_attn_time_decay': _L2_attn_in['time_decay'], 'L2_attn_time_faaaa': _L2_attn_in['time_faaaa'], 'L2_attn_ln_g': _L2_attn_in['ln_g'], 'L2_attn_ln_b': _L2_attn_in['ln_b'], 'L2_ffn_wg_red': _L2_ffn_in['wg_red'], 'L2_ffn_wg': _L2_ffn_in['wg'], 'L2_ffn_w1': _L2_ffn_in['w1'], 'L2_ffn_b1': _L2_ffn_in['b1'], 'L2_ffn_w2': _L2_ffn_in['w2'], 'L2_ffn_b2': _L2_ffn_in['b2'], 'L3_attn_W': _L3_attn_in['W'], 'L3_ffn_w_gate': _L3_ffn_in['w_gate'], 'L3_ffn_w1': _L3_ffn_in['w1'], 'L3_ffn_w3': _L3_ffn_in['w3'], 'L3_ffn_w2': _L3_ffn_in['w2']}
    _x0 = _d['L0_attn_x']
    _d['L0_attn_x'] = jax.random.normal(jax.random.fold_in(jax.random.key(seed), 1), (8, 256, 128), dtype=_x0.dtype)
    del _x0
    return _d

def reference(L0_attn_x, L0_attn_Wz, L0_attn_bz, L0_attn_Wza, L0_attn_bza, L0_attn_Wy, L0_attn_by, L0_attn_Wya, L0_attn_bya, L0_attn_norm_w, L0_attn_lc_re, L0_attn_lc_im, L0_ffn_router_w, L0_ffn_rg, L0_ffn_ru, L0_ffn_rd, L0_ffn_sg, L0_ffn_su, L0_ffn_sd, L1_attn_W_attn, L1_attn_b_attn, L1_attn_W_proj, L1_attn_b_proj, L1_ffn_w1_w, L1_ffn_w1_s, L1_ffn_w2_w, L1_ffn_w2_s, L1_ffn_h1_w, L1_ffn_h1_s, L1_ffn_h2_w, L1_ffn_h2_s, L1_ffn_w3_w, L1_ffn_w3_s, L2_attn_w_r, L2_attn_w_k, L2_attn_w_v, L2_attn_w_g, L2_attn_w_o, L2_attn_time_maa_k, L2_attn_time_maa_v, L2_attn_time_maa_r, L2_attn_time_maa_g, L2_attn_time_decay, L2_attn_time_faaaa, L2_attn_ln_g, L2_attn_ln_b, L2_ffn_wg_red, L2_ffn_wg, L2_ffn_w1, L2_ffn_b1, L2_ffn_w2, L2_ffn_b2, L3_attn_W, L3_ffn_w_gate, L3_ffn_w1, L3_ffn_w3, L3_ffn_w2):

    def _L0_attn_ref(x, Wz, bz, Wza, bza, Wy, by, Wya, bya, norm_w, lc_re, lc_im):
        import jax, jax.numpy as jnp
        import numpy as np
        B, L, D = (4, 512, 128)
        EPS_NORM = 1e-06
        EPS_PHAZOR = 1e-05
        b, l, d = x.shape
        scale = jnp.power(jnp.float32(0.001), jnp.linspace(0.0, 1.0, d, dtype=jnp.float32))
        ln_phazor = EPS_PHAZOR + 1j * scale.astype(jnp.complex64)
        z = (x @ Wz.T + bz) * jax.nn.silu(x @ Wza.T + bza)
        z = z.astype(jnp.complex64)
        t = jnp.arange(l, dtype=jnp.float32)
        phazor_prog = jnp.exp(t[:, None].astype(jnp.complex64) * ln_phazor[None, :])
        phazor_fft = jnp.fft.fft(phazor_prog, n=2 * l, axis=0)
        z_fft = jnp.fft.fft(z, n=2 * l, axis=1)
        h_inner = jnp.fft.ifft(z_fft * phazor_fft[None], axis=1)[:, :l]
        last_conv = (lc_re + 1j * lc_im).astype(jnp.complex64)
        h_cross = last_conv[None, None, :] * (phazor_prog * jnp.exp(ln_phazor)[None, :])[None]
        h = (h_inner + h_cross).real
        normed = h * jax.lax.rsqrt(jnp.mean(h * h, axis=-1, keepdims=True) + EPS_NORM) * norm_w
        y = (normed @ Wy.T + by) * jax.nn.silu(x @ Wya.T + bya)
        return y

    def _L0_ffn_ref(x, router_w, rg, ru, rd, sg, su, sd):
        import jax, jax.numpy as jnp
        import numpy as np
        B, S, H = (4, 256, 128)
        E, K = (8, 2)
        I_R, I_S = (4 * H, 8 * H)
        CAP_FACTOR = 1.25
        SCALE = 1.0
        b, s, h = x.shape
        T = b * s
        capacity = max(int(CAP_FACTOR * T / E), 1)
        xf = x.reshape(T, h)
        eps = jnp.finfo(x.dtype).eps
        xn = xf * jax.lax.rsqrt(jnp.mean(xf * xf, axis=-1, keepdims=True) + eps)
        logits = xn @ router_w.T
        probs = jax.nn.softmax(logits, axis=-1)
        topk_p, topk_i = jax.lax.top_k(probs, K)
        rw = topk_p / jnp.sum(topk_p, axis=-1, keepdims=True)
        one_hot = jax.nn.one_hot(topk_i, E, dtype=x.dtype)
        mask = one_hot.sum(1)
        wdense = (one_hot * rw[..., None]).sum(1)
        sel = mask.T.astype(bool)
        order = jnp.argsort(~sel, axis=1, stable=True)
        dispatch = order[:, :capacity]
        count = sel.sum(axis=1)
        valid = (jnp.arange(capacity)[None, :] < count[:, None]).astype(x.dtype)
        xg = xf[dispatch]
        gate = jax.nn.silu(jnp.einsum('ech,ehi->eci', xg, rg))
        up = jnp.einsum('ech,ehi->eci', xg, ru)
        eout = jnp.einsum('eci,eih->ech', gate * up, rd)
        w = jnp.take_along_axis(wdense.T, dispatch, axis=1)
        contrib = eout * (w * valid)[..., None]
        routed = jnp.zeros_like(xf).at[dispatch.reshape(-1)].add(contrib.reshape(-1, h))
        shared = jax.nn.silu(x @ sg) * (x @ su) @ sd
        return shared + SCALE * routed.reshape(b, s, h)

    def _L1_attn_ref(x, W_attn, b_attn, W_proj, b_proj):
        import jax, jax.numpy as jnp
        import numpy as np
        import math
        N_EMBD = 128
        N_HEAD = 16
        HEAD_DIM = N_EMBD // N_HEAD
        BLOCK_SIZE = 256
        ROPE_BASE = 10000.0
        B, T = (4, 256)

        def _rope_cache(n_pos):
            theta = 1.0 / ROPE_BASE ** (jnp.arange(0, HEAD_DIM, 2, dtype=jnp.float32) / HEAD_DIM)
            idx_theta = jnp.arange(n_pos, dtype=jnp.float32)[:, None] * theta[None, :]
            return (jnp.cos(idx_theta), jnp.sin(idx_theta))

        def _apply_rope(x):
            cos, sin = _rope_cache(x.shape[1])
            cos = cos[None, :, None, :]
            sin = sin[None, :, None, :]
            xs = x.reshape(*x.shape[:-1], HEAD_DIM // 2, 2)
            x0, x1 = (xs[..., 0], xs[..., 1])
            out = jnp.stack([x0 * cos - x1 * sin, x1 * cos + x0 * sin], axis=-1)
            return out.reshape(x.shape)
        Bx, Tx, C = x.shape
        qkv = jnp.einsum('btc,cd->btd', x, W_attn) + b_attn
        q, k, v = jnp.split(qkv, 3, axis=2)
        q = q.reshape(Bx, Tx, N_HEAD, HEAD_DIM).transpose(0, 2, 1, 3)
        k = k.reshape(Bx, Tx, N_HEAD, HEAD_DIM).transpose(0, 2, 1, 3)
        v = v.reshape(Bx, Tx, N_HEAD, HEAD_DIM).transpose(0, 2, 1, 3)
        q = _apply_rope(q)
        k = _apply_rope(k)
        scale = 1.0 / math.sqrt(HEAD_DIM)
        att = jnp.einsum('bhqd,bhkd->bhqk', q, k) * scale
        causal = jnp.tril(jnp.ones((Tx, Tx), dtype=bool))
        att = jnp.where(causal[None, None], att, -jnp.inf)
        att = jax.nn.softmax(att, axis=-1)
        y = jnp.einsum('bhqk,bhkd->bhqd', att, v)
        y = y.transpose(0, 2, 1, 3).reshape(Bx, Tx, C)
        return jnp.einsum('btc,cd->btd', y, W_proj) + b_proj

    def _L1_ffn_ref(x, w1_w, w1_s, w2_w, w2_s, h1_w, h1_s, h2_w, h2_s, w3_w, w3_s):
        import jax, jax.numpy as jnp
        import numpy as np
        D_IN, D_HID = (128, 512)

        def _ternary(key, shape):
            return jax.random.randint(key, shape, -1, 2).astype(jnp.float32)

        def _tlin(x, w, s):
            return jnp.einsum('bsi,oi->bso', x, w) * s
        h = jax.nn.silu(_tlin(x, w1_w, w1_s)) * _tlin(x, w2_w, w2_s)
        h = jax.nn.gelu(_tlin(h, h1_w, h1_s), approximate=False)
        h = jax.nn.gelu(_tlin(h, h2_w, h2_s), approximate=False)
        return _tlin(h, w3_w, w3_s)

    def _L2_attn_ref(x, w_r, w_k, w_v, w_g, w_o, time_maa_k, time_maa_v, time_maa_r, time_maa_g, time_decay, time_faaaa, ln_g, ln_b):
        import jax, jax.numpy as jnp
        import numpy as np
        D = 128
        H = 16
        N = D // H
        B = 4
        T = 256
        NLAYERS = 12
        LAYER_ID = 6
        EPS = 1e-05 * 64

        def _forward(x, w_r, w_k, w_v, w_g, w_o, time_maa_k, time_maa_v, time_maa_r, time_maa_g, time_decay, time_faaaa, ln_g, ln_b):
            Bs, Ts, C = x.shape
            if Ts % 32 == 0:
                Q = 32
            elif Ts % 128 == 0:
                Q = 128
            else:
                Q = Ts
            nC = Ts // Q
            xs = jnp.pad(x, ((0, 0), (1, 0), (0, 0)))[:, :-1]
            xx = xs - x
            xk = x + xx * time_maa_k
            xv = x + xx * time_maa_v
            xr = x + xx * time_maa_r
            xg = x + xx * time_maa_g
            r = (xr @ w_r.T).reshape(Bs, Ts, H, N).transpose(0, 2, 1, 3)
            k = (xk @ w_k.T).reshape(Bs, Ts, H, N).transpose(0, 2, 3, 1)
            v = (xv @ w_v.T).reshape(Bs, Ts, H, N).transpose(0, 2, 1, 3)
            g = jax.nn.silu(xg @ w_g.T)
            w = jnp.exp(-jnp.exp(time_decay))
            u = time_faaaa
            ws = (w ** Q)[None, :, None, None]
            q = jnp.arange(Q)
            wk = (w[:, None] ** (Q - 1 - q)[None, :])[None, :, None, :]
            wb = (w[:, None] ** q[None, :])[None, :, :, None]
            ii = q[:, None]
            jj = q[None, :]
            e = jnp.maximum(ii - jj - 1, 0)
            Wmat = jnp.where((jj < ii)[None], w[:, None, None] ** e[None], 0.0)
            Wmat = Wmat + jnp.eye(Q, dtype=x.dtype)[None] * u[:, None, None]
            Wmat = Wmat[None]
            rC = r.reshape(Bs, H, nC, Q, N).transpose(2, 0, 1, 3, 4)
            kC = k.reshape(Bs, H, N, nC, Q).transpose(3, 0, 1, 2, 4)
            vC = v.reshape(Bs, H, nC, Q, N).transpose(2, 0, 1, 3, 4)

            def step(state, inp):
                rr, kk, vv = inp
                y = rr @ kk * Wmat @ vv + rr @ state * wb
                state = ws * state + kk * wk @ vv
                return (state, y)
            state0 = jnp.zeros((Bs, H, N, N), x.dtype)
            _, yC = jax.lax.scan(step, state0, (rC, kC, vC))
            y = yC.transpose(1, 2, 0, 3, 4).reshape(Bs, H, Ts, N)
            y = y.transpose(0, 2, 1, 3).reshape(Bs * Ts, H, N)
            mu = y.mean(-1, keepdims=True)
            var = y.var(-1, keepdims=True)
            y = (y - mu) / jnp.sqrt(var + EPS)
            y = y.reshape(Bs, Ts, C) * ln_g + ln_b
            y = y * g
            return y @ w_o.T
        return _forward(x, w_r, w_k, w_v, w_g, w_o, time_maa_k, time_maa_v, time_maa_r, time_maa_g, time_decay, time_faaaa, ln_g, ln_b)

    def _L2_ffn_ref(hidden_states, wg_red, wg, w1, b1, w2, b2):
        import jax, jax.numpy as jnp
        import numpy as np
        NUM_EXPERTS = 8
        IN_FEATURES = 128
        HIDDEN_FEATURES = 512
        GATE_DIM = 16
        EPS = 0.0001
        b, t, c = hidden_states.shape
        x = hidden_states.reshape(-1, c)
        xr = x @ wg_red.T
        wg_unit = wg / jnp.maximum(jnp.linalg.norm(wg, axis=1, keepdims=True), EPS)
        logits = xr @ wg_unit.T
        gates = jax.nn.softmax(logits, axis=1)
        indices_s = jnp.argmax(gates, axis=1)
        scores = jnp.max(gates, axis=1)
        E = wg.shape[0]
        out = jnp.zeros_like(x)
        for e in range(E):
            mask = (indices_s == e).astype(x.dtype)[:, None]
            h = jax.nn.gelu(x @ w1[e] + b1[e], approximate=False)
            out = out + mask * (h @ w2[e] + b2[e])
        out = out * scores[:, None]
        return out.reshape(b, t, c)

    def _L3_attn_ref(x, W):
        import jax, jax.numpy as jnp
        import numpy as np
        KEY_DIM = 128
        EMBED_DIM = 128
        key_dim = KEY_DIM
        qkv = jnp.einsum('bsd,de->bse', x, W)
        q = qkv[:, :, :key_dim]
        k = qkv[:, :, key_dim:2 * key_dim]
        v = qkv[:, :, 2 * key_dim:]
        scores = jnp.einsum('bqd,bkd->bqk', q, k) / np.sqrt(key_dim).astype(np.float32)
        attn = jax.nn.softmax(scores, axis=1)
        return jnp.einsum('bqk,bkd->bqd', attn, v)

    def _L3_ffn_ref(x, w_gate, w1, w3, w2):
        import jax, jax.numpy as jnp
        import numpy as np
        B, S, D = (4, 256, 128)
        E, H, TOP_K = (8, 256, 2)
        bsz, seq_len, embed_dim = x.shape
        xt = x.reshape(-1, embed_dim)
        T = xt.shape[0]
        logits = xt @ w_gate
        top_logits, sel = jax.lax.top_k(logits, TOP_K)
        probs = jax.nn.softmax(top_logits, axis=-1).astype(x.dtype)
        h = jax.nn.silu(jnp.einsum('td,edh->eth', xt, w1)) * jnp.einsum('td,edh->eth', xt, w3)
        y = jnp.einsum('eth,ehd->etd', h, w2)
        t_idx = jnp.arange(T)
        yk = y[sel.T, t_idx[None, :], :]
        out = jnp.einsum('ktd,tk->td', yk, probs)
        return out.reshape(bsz, seq_len, embed_dim)
    x = L0_attn_x
    xn = _layernorm(x, axis=-1)
    x = x + _L0_attn_ref(xn, L0_attn_Wz, L0_attn_bz, L0_attn_Wza, L0_attn_bza, L0_attn_Wy, L0_attn_by, L0_attn_Wya, L0_attn_bya, L0_attn_norm_w, L0_attn_lc_re, L0_attn_lc_im) + _L0_ffn_ref(xn, L0_ffn_router_w, L0_ffn_rg, L0_ffn_ru, L0_ffn_rd, L0_ffn_sg, L0_ffn_su, L0_ffn_sd)
    xn = _layernorm(x, axis=-1)
    x = x + _L1_attn_ref(xn, L1_attn_W_attn, L1_attn_b_attn, L1_attn_W_proj, L1_attn_b_proj) + _L1_ffn_ref(xn, L1_ffn_w1_w, L1_ffn_w1_s, L1_ffn_w2_w, L1_ffn_w2_s, L1_ffn_h1_w, L1_ffn_h1_s, L1_ffn_h2_w, L1_ffn_h2_s, L1_ffn_w3_w, L1_ffn_w3_s)
    xn = _layernorm(x, axis=-1)
    x = x + _L2_attn_ref(xn, L2_attn_w_r, L2_attn_w_k, L2_attn_w_v, L2_attn_w_g, L2_attn_w_o, L2_attn_time_maa_k, L2_attn_time_maa_v, L2_attn_time_maa_r, L2_attn_time_maa_g, L2_attn_time_decay, L2_attn_time_faaaa, L2_attn_ln_g, L2_attn_ln_b) + _L2_ffn_ref(xn, L2_ffn_wg_red, L2_ffn_wg, L2_ffn_w1, L2_ffn_b1, L2_ffn_w2, L2_ffn_b2)
    xn = _layernorm(x, axis=-1)
    x = x + _L3_attn_ref(xn, L3_attn_W) + _L3_ffn_ref(xn, L3_ffn_w_gate, L3_ffn_w1, L3_ffn_w3, L3_ffn_w2)
    return x

_drawn_inputs = setup_inputs


def setup_inputs(seed=0):
    import zlib

    import numpy as np

    out = dict(_drawn_inputs(seed))
    spreads = {'L0_attn_bz': (0.0, 2.0),
     'L0_attn_bza': (0.0, 2.0),
     'L0_attn_by': (0.0, 0.837),
     'L0_attn_bya': (0.0, 0.364),
     'L0_attn_norm_w': (1.0, 0.6),
     'L2_attn_ln_g': (1.0, 0.6),
     'L2_attn_ln_b': (0.0, 2.0)}
    factors = {'L0_attn_Wz': 200.0,
     'L0_attn_Wza': 186.519,
     'L0_attn_Wy': 39.908,
     'L0_attn_Wya': 25.791,
     'L0_attn_lc_re': 43.792,
     'L0_attn_lc_im': 64.0,
     'L1_ffn_w1_w': 3.251,
     'L1_ffn_w1_s': 4.817,
     'L1_ffn_w2_w': 3.505,
     'L1_ffn_w2_s': 5.475,
     'L1_ffn_h1_w': 3.304,
     'L1_ffn_h1_s': 6.767,
     'L1_ffn_h2_w': 3.438,
     'L1_ffn_h2_s': 5.942,
     'L1_ffn_w3_w': 3.222,
     'L1_ffn_w3_s': 6.607,
     'L2_attn_w_r': 27.08,
     'L2_attn_w_k': 28.952,
     'L2_attn_w_v': 28.488,
     'L2_attn_w_g': 28.376,
     'L2_attn_w_o': 27.312,
     'L2_attn_time_maa_k': 64.0,
     'L2_attn_time_maa_v': 64.0,
     'L2_attn_time_maa_r': 64.0,
     'L2_attn_time_maa_g': 64.0,
     'L2_attn_time_decay': 52.8,
     'L2_attn_time_faaaa': 172.563,
     'L3_ffn_w_gate': 31.226,
     'L3_ffn_w1': 37.271,
     'L3_ffn_w3': 31.898,
     'L3_ffn_w2': 31.874,
     'L0_ffn_router_w': 6.703,
     'L0_ffn_rg': 5.935,
     'L0_ffn_ru': 5.861,
     'L0_ffn_rd': 5.887,
     'L1_attn_W_attn': 64.0,
     'L1_attn_b_attn': 64.0,
     'L1_attn_W_proj': 64.0,
     'L1_attn_b_proj': 64.0,
     'L2_ffn_wg_red': 8.0,
     'L2_ffn_wg': 8.0,
     'L2_ffn_w1': 8.0,
     'L2_ffn_b1': 44.735,
     'L2_ffn_w2': 8.0,
     'L2_ffn_b2': 64.0,
     'L3_attn_W': 61.914}
    for name, (base, spread) in spreads.items():
        noise = np.random.default_rng([zlib.crc32(name.encode()), seed]).standard_normal(out[name].shape)
        drawn = base * np.exp(spread * noise) if base else spread * noise
        out[name] = jnp.asarray(drawn.astype(out[name].dtype))
    for name, factor in factors.items():
        out[name] = (out[name] * factor).astype(out[name].dtype)
    return out
```

```python
import math
from contextlib import ExitStack

import concourse.bass as bass
from concourse import mybir

F32 = mybir.dt.float32
BF16 = mybir.dt.bfloat16
ALU = mybir.AluOpType
ACT = mybir.ActivationFunctionType
AX_X = mybir.AxisListType.X

P = 128
B, SEQ = 8, 256
N = B * SEQ
T = 512
NT = N // T
NTOK = N // P
SPT = T // SEQ
E = 8
CAP = int(1.25 * N / E)
H, HD = 16, 8
HID0, SH0 = 512, 1024
HID1 = 512
HID2 = 512
HID3 = 256
EPS_LN = 1e-5
EPS_RMS = 1e-6
EPS_GN = 1e-5 * 64
EPS_GATE = 1e-4
EPS_F32 = 1.1920928955078125e-07
NEG = -1e30
DOWN = 2.0 ** -16

MATS = ["z0", "za0", "y0", "ya0", "q1", "qs1", "k1", "ks1", "v1", "p1",
        "r2", "k2", "v2", "g2", "o2", "q3", "k3", "v3"]
COLS = [("bz", 1), ("bza", 1), ("by", 1), ("bya", 1), ("norm_w", 1), ("lc_re", 1), ("lc_im", 1),
        ("bq", 1), ("bqs", 1), ("bk", 1), ("bks", 1), ("bv", 1), ("bp", 1),
        ("w1_s", 4), ("w2_s", 4), ("h1_s", 4), ("h2_s", 4), ("w3_s", 1),
        ("maa_k", 1), ("maa_v", 1), ("maa_r", 1), ("maa_g", 1), ("td_ch", 1), ("ln_g", 1), ("ln_b", 1),
        ("td_bc", H), ("u_bc", H), ("b1_2", E * 4),
        ("router0", E), ("wgred2", 16), ("wg2", E), ("gate3", E)]
TABS = [("ones_d", P), ("ident", P), ("dec_c", SEQ), ("dec_s", SEQ), ("gro_c", SEQ), ("gro_s", SEQ),
        ("nxt_c", SEQ), ("nxt_s", SEQ), ("keep", T), ("cosq", SEQ), ("sinq", SEQ), ("cosk", SEQ), ("sink", SEQ),
        ("hmask", H), ("code", E), ("lag", P), ("before", P), ("iota_q", P), ("rev_j", 1), ("grp", P), ("sel16", P)]


def offsets(items):
    at, out = 0, {}
    for name, n in items:
        out[name] = (at, n)
        at += n
    return out, at


COL_AT, COL_N = offsets(COLS)
TAB_AT, TAB_N = offsets(TABS)


class Steps:

    def __init__(self, sem, names, turns=1, base=0):
        self.sem, self.names, self.base = sem, {n: k + 1 for k, n in enumerate(names)}, base
        self.per = len(names)
        self.end = base + turns * self.per

    def at(self, name, turn=0):
        return turn * self.per + (self.base + self.names[name])

    def turn_end(self, turn=0):
        return turn * self.per + (self.base + self.per)


def build(nc, d):
    ctx = ExitStack()
    with ctx:
        def sb(name, shape, dt=F32):
            return ctx.enter_context(nc.sbuf_tensor(name, shape, dt))

        def sem(name):
            return ctx.enter_context(nc.semaphore(name))

        x = sb("x", [P, N])
        xn = sb("xn", [P, N])
        mats = sb("mats", [P, len(MATS) * P])
        cols = sb("cols", [P, COL_N])
        tabs = sb("tabs", [P, TAB_N])
        b2rows = sb("b2rows", [E, P])
        bft = sb("bft", [P, E * P + P + P], BF16)
        wa = sb("wa", [P, 15360])
        wb = sb("wb", [P, 5632])
        work = sb("work", [P, 19968])
        rt = work[:, 10240:11520].rearrange("p (a b) -> p a b", b=NTOK * E)
        rs = sb("rs", [P, 8, NTOK])
        wT = work[0:E, 15360:17408]
        w24 = work[0:24, 17408:18432].bitcast(BF16)
        ps = ctx.enter_context(nc.psum_tensor("ps", [P, 8, T], F32))

        def mat(name):
            k = MATS.index(name)
            return mats[:, k * P:(k + 1) * P]

        def col(name, k=0, rows=P):
            return cols[0:rows, COL_AT[name][0] + k:COL_AT[name][0] + k + 1]

        def colv(name, rows=P):
            a, n = COL_AT[name]
            return cols[0:rows, a:a + n]

        def tab(name, rows=P):
            a, n = TAB_AT[name]
            return tabs[0:rows, a:a + n]

        def tabseq(name):
            return tab(name).rearrange("p (o s) -> p o s", o=1).broadcast_to([P, SPT, SEQ])

        def two(ap):
            return ap.rearrange("p (o s) -> p o s", s=SEQ)

        sel_e = [bft[0:24, e * P:(e + 1) * P] for e in range(E)]
        identb = bft[:, E * P:E * P + P]
        causalb = bft[:, E * P + P:E * P + 2 * P]
        ident = tab("ident")

        def tile(ap, i):
            return ap[:, bass.ds(i * T, T)]

        def bank(k):
            return ps[:, k, :] if isinstance(k, int) else ps[:, bass.ds(k, 1), :].rearrange("p o t -> p (o t)")

        ld_x, ld_small, ld_w0, ld_w1, ld_w23, stored = [sem(n) for n in
            ("ld_x", "ld_small", "ld_w0", "ld_w1", "ld_w23", "stored")]
        met = {n: sem(f"met_{n}") for n in ("pe", "act", "dve", "pool")}
        passed = {n: [0] for n in met}
        b_parts = sem("parts_moved")

        def meet(name, eng):
            passed[name][0] += 1
            eng.drain().then_inc(met[name], 1)
            for other in met:
                if other != name:
                    eng.wait_ge(met[other], passed[name][0])

        s = {}
        started = []

        def steps(key, names, turns=1, after=None):
            if after is None:
                s[key] = Steps(sem(key), names, turns, 1)
                started.append(s[key].sem)
            else:
                s[key] = Steps(s[after].sem, names, turns, s[after].end)
            return s[key]

        for L in range(4):
            prev = (lambda k: None if L == 0 else f"ln{L - 1}_{k}")
            steps(f"ln{L}_pe1", ["mean"], NT, f"ln{L-1}_pe2" if L else None)
            steps(f"ln{L}_pe2", ["var"], NT, f"ln{L}_pe1")
            steps(f"ln{L}_dve1", ["centred"], NT, f"ln{L-1}_dve2" if L else None)
            steps(f"ln{L}_dve2", ["normed"], NT, f"ln{L}_dve1")
            steps(f"ln{L}_act1", ["sq"], NT, f"ln{L-1}_act3" if L else None)
            steps(f"ln{L}_act2", ["log"], NT, f"ln{L}_act1")
            steps(f"ln{L}_act3", ["rstd"], NT, f"ln{L}_act2")

        ln_sq = work[:, 0:2048]
        ln_rs = work[:, 2048:4096]

        def ln_pe(L, eng):
            a, b = s[f"ln{L}_pe1"], s[f"ln{L}_pe2"]
            with eng.Fori(0, NT) as i:
                eng.matmul(bank(i), tab("ones_d"), tile(x, i), start=True, stop=True).then_inc(a.sem, 1)
            with eng.Fori(0, NT) as i:
                q = s[f"ln{L}_act1"]
                eng.wait_ge(q.sem, q.at("sq", i))
                eng.matmul(bank(i + 4), tab("ones_d"), tile(ln_sq, i), start=True, stop=True).then_inc(b.sem, 1)
            meet("pe", eng)

        def ln_dve(L, eng):
            a, b = s[f"ln{L}_dve1"], s[f"ln{L}_dve2"]
            with eng.Fori(0, NT) as i:
                q = s[f"ln{L}_pe1"]
                eng.wait_ge(q.sem, q.at("mean", i))
                eng.tensor_tensor(tile(xn, i), tile(x, i), bank(i), ALU.subtract).then_inc(a.sem, 1)
            with eng.Fori(0, NT) as i:
                q = s[f"ln{L}_act3"]
                eng.wait_ge(q.sem, q.at("rstd", i))
                eng.tensor_tensor(tile(xn, i), tile(xn, i), tile(ln_rs, i), ALU.mult).then_inc(b.sem, 1)
            meet("dve", eng)

        def ln_act(L, eng):
            a, b, c = s[f"ln{L}_act1"], s[f"ln{L}_act2"], s[f"ln{L}_act3"]
            with eng.Fori(0, NT) as i:
                q = s[f"ln{L}_dve1"]
                eng.wait_ge(q.sem, q.at("centred", i))
                eng.activation(tile(ln_sq, i), tile(xn, i), ACT.Square).then_inc(a.sem, 1)
            with eng.Fori(0, NT) as i:
                q = s[f"ln{L}_pe2"]
                eng.wait_ge(q.sem, q.at("var", i))
                eng.activation(tile(ln_rs, i), bank(i + 4), ACT.Ln, bias=eps_ap(EPS_LN), scale=DOWN).then_inc(b.sem, 1)
            with eng.Fori(0, NT) as i:
                eng.wait_ge(b.sem, b.at("log", i))
                eng.activation(tile(ln_rs, i), tile(ln_rs, i), ACT.Exp, bias=epst[:, 4:5], scale=-0.5).then_inc(c.sem, 1)
            meet("act", eng)

        epst = sb("epst", [P, 5])
        EPSV = [EPS_LN, EPS_RMS, EPS_GN, EPS_F32]

        def eps_ap(v):
            k = EPSV.index(v)
            return epst[:, k:k + 1]

        a0 = dict(sz=0, zc=2048, zs=4096, h=6144, rs=8192, hc=10240)
        A0 = {k: work[:, v:v + 2048] for k, v in a0.items()}
        A0["hc"] = work[:, 10240:10496]
        A0["h2"] = work[:, 10496:10496 + 2048]
        steps("a0_pe1", ["z"], NT)
        steps("a0_pe2", ["ms"], NT, "a0_pe1")
        steps("a0_pe3", ["y"], NT, "a0_pe2")
        steps("a0_act1", ["silu_z"], NT)
        steps("a0_act2", ["sq"], NT, "a0_act1")
        steps("a0_act3", ["log"], NT, "a0_act2")
        steps("a0_act4", ["rstd"], NT, "a0_act3")
        steps("a0_act5", ["silu_y"], NT, "a0_act4")
        steps("a0_dve0", ["cross_re", "cross"])
        steps("a0_dve1", ["z", "zc", "cc", "cs", "hc", "hs", "h", "hx"], NT, "a0_dve0")
        steps("a0_dve2", ["normed"], NT, "a0_dve1")
        steps("a0_dve3", ["y", "x"], NT, "a0_dve2")
        steps("a0_pool", ["zs"], NT)

        def a0_pe(eng):
            with eng.Fori(0, NT) as i:
                eng.matmul(bank(i), mat("z0"), tile(xn, i), start=True, stop=True)
                eng.matmul(bank(i + 4), mat("za0"), tile(xn, i), start=True, stop=True)\
                   .then_inc(s["a0_pe1"].sem, 1)
            with eng.Fori(0, NT) as i:
                q = s["a0_act2"]
                eng.wait_ge(q.sem, q.at("sq", i))
                eng.matmul(bank(i), tab("ones_d"), tile(A0["sz"], i), start=True, stop=True)\
                   .then_inc(s["a0_pe2"].sem, 1)
            with eng.Fori(0, NT) as i:
                q = s["a0_dve2"]
                eng.wait_ge(q.sem, q.at("normed", i))
                eng.matmul(bank(i), mat("y0"), tile(A0["h2"], i), start=True, stop=True)
                eng.matmul(bank(i + 4), mat("ya0"), tile(xn, i), start=True, stop=True)\
                   .then_inc(s["a0_pe3"].sem, 1)
            meet("pe", eng)

        def a0_act(eng):
            with eng.Fori(0, NT) as i:
                q = s["a0_pe1"]
                eng.wait_ge(q.sem, q.at("z", i))
                eng.activation(tile(A0["sz"], i), bank(i + 4), ACT.Silu, bias=col("bza"))\
                   .then_inc(s["a0_act1"].sem, 1)
            with eng.Fori(0, NT) as i:
                q = s["a0_dve1"]
                eng.wait_ge(q.sem, q.at("hx", i))
                eng.activation(tile(A0["sz"], i), tile(A0["h"], i), ACT.Square).then_inc(s["a0_act2"].sem, 1)
            with eng.Fori(0, NT) as i:
                q = s["a0_pe2"]
                eng.wait_ge(q.sem, q.at("ms", i))
                eng.activation(tile(A0["rs"], i), bank(i), ACT.Ln, bias=eps_ap(EPS_RMS), scale=DOWN)\
                   .then_inc(s["a0_act3"].sem, 1)
            with eng.Fori(0, NT) as i:
                q = s["a0_act3"]
                eng.wait_ge(q.sem, q.at("log", i))
                eng.activation(tile(A0["rs"], i), tile(A0["rs"], i), ACT.Exp, bias=epst[:, 4:5], scale=-0.5)\
                   .then_inc(s["a0_act4"].sem, 1)
            with eng.Fori(0, NT) as i:
                q = s["a0_pe3"]
                eng.wait_ge(q.sem, q.at("y", i))
                eng.activation(tile(A0["sz"], i), bank(i + 4), ACT.Silu, bias=col("bya"))\
                   .then_inc(s["a0_act5"].sem, 1)
            meet("act", eng)

        def a0_pool(eng):
            with eng.Fori(0, NT) as i:
                q = s["a0_dve1"]
                eng.wait_ge(q.sem, q.at("z", i))
                eng.tensor_tensor(two(tile(A0["zs"], i)), two(tile(A0["h2"], i)), tabseq("dec_s"), ALU.mult)\
                   .then_inc(s["a0_pool"].sem, 1)
            meet("pool", eng)

        def a0_dve(eng):
            c = s["a0_dve0"]
            eng.tensor_scalar(A0["hc"], tab("nxt_c"), col("lc_re"), None, ALU.mult).then_inc(c.sem, 1)
            eng.wait_ge(c.sem, c.at("cross_re"))
            eng.scalar_tensor_tensor(out=A0["hc"], in0=tab("nxt_s"), scalar=col("lc_im"), in1=A0["hc"],
                                     op0=ALU.mult, op1=ALU.add).then_inc(c.sem, 1)
            eng.wait_ge(c.sem, c.at("cross"))
            hc = A0["hc"].rearrange("p (o s) -> p o s", o=1).broadcast_to([P, SPT, SEQ])
            st = s["a0_dve1"]
            with eng.Fori(0, NT) as i:
                q = s["a0_act1"]
                eng.wait_ge(q.sem, q.at("silu_z", i))
                eng.scalar_tensor_tensor(out=tile(A0["h2"], i), in0=bank(i), scalar=col("bz"),
                                         in1=tile(A0["sz"], i), op0=ALU.add, op1=ALU.mult).then_inc(st.sem, 1)
                eng.wait_ge(st.sem, st.at("z", i))
                eng.tensor_tensor(two(tile(A0["zc"], i)), two(tile(A0["h2"], i)), tabseq("dec_c"), ALU.mult)\
                   .then_inc(st.sem, 1)
                eng.wait_ge(st.sem, st.at("zc", i))
                eng.tensor_tensor_scan(tile(A0["h"], i), tab("keep"), tile(A0["zc"], i), 0.0,
                                       ALU.mult, ALU.add).then_inc(st.sem, 1)
                q = s["a0_pool"]
                eng.wait_ge(q.sem, q.at("zs", i))
                eng.wait_ge(st.sem, st.at("cc", i))
                eng.tensor_tensor_scan(tile(A0["rs"], i), tab("keep"), tile(A0["zs"], i), 0.0,
                                       ALU.mult, ALU.add).then_inc(st.sem, 1)
                eng.tensor_tensor(two(tile(A0["zc"], i)), two(tile(A0["h"], i)), tabseq("gro_c"), ALU.mult)\
                   .then_inc(st.sem, 1)
                eng.wait_ge(st.sem, st.at("cs", i))
                eng.tensor_tensor(two(tile(A0["zs"], i)), two(tile(A0["rs"], i)), tabseq("gro_s"), ALU.mult)\
                   .then_inc(st.sem, 1)
                eng.wait_ge(st.sem, st.at("hs", i))
                eng.tensor_tensor(tile(A0["h"], i), tile(A0["zc"], i), tile(A0["zs"], i), ALU.add)\
                   .then_inc(st.sem, 1)
                eng.wait_ge(st.sem, st.at("h", i))
                eng.tensor_tensor(two(tile(A0["h"], i)), two(tile(A0["h"], i)), hc, ALU.add)\
                   .then_inc(st.sem, 1)
            with eng.Fori(0, NT) as i:
                q = s["a0_act4"]
                eng.wait_ge(q.sem, q.at("rstd", i))
                eng.scalar_tensor_tensor(out=tile(A0["h2"], i), in0=tile(A0["h"], i), scalar=col("norm_w"),
                                         in1=tile(A0["rs"], i), op0=ALU.mult, op1=ALU.mult)\
                   .then_inc(s["a0_dve2"].sem, 1)
            st = s["a0_dve3"]
            with eng.Fori(0, NT) as i:
                q = s["a0_act5"]
                eng.wait_ge(q.sem, q.at("silu_y", i))
                eng.scalar_tensor_tensor(out=tile(A0["zc"], i), in0=bank(i), scalar=col("by"),
                                         in1=tile(A0["sz"], i), op0=ALU.add, op1=ALU.mult).then_inc(st.sem, 1)
                eng.wait_ge(st.sem, st.at("y", i))
                eng.tensor_tensor(tile(x, i), tile(x, i), tile(A0["zc"], i), ALU.add).then_inc(st.sem, 1)
            meet("dve", eng)

        R = {k: rt[:, n, :].rearrange("p (t e) -> p t e", e=E) for n, k in enumerate(
            ("lg", "eq", "oh1", "lg2", "oh2", "w", "t1", "t2"))}
        Q = {k: rs[:, n, :] for n, k in enumerate(("m1", "cm", "m2", "d", "e2", "w1", "w2", "rms"))}
        wgn = sb("wgn", [16, 3, E])

        def bce(ap):
            return ap.rearrange("p (t o) -> p t o", o=1).broadcast_to([P, NTOK, E])

        code = tab("code").rearrange("p (o e) -> p o e", o=1).broadcast_to([P, NTOK, E])
        DVE_R = {
            0: ["rms", "lg", "m1", "eq", "cd", "cm", "oh1", "lg2", "m2", "eq2", "cd2", "cm2", "oh2",
                "d", "den", "w1", "w2", "t1", "t2", "w", "selT", "cum", "wTraw", "kept", "p1", "r1", "p2", "r2", "p3"],
            2: ["nmax", "wginv", "wgu", "xr", "lg", "m1", "eq", "cd", "cm", "oh1", "lgm", "den", "w1", "w",
                "wT", "p1", "r1", "p2", "r2", "p3"],
            3: ["lg", "m1", "eq", "cd", "cm", "oh1", "lg2", "m2", "eq2", "cd2", "cm2", "oh2",
                "d", "den", "w1", "w2", "t1", "t2", "w", "wT", "p1", "r1", "p2", "r2", "p3"]}
        PE_R = {0: ["lg", "selT", "wT"], 2: ["nrm", "xr", "lg", "wT"], 3: ["lg", "wT"]}
        ACT_R = {0: ["sq", "log", "rms", "e2"], 2: ["sqw", "log", "e2"], 3: ["e2"]}
        for L in (0, 2, 3):
            steps(f"r{L}_dve", DVE_R[L])
            steps(f"r{L}_pe", PE_R[L])
            steps(f"r{L}_act", ACT_R[L])
        xsq = work[:, 0:2048]
        xr_sb = work[0:16, 0:2048]
        selT = work[0:E, 2048:4096]
        cum = work[0:E, 4096:6144]
        rest = work[0:E, 6144:8192]
        part = work[0:E, 11520:14592].bitcast(BF16).rearrange("p (k n) -> p k n", k=3)
        sel_tok = rt[:, 8, :].rearrange("p (t e) -> p t e", e=E)

        def r_pe(L, eng):
            st, dv, ac = s[f"r{L}_pe"], s[f"r{L}_dve"], s[f"r{L}_act"]
            lg = ps[:, 0, 0:NTOK * E].rearrange("p (t e) -> p t e", e=E)
            if L == 0:
                for t in range(NTOK):
                    eng.matmul(lg[:, t, :], xn[:, t * P:(t + 1) * P], colv("router0"), start=True, stop=True)
                eng.wait_ge(ac.sem, ac.at("sq"))
                for t in range(NTOK):
                    mm = eng.matmul(ps[:, 1, t:t + 1], xsq[:, t * P:(t + 1) * P], tab("ones_d")[:, 0:1],
                                    start=True, stop=True)
                mm.then_inc(st.sem, 1)
            elif L == 2:
                eng.wait_ge(ac.sem, ac.at("sqw"))
                eng.matmul(ps[0:16, 1, 0:E], ones16[:, :], wgn[:, 0, :],
                           start=True, stop=True).then_inc(st.sem, 1)
                for i in range(NT):
                    mm = eng.matmul(ps[0:16, 4 + i, :], colv("wgred2"), xn[:, i * T:(i + 1) * T],
                                    start=True, stop=True)
                mm.then_inc(st.sem, 1)
                eng.wait_ge(dv.sem, dv.at("xr"))
                for t in range(NTOK):
                    mm = eng.matmul(lg[:, t, :], xr_sb[:, t * P:(t + 1) * P], wgn[:, 2, :], start=True, stop=True)
                mm.then_inc(st.sem, 1)
            else:
                for t in range(NTOK):
                    mm = eng.matmul(lg[:, t, :], xn[:, t * P:(t + 1) * P], colv("gate3"), start=True, stop=True)
                mm.then_inc(st.sem, 1)
            eng.wait_ge(dv.sem, dv.at("w"))
            if L == 0:
                for t in range(NTOK):
                    mm = eng.transpose(ps[0:E, 4 + t // 4, (t % 4) * P:(t % 4 + 1) * P], sel_tok[:, t, :], ident)
                mm.then_inc(st.sem, 1)
            for t in range(NTOK):
                mm = eng.transpose(ps[0:E, t // 4, (t % 4) * P:(t % 4 + 1) * P], R["w"][:, t, :], ident)
            mm.then_inc(st.sem, 1)
            meet("pe", eng)

        def r_act(L, eng):
            st, dv, pe = s[f"r{L}_act"], s[f"r{L}_dve"], s[f"r{L}_pe"]
            if L == 0:
                eng.activation(xsq, xn[:, :], ACT.Square).then_inc(st.sem, 1)
                eng.wait_ge(pe.sem, pe.at("lg"))
                eng.activation(Q["d"], ps[:, 1, 0:NTOK], ACT.Ln, bias=eps_ap(EPS_F32), scale=DOWN).then_inc(st.sem, 1)
                eng.wait_ge(st.sem, st.at("log"))
                eng.activation(Q["rms"], Q["d"], ACT.Exp, bias=epst[:, 4:5], scale=-0.5).then_inc(st.sem, 1)
                eng.wait_ge(dv.sem, dv.at("d"))
                eng.activation(Q["e2"], Q["d"], ACT.Exp).then_inc(st.sem, 1)
            elif L == 2:
                eng.activation(wgn[:, 0, :], colv("wg2", 16), ACT.Square).then_inc(st.sem, 1)
                eng.wait_ge(pe.sem, pe.at("nrm"))
                eng.activation(wgn[:, 1, :], ps[0:16, 1, 0:E], ACT.Sqrt).then_inc(st.sem, 1)
                eng.wait_ge(dv.sem, dv.at("lgm"))
                eng.activation(R["t1"], R["t2"], ACT.Exp).then_inc(st.sem, 1)
            else:
                eng.wait_ge(dv.sem, dv.at("d"))
                eng.activation(Q["e2"], Q["d"], ACT.Exp).then_inc(st.sem, 1)
            meet("act", eng)

        ones16 = sb("ones16", [16, 16])

        def r_dve(L, eng):
            st, pe, ac = s[f"r{L}_dve"], s[f"r{L}_pe"], s[f"r{L}_act"]
            lgp = ps[:, 0, 0:NTOK * E].rearrange("p (t e) -> p t e", e=E)

            def did(ins):
                ins.then_inc(st.sem, 1)
                n[0] += 1
                eng.wait_ge(st.sem, st.base + n[0])

            n = [0]
            if L == 0:
                eng.wait_ge(ac.sem, ac.at("rms"))
                did(eng.tensor_copy(R["t1"], bce(Q["rms"])))
                did(eng.tensor_tensor(R["lg"], lgp, R["t1"], ALU.mult))
            elif L == 2:
                eng.wait_ge(ac.sem, ac.at("log"))
                did(eng.tensor_scalar(wgn[:, 1, :], wgn[:, 1, :], EPS_GATE, None, ALU.max))
                did(eng.reciprocal(wgn[:, 0, :], wgn[:, 1, :]))
                did(eng.tensor_tensor(wgn[:, 2, :], wgn[:, 0, :], colv("wg2", 16), ALU.mult))
                eng.wait_ge(pe.sem, pe.at("xr"))
                did(eng.tensor_copy(xr_sb, ps[0:16, 4:8, :].rearrange("p a t -> p (a t)")))
                eng.wait_ge(pe.sem, pe.at("lg"))
                did(eng.tensor_copy(R["lg"], lgp))
            else:
                eng.wait_ge(pe.sem, pe.at("lg"))
                did(eng.tensor_copy(R["lg"], lgp))

            def first_best(lg, m, oh):
                did(eng.tensor_reduce(Q[m], lg, AX_X, ALU.max))
                did(eng.tensor_tensor(R["eq"], lg, bce(Q[m]), ALU.is_equal))
                did(eng.tensor_tensor(R["eq"], R["eq"], code, ALU.mult))
                did(eng.tensor_reduce(Q["cm"], R["eq"], AX_X, ALU.max))
                did(eng.tensor_tensor(R[oh], R["eq"], bce(Q["cm"]), ALU.is_equal))

            first_best(R["lg"], "m1", "oh1")
            if L == 2:
                did(eng.tensor_tensor(R["t2"], R["lg"], bce(Q["m1"]), ALU.subtract))
                eng.wait_ge(ac.sem, ac.at("e2"))
                did(eng.tensor_reduce(Q["d"], R["t1"], AX_X, ALU.add))
                did(eng.reciprocal(Q["w1"], Q["d"]))
                did(eng.tensor_tensor(R["w"], R["oh1"], bce(Q["w1"]), ALU.mult))
            else:
                did(eng.scalar_tensor_tensor(out=R["lg2"], in0=R["oh1"], scalar=NEG, in1=R["lg"],
                                             op0=ALU.mult, op1=ALU.add))
                first_best(R["lg2"], "m2", "oh2")
                did(eng.tensor_tensor(Q["d"], Q["m2"], Q["m1"], ALU.subtract))
                eng.wait_ge(ac.sem, ac.at("e2"))
                did(eng.tensor_scalar(Q["w2"], Q["e2"], 1.0, None, ALU.add))
                did(eng.reciprocal(Q["w1"], Q["w2"]))
                did(eng.tensor_tensor(Q["w2"], Q["e2"], Q["w1"], ALU.mult))
                did(eng.tensor_tensor(R["t1"], R["oh1"], bce(Q["w1"]), ALU.mult))
                did(eng.tensor_tensor(R["t2"], R["oh2"], bce(Q["w2"]), ALU.mult))
                if L == 0:
                    eng.tensor_tensor(sel_tok, R["oh1"], R["oh2"], ALU.add)
                did(eng.tensor_tensor(R["w"], R["t1"], R["t2"], ALU.add))
            wTp = ps[0:E, 0:4, :].rearrange("p a t -> p (a t)")
            if L == 0:
                eng.wait_ge(pe.sem, pe.at("selT"))
                did(eng.tensor_copy(selT, ps[0:E, 4:8, :].rearrange("p a t -> p (a t)")))
                did(eng.tensor_tensor_scan(cum, onesrow, selT, 0.0, ALU.mult, ALU.add))
                eng.wait_ge(pe.sem, pe.at("wT"))
                did(eng.tensor_copy(rest, wTp))
                did(eng.scalar_tensor_tensor(out=wT[:, :], in0=cum, scalar=float(CAP), in1=rest,
                                             op0=ALU.is_le, op1=ALU.mult))
            else:
                eng.wait_ge(pe.sem, pe.at("wT"))
                did(eng.tensor_copy(wT[:, :], wTp))
            did(eng.tensor_copy(part[:, 0, :], wT[:, :]))
            did(eng.tensor_tensor(rest, wT[:, :], part[:, 0, :], ALU.subtract))
            did(eng.tensor_copy(part[:, 1, :], rest))
            did(eng.tensor_tensor(rest, rest, part[:, 1, :], ALU.subtract))
            did(eng.tensor_copy(part[:, 2, :], rest))
            assert n[0] == st.per, (L, n[0], st.per)
            meet("dve", eng)

        onesrow = work[0:E, 8192:10240]

        moves = {0: 1, 2: 2, 3: 3}

        def r_sync(L, eng):
            dv = s[f"r{L}_dve"]
            eng.wait_ge(dv.sem, dv.at("p3"))
            for k in range(3):
                eng.dma_start(w24[k * E:(k + 1) * E, :], part[:, k, :]).then_inc(b_parts, 16)

        def gated(L):
            if L == 0:
                g0, u0, d0 = 0, E * HID0, 2 * E * HID0
                sg0, su0, sd0 = 3 * E * HID0, 3 * E * HID0 + SH0, 3 * E * HID0 + 2 * SH0
                nb = HID0 // P
                blocks = [(None, wa[:, sg0 + j * P:sg0 + (j + 1) * P], wa[:, su0 + j * P:su0 + (j + 1) * P],
                           wa[:, sd0 + j * P:sd0 + (j + 1) * P]) for j in range(SH0 // P)]
                base = 0
                hid = HID0
            else:
                base = 2 * E * HID2
                hid = HID3
                nb = HID3 // P
                g0, u0, d0 = base, base + E * hid, base + 2 * E * hid
                blocks = []
            for e in range(E):
                for j in range(nb):
                    c = e * hid + j * P
                    blocks.append((e, wa[:, g0 + c:g0 + c + P], wa[:, u0 + c:u0 + c + P], wa[:, d0 + c:d0 + c + P]))
            return blocks, nb

        FB = {}
        for L in (0, 3):
            blocks, nb = gated(L)
            first = {}
            for k, b in enumerate(blocks):
                if b[0] is not None:
                    first.setdefault(b[0], k)
            make = {max(first[e] - nb, 0) if e else 0: [] for e in range(E)}
            for e in range(E):
                make[max(first[e] - nb, 0) if e else 0].append(e)
            pe_names, dve_names = [], []
            for k in range(len(blocks)):
                pe_names += [f"w{e}" for e in make.get(k, [])] + [f"g{k}", f"u{k}"]
                dve_names += [f"xw{e}" for e in make.get(k, [])] + [f"h{k}"]
            pe_names += ["y"]
            pe_names = []
            for k in range(len(blocks) + 2):
                if k < len(blocks):
                    pe_names += [f"w{e}" for e in make.get(k, [])] + [f"g{k}", f"u{k}"]
                if k >= 2:
                    pe_names += [f"d{k - 2}"]
            steps(f"f{L}_pe", pe_names, NT)
            steps(f"f{L}_act", [f"s{k}" for k in range(len(blocks))], NT)
            steps(f"f{L}_dve", dve_names + ["x"], NT)
            FB[L] = (blocks, make)
        f_sg = [work[:, k * T:(k + 1) * T] for k in range(2)]
        f_h = [work[:, (2 + k) * T:(3 + k) * T] for k in range(3)]
        f_xw = [work[:, (5 + k) * T:(6 + k) * T] for k in range(2)]

        def f_pe(L, eng):
            blocks, make = FB[L]
            st, ac, dv = s[f"f{L}_pe"], s[f"f{L}_act"], s[f"f{L}_dve"]
            eng.wait_ge(b_parts, 48 * moves[L])
            with eng.Fori(0, NT) as i:
                for k in range(len(blocks) + 2):
                    if k < len(blocks):
                        for e in make.get(k, []):
                            eng.wait_ge(b_parts, 48 * moves[L])
                            if e >= 2:
                                eng.wait_ge(dv.sem, dv.at(f"xw{e - 2}", i))
                            eng.matmul(bank(4 + e % 2), sel_e[e], tile(w24, i), start=True, stop=True)\
                               .then_inc(st.sem, 1)
                        e, g, u, dn = blocks[k]
                        if k >= 2:
                            eng.wait_ge(dv.sem, dv.at(f"h{k - 2}", i))
                        eng.matmul(bank(k % 2), g, tile(xn, i), start=True, stop=True).then_inc(st.sem, 1)
                        if e is None:
                            rhs = tile(xn, i)
                        else:
                            rhs = f_xw[e % 2]
                            eng.wait_ge(dv.sem, dv.at(f"xw{e}", i))
                        eng.matmul(bank(2 + k % 2), u, rhs, start=True, stop=True).then_inc(st.sem, 1)
                    if k >= 2:
                        j = k - 2
                        if j == 0:
                            eng.wait_ge(dv.sem, i * dv.per + dv.base)
                        eng.wait_ge(dv.sem, dv.at(f"h{j}", i))
                        eng.matmul(bank(6), blocks[j][3], f_h[j % 3], start=(j == 0), stop=(j == len(blocks) - 1))\
                           .then_inc(st.sem, 1)
            meet("pe", eng)

        def f_act(L, eng):
            blocks, make = FB[L]
            st, pe, dv = s[f"f{L}_act"], s[f"f{L}_pe"], s[f"f{L}_dve"]
            with eng.Fori(0, NT) as i:
                for k in range(len(blocks)):
                    eng.wait_ge(pe.sem, pe.at(f"g{k}", i))
                    if k >= 2:
                        eng.wait_ge(dv.sem, dv.at(f"h{k - 2}", i))
                    eng.activation(f_sg[k % 2], bank(k % 2), ACT.Silu).then_inc(st.sem, 1)
            meet("act", eng)

        def f_dve(L, eng):
            blocks, make = FB[L]
            st, pe, ac = s[f"f{L}_dve"], s[f"f{L}_pe"], s[f"f{L}_act"]
            with eng.Fori(0, NT) as i:
                for k in range(len(blocks)):
                    for e in make.get(k, []):
                        eng.wait_ge(pe.sem, pe.at(f"w{e}", i))
                        if e >= 2:
                            last = max(j for j, b in enumerate(blocks) if b[0] == e - 2)
                            eng.wait_ge(pe.sem, pe.at(f"u{last}", i))
                        eng.tensor_tensor(f_xw[e % 2], tile(xn, i), bank(4 + e % 2), ALU.mult).then_inc(st.sem, 1)
                    eng.wait_ge(pe.sem, pe.at(f"u{k}", i))
                    eng.wait_ge(ac.sem, ac.at(f"s{k}", i))
                    if k >= 3:
                        eng.wait_ge(pe.sem, pe.at(f"d{k - 3}", i))
                    eng.tensor_tensor(f_h[k % 3], f_sg[k % 2], bank(2 + k % 2), ALU.mult).then_inc(st.sem, 1)
                eng.wait_ge(pe.sem, pe.at(f"d{len(blocks) - 1}", i))
                eng.tensor_tensor(tile(x, i), tile(x, i), bank(6), ALU.add).then_inc(st.sem, 1)
            meet("dve", eng)

        def values_pe(eng, name, src, st):
            for t in range(NTOK):
                mm = eng.matmul(ps[:, t // 4, (t % 4) * P:(t % 4 + 1) * P], src[:, t * P:(t + 1) * P], mat(name),
                                start=True, stop=True)
                if t % 4 == 3:
                    mm.then_inc(st.sem, 1)

        VP = 16 * 136
        q1, k1, v1 = [work[:, k * N:(k + 1) * N] for k in range(3)]
        y1 = q1
        kpad = [wa[:, k * 4096:(k + 1) * 4096] for k in range(2)]
        vpad = [[work[:, 6144 + (2 * k + c) * VP:6144 + (2 * k + c + 1) * VP] for c in range(2)] for k in range(2)]
        o = 6144 + 4 * VP
        qst = [work[:, o + k * SEQ:o + (k + 1) * SEQ] for k in range(2)]
        o += 2 * SEQ
        p0 = [work[:, o + k * 512:o + (k + 1) * 512] for k in range(2)]
        o += 1024
        p1 = [wa[:, 8192 + k * 1024:8192 + (k + 1) * 1024] for k in range(2)]
        pT = [wa[:, 10240 + k * 384:10240 + (k + 1) * 384] for k in range(3)]
        nmx = wa[:, 11392:11392 + 64]
        den1 = wa[:, 11456:11456 + 64]
        den_all = wa[:, 11520:11520 + 256]
        rden_all = wa[:, 11776:11776 + 256]
        rT = wa[0:16, 12032:12032 + 2048]
        tmpa = [wa[:, k * 2048:(k + 1) * 2048] for k in range(4)]
        assert o <= 19968

        steps("p1_pe", ["q", "k"], NT)
        steps("p1_pe_v", ["v"], NTOK // 4, "p1_pe")
        steps("p1_dve0", ["z0", "z1", "z2", "z3"])
        steps("p1_dve", ["qa", "qb", "q", "ka", "kb", "k"], NT, "p1_dve0")
        steps("p1_dve_v", ["v"], NT, "p1_dve")

        def p1_pe(eng):
            st = s["p1_pe"]
            with eng.Fori(0, NT) as i:
                dv = s["p1_dve"]
                eng.wait_ge(dv.sem, i * dv.per + dv.base)
                eng.matmul(bank(0), mat("q1"), tile(xn, i), start=True, stop=True)
                eng.matmul(bank(1), mat("qs1"), tile(xn, i), start=True, stop=True).then_inc(st.sem, 1)
                eng.matmul(bank(2), mat("k1"), tile(xn, i), start=True, stop=True)
                eng.matmul(bank(3), mat("ks1"), tile(xn, i), start=True, stop=True).then_inc(st.sem, 1)
            for t in range(NTOK):
                mm = eng.matmul(ps[:, 4 + t // 4, (t % 4) * P:(t % 4 + 1) * P], xn[:, t * P:(t + 1) * P], mat("v1"),
                                start=True, stop=True)
                if t % 4 == 3:
                    mm.then_inc(s["p1_pe_v"].sem, 1)
            meet("pe", eng)

        def p1_dve(eng):
            z = s["p1_dve0"]
            for k in range(2):
                for c in range(2):
                    eng.memset(vpad[k][c], 0.0).then_inc(z.sem, 1)
            st = s["p1_dve"]
            pe = s["p1_pe"]
            with eng.Fori(0, NT) as i:
                for dst, b0, bb, cs, sn, nm in ((q1, 0, ("bq", "bqs"), "cosq", "sinq", "q"),
                                                (k1, 2, ("bk", "bks"), "cosk", "sink", "k")):
                    eng.wait_ge(pe.sem, pe.at(nm, i))
                    eng.scalar_tensor_tensor(out=two(tile(tmpa[0], i)), in0=two(bank(b0)), scalar=col(bb[0]),
                                             in1=tabseq(cs), op0=ALU.add, op1=ALU.mult).then_inc(st.sem, 1)
                    eng.scalar_tensor_tensor(out=two(tile(tmpa[1], i)), in0=two(bank(b0 + 1)), scalar=col(bb[1]),
                                             in1=tabseq(sn), op0=ALU.add, op1=ALU.mult).then_inc(st.sem, 1)
                    eng.wait_ge(st.sem, st.at(nm + "b", i))
                    eng.tensor_tensor(tile(dst, i), tile(tmpa[0], i), tile(tmpa[1], i), ALU.add)\
                       .then_inc(st.sem, 1)
                    eng.wait_ge(st.sem, st.at(nm, i))
            sv, pv = s["p1_dve_v"], s["p1_pe_v"]
            for i in range(NT):
                eng.wait_ge(pv.sem, pv.at("v", i))
                eng.tensor_copy(v1[:, i * T:(i + 1) * T], bank(4 + i)).then_inc(sv.sem, 1)
            meet("dve", eng)

        def dve_names(a):
            out = [f"{a}qs"] + [f"{a}kp{h}" for h in range(H)] + [f"{a}v0", f"{a}v1"]
            out += [f"{a}mx{n}" for n in range(3)]
            for u in range(4):
                for h in range(4 * u, 4 * u + 4):
                    out += [f"{a}c{h}"]
                    if u < 3 and h % 4 != 1:
                        out += [f"{a}mx{3 * (u + 1) + (0, None, 1, 2)[h % 4]}"]
            return out + [f"{a}den"]

        def pe_names1(a):
            out = [f"{a}S{n}" for n in range(3)]
            for h in range(H):
                if h < 12 and h % 4 != 1:
                    out += [f"{a}S{3 * (h // 4 + 1) + (0, None, 1, 2)[h % 4]}"]
                out += [f"{a}T{h}"]
                if h:
                    out += [f"{a}Y{h - 1}"]
            return out + [f"{a}Y{H - 1}"]

        def act_names1(a):
            out = []
            for u in range(4):
                out += [f"{a}e0_{h}" for h in range(4 * u, 4 * u + 4)] + [f"{a}e1_{h}" for h in range(4 * u, 4 * u + 4)]
            return out + [f"{a}y"]

        steps("c1_dve", dve_names(0) + dve_names(1), B // 2)
        steps("c1_pe", pe_names1(0) + pe_names1(1), B // 2)
        steps("c1_act", act_names1(0) + act_names1(1), B // 2)

        def c1_pe(eng):
            st, dv, ac = s["c1_pe"], s["c1_dve"], s["c1_act"]
            with eng.Fori(0, B // 2) as i:
                for a in range(2):
                    kp = kpad[a].rearrange("p (h k) -> p h k", h=H)

                    def S(n):
                        u, w = n // 3, n % 3
                        bk = ps[:, n % 4, :]
                        if n == 0:
                            eng.wait_ge(dv.sem, dv.at(f"{a}qs", i))
                        need = 4 * u + 4 if w == 0 else 4 * u + 2 * w
                        eng.wait_ge(dv.sem, dv.at(f"{a}kp{need - 1}", i))
                        if n >= 4:
                            m = n - 4
                            hl = 4 * (m // 3) + (3 if m % 3 == 0 else 2 * (m % 3) - 1)
                            eng.wait_ge(ac.sem, ac.at(f"{a}e{0 if m % 3 == 0 else 1}_{hl}", i))
                        if w == 0:
                            eng.matmul(bk.rearrange("p (h k) -> p h k", h=4), qst[a][:, 0:P],
                                       kp[:, 4 * u:4 * u + 4, 0:P], start=True, stop=False)
                            eng.matmul(bk.rearrange("p (h k) -> p h k", h=4), identb,
                                       causalb.rearrange("p (o k) -> p o k", o=1).broadcast_to([P, 4, P]),
                                       start=False, stop=True).then_inc(st.sem, 1)
                        else:
                            h0 = 4 * u + 2 * (w - 1)
                            o2 = bk.rearrange("p (h k) -> p h k", h=2)
                            eng.matmul(o2, qst[a][:, P:SEQ], kp[:, h0:h0 + 2, :], start=True, stop=False)
                            eng.matmul(o2[:, :, P:SEQ], identb,
                                       causalb.rearrange("p (o k) -> p o k", o=1).broadcast_to([P, 2, P]),
                                       start=False, stop=True).then_inc(st.sem, 1)

                    def tr(h):
                        u = h // 4
                        eng.wait_ge(ac.sem, ac.at(f"{a}e1_{h}", i))
                        if h >= 2:
                            eng.wait_ge(dv.sem, dv.at(f"{a}c{h - 2}", i))
                        pp0 = p0[u % 2][:, (h % 4) * P:(h % 4 + 1) * P]
                        pp1 = p1[u % 2][:, (h % 4) * SEQ:(h % 4 + 1) * SEQ]
                        bk = ps[:, 4 + h % 2, :]
                        eng.transpose(bk[:, 0:P], pp0, ident)
                        eng.transpose(bk[:, P:2 * P], pp1[:, 0:P], ident)
                        eng.transpose(bk[:, 2 * P:3 * P], pp1[:, P:SEQ], ident).then_inc(st.sem, 1)

                    def pv(h):
                        eng.wait_ge(dv.sem, dv.at(f"{a}c{h}", i))
                        if h == 0 and a == 0:
                            eng.wait_ge(ac.sem, i * ac.per + ac.base)
                        yy = ps[:, 6 + a, 0:SEQ]
                        eng.matmul(yy, vpad[a][0][:, h * P:(h + 1) * P], pT[h % 3][:, 0:SEQ],
                                   start=(h == 0), stop=False, skip_group_check=True)
                        eng.matmul(yy[:, P:SEQ], vpad[a][1][:, h * P:(h + 1) * P], pT[h % 3][:, SEQ:SEQ + P],
                                   start=False, stop=(h == H - 1), skip_group_check=True).then_inc(st.sem, 1)

                    for n in range(3):
                        S(n)
                    for h in range(H):
                        if h < 12 and h % 4 != 1:
                            S(3 * (h // 4 + 1) + (0, None, 1, 2)[h % 4])
                        tr(h)
                        if h:
                            pv(h - 1)
                    pv(H - 1)
            meet("pe", eng)

        def c1_act(eng):
            st, pe, dv = s["c1_act"], s["c1_pe"], s["c1_dve"]
            with eng.Fori(0, B // 2) as i:
                for a in range(2):
                    for u in range(4):
                        for h in range(4 * u, 4 * u + 4):
                            n = 3 * u
                            if h == 4 * u:
                                eng.wait_ge(dv.sem, dv.at(f"{a}mx{n}", i))
                                if u >= 2:
                                    eng.wait_ge(pe.sem, pe.at(f"{a}T{4 * u - 5}", i))
                            eng.activation(p0[u % 2][:, (h % 4) * P:(h % 4 + 1) * P],
                                           ps[:, n % 4, (h % 4) * P:(h % 4 + 1) * P], ACT.Exp,
                                           bias=nmx[:, 32 * a + h:32 * a + h + 1],
                                           accum_out=den1[:, 32 * a + h:32 * a + h + 1]).then_inc(st.sem, 1)
                        for h in range(4 * u, 4 * u + 4):
                            n = 3 * u + 1 + (h % 4) // 2
                            if h % 2 == 0:
                                eng.wait_ge(dv.sem, dv.at(f"{a}mx{n}", i))
                            eng.activation(p1[u % 2][:, (h % 4) * SEQ:(h % 4 + 1) * SEQ],
                                           ps[:, n % 4, (h % 2) * SEQ:(h % 2 + 1) * SEQ], ACT.Exp,
                                           bias=nmx[:, 32 * a + 16 + h:32 * a + 17 + h],
                                           accum_out=den1[:, 32 * a + 16 + h:32 * a + 17 + h]).then_inc(st.sem, 1)
                    eng.wait_ge(pe.sem, pe.at(f"{a}Y{H - 1}", i))
                    eng.activation(y1[:, bass.ds((i * 2 + a) * SEQ, SEQ)], ps[:, 6 + a, 0:SEQ], ACT.Copy)\
                       .then_inc(st.sem, 1)
            meet("act", eng)

        def c1_dve(eng):
            st, pe, ac = s["c1_dve"], s["c1_pe"], s["c1_act"]
            with eng.Fori(0, B // 2) as i:
                for a in range(2):
                    b = i * 2 + a
                    eng.tensor_copy(qst[a], q1[:, bass.ds(b * SEQ, SEQ)]).then_inc(st.sem, 1)
                    for h in range(H):
                        eng.tensor_scalar(kpad[a][:, h * SEQ:(h + 1) * SEQ], k1[:, bass.ds(b * SEQ, SEQ)],
                                          tab("hmask")[:, h:h + 1], None, ALU.mult).then_inc(st.sem, 1)
                    for c in range(2):
                        eng.tensor_copy(vpad[a][c].rearrange("p (h c) -> p h c", c=136)[:, :, 0:HD],
                                        v1[:, bass.ds(b * SEQ + c * P, P)].rearrange("p (h c) -> p h c", c=HD))\
                           .then_inc(st.sem, 1)

                    def mx(n):
                        u, w = n // 3, n % 3
                        eng.wait_ge(pe.sem, pe.at(f"{a}S{n}", i))
                        if w == 0:
                            eng.tensor_reduce(nmx[:, 32 * a + 4 * u:32 * a + 4 * u + 4],
                                              ps[:, n % 4, :].rearrange("p (h k) -> p h k", h=4), AX_X, ALU.max,
                                              negate=True).then_inc(st.sem, 1)
                        else:
                            h0 = 32 * a + 16 + 4 * u + 2 * (w - 1)
                            eng.tensor_reduce(nmx[:, h0:h0 + 2], ps[:, n % 4, :].rearrange("p (h k) -> p h k", h=2),
                                              AX_X, ALU.max, negate=True).then_inc(st.sem, 1)

                    for n in range(3):
                        mx(n)
                    for h in range(H):
                        eng.wait_ge(pe.sem, pe.at(f"{a}T{h}", i))
                        if h >= 3:
                            eng.wait_ge(pe.sem, pe.at(f"{a}Y{h - 3}", i))
                        eng.tensor_copy(pT[h % 3], ps[:, 4 + h % 2, 0:3 * P]).then_inc(st.sem, 1)
                        if h < 12 and h % 4 != 1:
                            mx(3 * (h // 4 + 1) + (0, None, 1, 2)[h % 4])
                    eng.wait_ge(ac.sem, ac.at(f"{a}e1_{H - 1}", i))
                    eng.tensor_copy(den_all[:, bass.ds(b * 32, 32)], den1[:, 32 * a:32 * a + 32])\
                       .then_inc(st.sem, 1)
            meet("dve", eng)

        steps("o1_dve0", ["rden", "rT"])
        steps("o1_dve", ["y", "yb"], NT, "o1_dve0")
        steps("o1_dve2", ["x"], NT, "o1_dve")
        steps("o1_pe0", ["rT"])
        steps("o1_pe", ["bc"], NT, "o1_pe0")
        steps("o1_pe2", ["o"], NT, "o1_pe")

        def o1_pe(eng):
            dz = s["o1_dve0"]
            eng.wait_ge(dz.sem, dz.at("rden"))
            for t in range(NTOK):
                mm = eng.transpose(ps[0:16, 4 + t // 4, (t % 4) * P:(t % 4 + 1) * P],
                                   rden_all[:, t * H:(t + 1) * H], ident)
            mm.then_inc(s["o1_pe0"].sem, 1)
            eng.wait_ge(dz.sem, dz.at("rT"))
            with eng.Fori(0, NT) as i:
                eng.matmul(bank(i), tab("sel16", 16), tile(rT, i), start=True, stop=True)\
                   .then_inc(s["o1_pe"].sem, 1)
            with eng.Fori(0, NT) as i:
                q = s["o1_dve"]
                eng.wait_ge(q.sem, q.at("yb", i))
                eng.matmul(bank(i + 4), mat("p1"), tile(y1, i), start=True, stop=True)\
                   .then_inc(s["o1_pe2"].sem, 1)
            meet("pe", eng)

        def o1_dve(eng):
            dz = s["o1_dve0"]
            eng.reciprocal(rden_all, den_all).then_inc(dz.sem, 1)
            q = s["o1_pe0"]
            eng.wait_ge(q.sem, q.at("rT"))
            eng.tensor_copy(rT, ps[0:16, 4:8, :].rearrange("p a t -> p (a t)")).then_inc(dz.sem, 1)
            st = s["o1_dve"]
            with eng.Fori(0, NT) as i:
                q = s["o1_pe"]
                eng.wait_ge(q.sem, q.at("bc", i))
                eng.tensor_tensor(tile(y1, i), tile(y1, i), bank(i), ALU.mult).then_inc(st.sem, 1)
                eng.wait_ge(st.sem, st.at("y", i))
                eng.tensor_scalar(tile(y1, i), tile(y1, i), col("bv"), None, ALU.add).then_inc(st.sem, 1)
            with eng.Fori(0, NT) as i:
                q = s["o1_pe2"]
                eng.wait_ge(q.sem, q.at("o", i))
                eng.scalar_tensor_tensor(out=tile(x, i), in0=bank(i + 4), scalar=col("bp"), in1=tile(x, i),
                                         op0=ALU.add, op1=ALU.add).then_inc(s["o1_dve2"].sem, 1)
            meet("dve", eng)

        ha = [work[:, k * N:(k + 1) * N] for k in range(4)]
        hb = [work[:, (4 + k) * N:(5 + k) * N] for k in range(4)]
        tern = {}
        at = 0
        for nm, n in (("w1", 512), ("w2", 512), ("h1", 2048), ("h2", 2048), ("w3", 512)):
            tern[nm] = wb[:, at:at + n]
            at += n
        sgl = [work[:, 16384 + k * T:16384 + (k + 1) * T] for k in range(2)]
        steps("g1_pe_a", [f"{w}{j}" for j in range(4) for w in "gu"], NT)
        steps("g1_pe_b", [f"o{j}" for j in range(4)], NT, "g1_pe_a")
        steps("g1_pe_c", [f"o{j}" for j in range(4)], NT, "g1_pe_b")
        steps("g1_pe_d", ["y"], NT, "g1_pe_c")
        steps("g1_act_a", [f"s{j}" for j in range(4)], NT)
        steps("g1_act_b", [f"h{j}" for j in range(4)], NT, "g1_act_a")
        steps("g1_act_c", [f"h{j}" for j in range(4)], NT, "g1_act_b")
        steps("g1_dve_a", [f"h{j}" for j in range(4)], NT)
        steps("g1_dve_d", ["x"], NT, "g1_dve_a")

        def g1_pe(eng):
            st, dv = s["g1_pe_a"], s["g1_dve_a"]
            eng.wait_ge(ld_w1, 16)
            with eng.Fori(0, NT) as i:
                for j in range(4):
                    if j >= 2:
                        eng.wait_ge(dv.sem, dv.at(f"h{j - 2}", i))
                    else:
                        eng.wait_ge(dv.sem, i * dv.per + dv.base)
                    eng.matmul(bank(j % 2), tern["w1"][:, j * P:(j + 1) * P], tile(xn, i), start=True, stop=True)\
                       .then_inc(st.sem, 1)
                    eng.matmul(bank(2 + j % 2), tern["w2"][:, j * P:(j + 1) * P], tile(xn, i), start=True, stop=True)\
                       .then_inc(st.sem, 1)
            for nm, src, key, akey in (("h1", ha, "g1_pe_b", "g1_act_b"), ("h2", hb, "g1_pe_c", "g1_act_c")):
                st, ac = s[key], s[akey]
                with eng.Fori(0, NT) as i:
                    if nm == "h1":
                        eng.wait_ge(dv.sem, dv.turn_end(i))
                    else:
                        pa = s["g1_act_b"]
                        eng.wait_ge(pa.sem, pa.turn_end(i))
                    for o in range(4):
                        eng.wait_ge(ac.sem, i * ac.per + (ac.base - ac.per + o + 1))
                        for k in range(4):
                            mm = eng.matmul(bank(4 + o), tern[nm][:, k * 512 + o * P:k * 512 + (o + 1) * P],
                                            tile(src[k], i), start=(k == 0), stop=(k == 3))
                        mm.then_inc(st.sem, 1)
            st, ac, dv = s["g1_pe_d"], s["g1_act_c"], s["g1_dve_d"]
            with eng.Fori(0, NT) as i:
                eng.wait_ge(ac.sem, ac.turn_end(i))
                for k in range(4):
                    mm = eng.matmul(bank(i), tern["w3"][:, k * P:(k + 1) * P], tile(ha[k], i),
                                    start=(k == 0), stop=(k == 3))
                mm.then_inc(st.sem, 1)
            meet("pe", eng)

        def g1_act(eng):
            st, pe, dv = s["g1_act_a"], s["g1_pe_a"], s["g1_dve_a"]
            with eng.Fori(0, NT) as i:
                for j in range(4):
                    eng.wait_ge(pe.sem, pe.at(f"g{j}", i))
                    if j >= 2:
                        eng.wait_ge(dv.sem, dv.at(f"h{j - 2}", i))
                    else:
                        eng.wait_ge(dv.sem, i * dv.per + dv.base)
                    eng.activation(sgl[j % 2], bank(j % 2), ACT.Silu, scale=col("w1_s", j)).then_inc(st.sem, 1)
            for key, pkey, dst, sc in (("g1_act_b", "g1_pe_b", hb, "h1_s"), ("g1_act_c", "g1_pe_c", ha, "h2_s")):
                st, pe = s[key], s[pkey]
                with eng.Fori(0, NT) as i:
                    for o in range(4):
                        eng.wait_ge(pe.sem, pe.at(f"o{o}", i))
                        eng.activation(tile(dst[o], i), bank(4 + o), ACT.Gelu, scale=col(sc, o)).then_inc(st.sem, 1)
            meet("act", eng)

        def g1_dve(eng):
            st, pe, ac = s["g1_dve_a"], s["g1_pe_a"], s["g1_act_a"]
            with eng.Fori(0, NT) as i:
                for j in range(4):
                    eng.wait_ge(pe.sem, pe.at(f"u{j}", i))
                    eng.wait_ge(ac.sem, ac.at(f"s{j}", i))
                    eng.scalar_tensor_tensor(out=tile(ha[j], i), in0=bank(2 + j % 2), scalar=col("w2_s", j),
                                             in1=sgl[j % 2], op0=ALU.mult, op1=ALU.mult).then_inc(st.sem, 1)
            st, pe = s["g1_dve_d"], s["g1_pe_d"]
            with eng.Fori(0, NT) as i:
                eng.wait_ge(pe.sem, pe.at("y", i))
                eng.scalar_tensor_tensor(out=tile(x, i), in0=bank(i), scalar=col("w3_s"), in1=tile(x, i),
                                         op0=ALU.mult, op1=ALU.add).then_inc(st.sem, 1)
            meet("dve", eng)

        r2, k2, v2 = [work[:, k * N:(k + 1) * N] for k in range(3)]
        y2 = r2
        rpad = [work[:, 6144 + k * 4096:6144 + (k + 1) * 4096] for k in range(1)] * 2
        vp2 = [work[:, 10240 + c * VP:10240 + (c + 1) * VP] for c in range(2)]
        decay = work[:, 14592:14592 + 2048]
        kst = work[:, 16640:16640 + SEQ]
        aT = [work[:, 16896 + k * 512:16896 + (k + 1) * 512] for k in range(3)]
        kw = wb[:, 0:1024]
        s0 = wb[:, 1024:2048]
        wkt = wb[:, 2048:2064]
        wbt = wb[:, 2064:2192]
        lam = wb[:, 2192:2192 + 16]
        lamc = wb[:, 2208:2209]
        expo = wb[:, 2216:2232]
        g2 = wb[:, 2304:4352]
        steps("t2_act0", ["lam", "lamc", "wk", "wb"] + [f"d{h}" for h in range(H)])
        steps("t2_dve0", ["lamm", "lamcm", "ex"] + [f"m{h}" for h in range(H)] + [f"u{h}" for h in range(H)]
              )
        mix = {"r": work[:, 6144:8192], "k": work[:, 8192:10240], "v": work[:, 10240:12288],
               "g": work[:, 12288:14336]}
        xxs = g2
        steps("p2_dve", ["xx", "xx0", "xr", "xk", "xv", "xg"], 1, "t2_dve0")
        steps("p2_dve1", ["r", "k"], NT, "p2_dve")
        steps("p2_dve2", ["v"], NT, "p2_dve1")
        steps("p2_dve3", ["kw0", "kw1", "s00", "s01"], 1, "p2_dve2")
        steps("p2_act", ["g"], NT, "t2_act0")
        steps("p2_pe", ["r", "k", "g"], NT)
        steps("p2_pe_v", ["v"], NT, "p2_pe")
        steps("p2_pe_k", ["k0", "k1", "s0"], 1, "p2_pe_v")

        def t2_act(eng):
            st, dv = s["t2_act0"], s["t2_dve0"]
            eng.activation(lam, colv("td_bc"), ACT.Exp).then_inc(st.sem, 1)
            eng.activation(lamc, col("td_ch"), ACT.Exp).then_inc(st.sem, 1)
            eng.wait_ge(dv.sem, dv.at("ex"))
            eng.activation(wkt, expo, ACT.Exp).then_inc(st.sem, 1)
            eng.activation(wbt, tab("iota_q"), ACT.Exp, scale=lamc).then_inc(st.sem, 1)
            for h in range(H):
                eng.activation(decay[:, h * P:(h + 1) * P], tab("lag"), ACT.Exp, scale=lam[:, h:h + 1])\
                   .then_inc(st.sem, 1)

        def t2_dve(eng):
            st, ac = s["t2_dve0"], s["t2_act0"]
            eng.wait_ge(ac.sem, ac.at("lamc"))
            eng.tensor_scalar(lam, lam, 1e30, -1.0, ALU.min, ALU.mult).then_inc(st.sem, 1)
            eng.tensor_scalar(lamc, lamc, 1e30, -1.0, ALU.min, ALU.mult).then_inc(st.sem, 1)
            eng.wait_ge(st.sem, st.at("lamm"))
            eng.tensor_scalar(expo, lam, tab("rev_j"), None, ALU.mult).then_inc(st.sem, 1)
            for h in range(H):
                dh = decay[:, h * P:(h + 1) * P]
                eng.wait_ge(ac.sem, ac.at(f"d{h}"))
                eng.tensor_tensor(dh, dh, tab("before"), ALU.mult).then_inc(st.sem, 1)
            for h in range(H):
                dh = decay[:, h * P:(h + 1) * P]
                eng.wait_ge(st.sem, st.at(f"m{h}"))
                eng.scalar_tensor_tensor(out=dh, in0=ident, scalar=cols[:, COL_AT["u_bc"][0] + h:COL_AT["u_bc"][0] + h + 1],
                                         in1=dh, op0=ALU.mult, op1=ALU.add).then_inc(st.sem, 1)
            eng.wait_ge(st.sem, st.at(f"u{H - 1}"))

        def p2_pe(eng):
            st, dv = s["p2_pe"], s["p2_dve"]
            d1, ac = s["p2_dve1"], s["p2_act"]
            eng.wait_ge(dv.sem, dv.at("xg"))
            with eng.Fori(0, NT) as i:
                eng.wait_ge(d1.sem, i * d1.per + d1.base)
                eng.matmul(bank(0), mat("r2"), tile(mix["r"], i), start=True, stop=True).then_inc(st.sem, 1)
                eng.matmul(bank(1), mat("k2"), tile(mix["k"], i), start=True, stop=True).then_inc(st.sem, 1)
                eng.wait_ge(ac.sem, i * ac.per + ac.base)
                eng.matmul(bank(2), mat("g2"), tile(mix["g"], i), start=True, stop=True).then_inc(st.sem, 1)
            sv = s["p2_pe_v"]
            for t in range(NTOK):
                mm = eng.matmul(ps[:, 4 + t // 4, (t % 4) * P:(t % 4 + 1) * P], mix["v"][:, t * P:(t + 1) * P],
                                mat("v2"), start=True, stop=True)
                if t % 4 == 3:
                    mm.then_inc(sv.sem, 1)
            sk = s["p2_pe_k"]
            eng.wait_ge(d1.sem, d1.end)
            for b in range(B):
                mm = eng.matmul(ps[:, b // 4, (b % 4) * P:(b % 4 + 1) * P], mix["k"][:, b * SEQ:b * SEQ + P],
                                mat("k2"), start=True, stop=True)
                if b % 4 == 3:
                    mm.then_inc(sk.sem, 1)
            d3, d2 = s["p2_dve3"], s["p2_dve2"]
            eng.wait_ge(ac.sem, ac.end)
            eng.wait_ge(d3.sem, d3.at("kw1"))
            for b in range(B):
                mm = eng.matmul(ps[:, 2 + b // 4, (b % 4) * P:(b % 4 + 1) * P], kw[:, b * P:(b + 1) * P],
                                v2[:, b * SEQ:b * SEQ + P], start=True, stop=True)
            mm.then_inc(sk.sem, 1)
            meet("pe", eng)

        def p2_act(eng):
            st, pe = s["p2_act"], s["p2_pe"]
            dv = s["p2_dve"]
            eng.wait_ge(dv.sem, dv.at("xg"))
            with eng.Fori(0, NT) as i:
                eng.wait_ge(pe.sem, pe.at("g", i))
                eng.activation(tile(g2, i), bank(2), ACT.Silu).then_inc(st.sem, 1)
            meet("act", eng)

        def p2_dve(eng):
            st = s["p2_dve"]
            x3 = xn[:, :].rearrange("p (b t) -> p b t", t=SEQ)
            d3 = xxs.rearrange("p (b t) -> p b t", t=SEQ)
            eng.tensor_tensor(d3[:, :, 1:SEQ], x3[:, :, 0:SEQ - 1], x3[:, :, 1:SEQ], ALU.subtract)\
               .then_inc(st.sem, 1)
            eng.tensor_scalar(d3[:, :, 0:1], x3[:, :, 0:1], -1.0, None, ALU.mult).then_inc(st.sem, 1)
            eng.wait_ge(st.sem, st.at("xx0"))
            for k in "rkvg":
                eng.scalar_tensor_tensor(out=mix[k], in0=xxs, scalar=col("maa_" + k), in1=xn[:, :],
                                         op0=ALU.mult, op1=ALU.add).then_inc(st.sem, 1)
            pe, d1 = s["p2_pe"], s["p2_dve1"]
            with eng.Fori(0, NT) as i:
                eng.wait_ge(pe.sem, pe.at("r", i))
                eng.tensor_copy(tile(r2, i), bank(0)).then_inc(d1.sem, 1)
                eng.wait_ge(pe.sem, pe.at("k", i))
                eng.tensor_copy(tile(k2, i), bank(1)).then_inc(d1.sem, 1)
            pv, d2 = s["p2_pe_v"], s["p2_dve2"]
            for i in range(NT):
                eng.wait_ge(pv.sem, pv.at("v", i))
                eng.tensor_copy(v2[:, i * T:(i + 1) * T], bank(4 + i)).then_inc(d2.sem, 1)
            pk, d3s = s["p2_pe_k"], s["p2_dve3"]
            wk = wkt.rearrange("p (o h c) -> p o h c", o=1, c=1).broadcast_to([P, 4, H, HD])
            for n in range(2):
                eng.wait_ge(pk.sem, pk.at(f"k{n}"))
                eng.tensor_tensor(kw[:, n * T:(n + 1) * T].rearrange("p (b h c) -> p b h c", h=H, c=HD),
                                  bank(n).rearrange("p (b h c) -> p b h c", h=H, c=HD), wk, ALU.mult)\
                   .then_inc(d3s.sem, 1)
            eng.wait_ge(pk.sem, pk.at("s0"))
            same = tab("grp").rearrange("p (o c) -> p o c", o=1).broadcast_to([P, 4, P])
            for n in range(2):
                eng.scalar_tensor_tensor(out=s0[:, n * T:(n + 1) * T].rearrange("p (b c) -> p b c", c=P),
                                         in0=bank(2 + n).rearrange("p (b c) -> p b c", c=P), scalar=float(HD),
                                         in1=same, op0=ALU.mult, op1=ALU.mult).then_inc(d3s.sem, 1)
            meet("dve", eng)

        steps("c2_dve0", ["z0", "z1"])
        steps("c2_dve", ["ks"] + [f"rp{h}" for h in range(H)] + ["v0", "v1"] + [f"a{n}" for n in range(8)], B, "c2_dve0")
        steps("c2_act", ["y"], B)
        steps("c2_pe", [f"S{n}" for n in range(3)] + [x_ for n in range(8) for x_ in
              ([f"S{n + 3}"] if n + 3 < 8 else []) + [f"Y{n}"]], B)

        def c2_pe(eng):
            st, dv, ac = s["c2_pe"], s["c2_dve"], s["c2_act"]
            rp = rpad[0].rearrange("p (h q) -> p h q", h=H)
            eng.wait_ge(dv.sem, dv.base)
            with eng.Fori(0, B) as b:
                def S(n):
                    c, u = n // 4, n % 4
                    eng.wait_ge(dv.sem, dv.at(f"rp{4 * u + 3}", b))
                    if n >= 4:
                        eng.wait_ge(dv.sem, dv.at(f"a{n - 4}", b))
                    eng.matmul(ps[:, n % 4, :].rearrange("p (h q) -> p h q", h=4), kst[:, c * P:(c + 1) * P],
                               rp[:, 4 * u:4 * u + 4, c * P:(c + 1) * P], start=True, stop=True).then_inc(st.sem, 1)

                def Y(n):
                    c, u = n // 4, n % 4
                    eng.wait_ge(dv.sem, dv.at(f"a{n}", b))
                    if n == 0:
                        eng.wait_ge(ac.sem, b * ac.per + ac.base)
                    for h in range(4 * u, 4 * u + 4):
                        mm = eng.matmul(ps[:, 4, c * P:(c + 1) * P], vp2[c][:, h * P:(h + 1) * P],
                                        aT[n % 3][:, (h % 4) * P:(h % 4 + 1) * P],
                                        start=(h == 0), stop=(h == H - 1), skip_group_check=True)
                    mm.then_inc(st.sem, 1)

                for n in range(3):
                    S(n)
                for n in range(8):
                    if n + 3 < 8:
                        S(n + 3)
                    Y(n)
            meet("pe", eng)

        def c2_act(eng):
            st, pe = s["c2_act"], s["c2_pe"]
            with eng.Fori(0, B) as b:
                eng.wait_ge(pe.sem, pe.turn_end(b))
                eng.activation(y2q[:, bass.ds(b * SEQ, SEQ)], ps[:, 4, 0:SEQ], ACT.Copy).then_inc(st.sem, 1)
            meet("act", eng)

        def c2_dve(eng):
            z, st, pe = s["c2_dve0"], s["c2_dve"], s["c2_pe"]
            for c in range(2):
                eng.memset(vp2[c], 0.0).then_inc(z.sem, 1)
            eng.wait_ge(z.sem, z.end)
            with eng.Fori(0, B) as b:
                eng.wait_ge(pe.sem, b * pe.per + pe.base)
                eng.tensor_copy(kst, k2[:, bass.ds(b * SEQ, SEQ)]).then_inc(st.sem, 1)
                for h in range(H):
                    eng.tensor_scalar(rpad[0][:, h * SEQ:(h + 1) * SEQ], r2[:, bass.ds(b * SEQ, SEQ)],
                                      tab("hmask")[:, h:h + 1], None, ALU.mult).then_inc(st.sem, 1)
                for c in range(2):
                    eng.tensor_copy(vp2[c].rearrange("p (h c) -> p h c", c=136)[:, :, 0:HD],
                                    v2[:, bass.ds(b * SEQ + c * P, P)].rearrange("p (h c) -> p h c", c=HD))\
                       .then_inc(st.sem, 1)
                for n in range(8):
                    u = n % 4
                    eng.wait_ge(pe.sem, pe.at(f"S{n}", b))
                    if n >= 3:
                        eng.wait_ge(pe.sem, pe.at(f"Y{n - 3}", b))
                    eng.tensor_tensor(aT[n % 3], ps[:, n % 4, :], decay[:, u * 4 * P:(u + 1) * 4 * P], ALU.mult)\
                       .then_inc(st.sem, 1)
            meet("dve", eng)

        y2q = k2
        gn = {"c": work[:, 6144:8192], "q": work[:, 8192:10240], "r": work[:, 10240:12288]}
        rwb = work[:, 12288:13312]
        steps("o2_dve0", ["rw", "x0", "x1"])
        steps("o2_dve1", ["c"], NT, "o2_dve0")
        steps("o2_dve2", ["n", "b", "g"], NT, "o2_dve1")
        steps("o2_dve3", ["x"], NT, "o2_dve2")
        steps("o2_act1", ["sq"], NT)
        steps("o2_act2", ["log"], NT, "o2_act1")
        steps("o2_act3", ["rstd"], NT, "o2_act2")
        steps("o2_pe0", ["x"])
        steps("o2_pe1", ["mean"], NT, "o2_pe0")
        steps("o2_pe2", ["var"], NT, "o2_pe1")
        steps("o2_pe3", ["o"], NT, "o2_pe2")

        def o2_pe(eng):
            dz = s["o2_dve0"]
            eng.wait_ge(dz.sem, dz.at("rw"))
            for b in range(B):
                mm = eng.matmul(ps[:, b // 4, (b % 4) * P:(b % 4 + 1) * P], s0[:, b * P:(b + 1) * P],
                                rwb[:, b * P:(b + 1) * P], start=True, stop=True)
            mm.then_inc(s["o2_pe0"].sem, 1)
            eng.wait_ge(dz.sem, dz.at("x1"))
            with eng.Fori(0, NT) as i:
                eng.matmul(bank(i), tab("grp"), tile(y2q, i), start=True, stop=True).then_inc(s["o2_pe1"].sem, 1)
            with eng.Fori(0, NT) as i:
                q = s["o2_act1"]
                eng.wait_ge(q.sem, q.at("sq", i))
                eng.matmul(bank(i + 4), tab("grp"), tile(gn["q"], i), start=True, stop=True)\
                   .then_inc(s["o2_pe2"].sem, 1)
            with eng.Fori(0, NT) as i:
                q = s["o2_dve2"]
                eng.wait_ge(q.sem, q.at("g", i))
                eng.matmul(bank(i), mat("o2"), tile(gn["c"], i), start=True, stop=True).then_inc(s["o2_pe3"].sem, 1)
            meet("pe", eng)

        def o2_act(eng):
            with eng.Fori(0, NT) as i:
                q = s["o2_dve1"]
                eng.wait_ge(q.sem, q.at("c", i))
                eng.activation(tile(gn["q"], i), tile(gn["c"], i), ACT.Square).then_inc(s["o2_act1"].sem, 1)
            with eng.Fori(0, NT) as i:
                q = s["o2_pe2"]
                eng.wait_ge(q.sem, q.at("var", i))
                eng.activation(tile(gn["r"], i), bank(i + 4), ACT.Ln, bias=eps_ap(EPS_GN), scale=DOWN)\
                   .then_inc(s["o2_act2"].sem, 1)
            with eng.Fori(0, NT) as i:
                q = s["o2_act2"]
                eng.wait_ge(q.sem, q.at("log", i))
                eng.activation(tile(gn["r"], i), tile(gn["r"], i), ACT.Exp, bias=epst[:, 4:5], scale=-0.5)\
                   .then_inc(s["o2_act3"].sem, 1)
            meet("act", eng)

        def o2_dve(eng):
            st = s["o2_dve0"]
            r3 = r2.rearrange("p (b t) -> p b t", t=SEQ)
            y3 = y2q.rearrange("p (b t) -> p b t", t=SEQ)
            eng.tensor_tensor(rwb.rearrange("p (b q) -> p b q", q=P), r3[:, :, P:SEQ],
                              wbt.rearrange("p (o q) -> p o q", o=1).broadcast_to([P, B, P]), ALU.mult)\
               .then_inc(st.sem, 1)
            q = s["o2_pe0"]
            eng.wait_ge(q.sem, q.at("x"))
            for n in range(2):
                yy = y3[:, 4 * n:4 * n + 4, P:SEQ]
                eng.tensor_tensor(yy, yy, bank(n).rearrange("p (b q) -> p b q", q=P), ALU.add).then_inc(st.sem, 1)
            with eng.Fori(0, NT) as i:
                q = s["o2_pe1"]
                eng.wait_ge(q.sem, q.at("mean", i))
                eng.tensor_tensor(tile(gn["c"], i), tile(y2q, i), bank(i), ALU.subtract)\
                   .then_inc(s["o2_dve1"].sem, 1)
            st = s["o2_dve2"]
            with eng.Fori(0, NT) as i:
                q = s["o2_act3"]
                eng.wait_ge(q.sem, q.at("rstd", i))
                eng.scalar_tensor_tensor(out=tile(gn["c"], i), in0=tile(gn["c"], i), scalar=col("ln_g"),
                                         in1=tile(gn["r"], i), op0=ALU.mult, op1=ALU.mult).then_inc(st.sem, 1)
                eng.wait_ge(st.sem, st.at("n", i))
                eng.tensor_scalar(tile(gn["c"], i), tile(gn["c"], i), col("ln_b"), None, ALU.add)\
                   .then_inc(st.sem, 1)
                eng.wait_ge(st.sem, st.at("b", i))
                eng.tensor_tensor(tile(gn["c"], i), tile(gn["c"], i), tile(g2, i), ALU.mult).then_inc(st.sem, 1)
            with eng.Fori(0, NT) as i:
                q = s["o2_pe3"]
                eng.wait_ge(q.sem, q.at("o", i))
                eng.tensor_tensor(tile(x, i), tile(x, i), bank(i), ALU.add).then_inc(s["o2_dve3"].sem, 1)
            meet("dve", eng)

        NB2 = E * HID2 // P
        e_g = [work[:, k * T:(k + 1) * T] for k in range(3)]
        e_h = [work[:, (3 + k) * T:(4 + k) * T] for k in range(3)]
        pn = []
        for k in range(NB2 + 2):
            if k < NB2:
                if k % 4 == 0:
                    pn += [f"w{k // 4}"]
                pn += [f"g{k}"]
            if k >= 2:
                pn += [f"d{k - 2}"]
        steps("e2_pe", pn, NT)
        steps("e2_act", [f"g{k}" for k in range(NB2)], NT)
        steps("e2_dve", [f"h{k}" for k in range(NB2)] + ["x"], NT)

        def e2_pe(eng):
            st, ac, dv = s["e2_pe"], s["e2_act"], s["e2_dve"]
            eng.wait_ge(b_parts, 48 * moves[2])
            with eng.Fori(0, NT) as i:
                for k in range(NB2 + 2):
                    if k < NB2:
                        e = k // 4
                        if k % 4 == 0:
                            eng.wait_ge(b_parts, 48 * moves[2])
                            if e >= 2:
                                eng.wait_ge(dv.sem, dv.at(f"h{4 * (e - 1) - 1}", i))
                            eng.matmul(bank(4 + e % 2), sel_e[e], tile(w24, i), start=True, stop=True)\
                               .then_inc(st.sem, 1)
                        if k >= 3:
                            eng.wait_ge(ac.sem, ac.at(f"g{k - 3}", i))
                        eng.matmul(bank(k % 3), wa[:, k * P:(k + 1) * P], tile(xn, i), start=True, stop=True)\
                           .then_inc(st.sem, 1)
                    if k >= 2:
                        j = k - 2
                        if j == 0:
                            eng.wait_ge(b_parts, 48 * moves[2])
                            eng.wait_ge(dv.sem, i * dv.per + dv.base)
                            eng.matmul(bank(6), b2rows[:, :], tile(wT, i), start=True, stop=False)
                        eng.wait_ge(dv.sem, dv.at(f"h{j}", i))
                        eng.matmul(bank(6), wa[:, E * HID2 + j * P:E * HID2 + (j + 1) * P], e_h[j % 3],
                                   start=False, stop=(j == NB2 - 1)).then_inc(st.sem, 1)
            meet("pe", eng)

        def e2_act(eng):
            st, pe, dv = s["e2_act"], s["e2_pe"], s["e2_dve"]
            with eng.Fori(0, NT) as i:
                for k in range(NB2):
                    eng.wait_ge(pe.sem, pe.at(f"g{k}", i))
                    if k >= 3:
                        eng.wait_ge(dv.sem, dv.at(f"h{k - 3}", i))
                    eng.activation(e_g[k % 3], bank(k % 3), ACT.Gelu, bias=col("b1_2", k)).then_inc(st.sem, 1)
            meet("act", eng)

        def e2_dve(eng):
            st, pe, ac = s["e2_dve"], s["e2_pe"], s["e2_act"]
            with eng.Fori(0, NT) as i:
                for k in range(NB2):
                    if k % 4 == 0:
                        eng.wait_ge(pe.sem, pe.at(f"w{k // 4}", i))
                    eng.wait_ge(ac.sem, ac.at(f"g{k}", i))
                    if k >= 3:
                        eng.wait_ge(pe.sem, pe.at(f"d{k - 3}", i))
                    eng.tensor_tensor(e_h[k % 3], e_g[k % 3], bank(4 + (k // 4) % 2), ALU.mult).then_inc(st.sem, 1)
                eng.wait_ge(pe.sem, pe.at(f"d{NB2 - 1}", i))
                eng.tensor_tensor(tile(x, i), tile(x, i), bank(6), ALU.add).then_inc(st.sem, 1)
            meet("dve", eng)

        q3, k3, v3 = [work[:, k * N:(k + 1) * N] for k in range(3)]
        SC3 = 1.0 / float(P) ** 0.5
        steps("p3_pe", ["q", "k"], NT)
        steps("p3_pe_v", ["v"], NT, "p3_pe")
        steps("p3_dve", ["q", "k"], NT)
        steps("p3_dve_v", ["v"], NT, "p3_dve")

        def p3_pe(eng):
            st, dv = s["p3_pe"], s["p3_dve"]
            with eng.Fori(0, NT) as i:
                eng.wait_ge(dv.sem, i * dv.per + dv.base)
                eng.matmul(bank(0), mat("q3"), tile(xn, i), start=True, stop=True).then_inc(st.sem, 1)
                eng.matmul(bank(1), mat("k3"), tile(xn, i), start=True, stop=True).then_inc(st.sem, 1)
            for t in range(NTOK):
                mm = eng.matmul(ps[:, 4 + t // 4, (t % 4) * P:(t % 4 + 1) * P], xn[:, t * P:(t + 1) * P], mat("v3"),
                                start=True, stop=True)
                if t % 4 == 3:
                    mm.then_inc(s["p3_pe_v"].sem, 1)
            meet("pe", eng)

        def p3_dve(eng):
            st, pe = s["p3_dve"], s["p3_pe"]
            with eng.Fori(0, NT) as i:
                for nm, dst, k in (("q", q3, 0), ("k", k3, 1)):
                    eng.wait_ge(pe.sem, pe.at(nm, i))
                    eng.tensor_copy(tile(dst, i), bank(k)).then_inc(st.sem, 1)
            for i in range(NT):
                q = s["p3_pe_v"]
                eng.wait_ge(q.sem, q.at("v", i))
                eng.tensor_copy(v3[:, i * T:(i + 1) * T], bank(4 + i)).then_inc(s["p3_dve_v"].sem, 1)
            meet("dve", eng)

        c3 = 6144
        pr3 = [work[:, c3 + k * 512:c3 + (k + 1) * 512] for k in range(2)]
        vs3 = [work[:, c3 + 1024 + k * SEQ:c3 + 1024 + (k + 1) * SEQ] for k in range(2)]
        sm3 = [work[:, c3 + 2048 + k * 16:c3 + 2048 + (k + 1) * 16] for k in range(2)]
        steps("c3_pe", [f"{a}{w}" for a in range(2) for w in ("S", "o")], B // 2)
        steps("c3_act", [f"{a}e{c}" for a in range(2) for c in range(2)], B // 2)
        steps("c3_dve", [f"{a}{w}" for a in range(2) for w in ("mx", "nb", "rd", "v0", "v1", "x")], B // 2)

        kst3 = [work[:, c3 + 3072 + k * SEQ:c3 + 3072 + (k + 1) * SEQ] for k in range(2)]
        steps("c3_pool", ["0k", "1k"], B // 2)

        def c3_pool(eng):
            st, pe = s["c3_pool"], s["c3_pe"]
            with eng.Fori(0, B // 2) as i:
                for a in range(2):
                    eng.wait_ge(pe.sem, i * pe.per + pe.base)
                    eng.tensor_copy(kst3[a], k3[:, bass.ds((i * 2 + a) * SEQ, SEQ)]).then_inc(st.sem, 1)
            meet("pool", eng)

        def c3_pe(eng):
            st, dv, ac, po = s["c3_pe"], s["c3_dve"], s["c3_act"], s["c3_pool"]
            with eng.Fori(0, B // 2) as i:
                for a in range(2):
                    b = i * 2 + a
                    eng.wait_ge(po.sem, po.at(f"{a}k", i))
                    eng.wait_ge(dv.sem, i * dv.per + dv.base)
                    for c in range(2):
                        mm = eng.matmul(ps[:, a, c * SEQ:(c + 1) * SEQ], kst3[a][:, c * P:(c + 1) * P],
                                        q3[:, bass.ds(b * SEQ, SEQ)], start=True, stop=True)
                    mm.then_inc(st.sem, 1)
                    eng.wait_ge(dv.sem, dv.at(f"{a}v1", i))
                    for c in range(2):
                        mm = eng.matmul(ps[:, 2 + a, 0:SEQ], vs3[a][:, c * P:(c + 1) * P],
                                        pr3[a][:, c * SEQ:(c + 1) * SEQ], start=(c == 0), stop=(c == 1))
                    mm.then_inc(st.sem, 1)
            meet("pe", eng)

        def c3_act(eng):
            st, dv = s["c3_act"], s["c3_dve"]
            with eng.Fori(0, B // 2) as i:
                for a in range(2):
                    eng.wait_ge(dv.sem, dv.at(f"{a}nb", i))
                    for c in range(2):
                        eng.activation(pr3[a][:, c * SEQ:(c + 1) * SEQ], ps[:, a, c * SEQ:(c + 1) * SEQ], ACT.Exp,
                                       bias=sm3[a][:, 2 + c:3 + c], scale=SC3,
                                       accum_out=sm3[a][:, 4 + c:5 + c]).then_inc(st.sem, 1)
            meet("act", eng)

        def c3_dve(eng):
            st, pe, ac = s["c3_dve"], s["c3_pe"], s["c3_act"]
            with eng.Fori(0, B // 2) as i:
                for a in range(2):
                    b = i * 2 + a
                    eng.wait_ge(pe.sem, pe.at(f"{a}S", i))
                    eng.tensor_reduce(sm3[a][:, 0:2], ps[:, a, :].rearrange("p (c q) -> p c q", c=2), AX_X, ALU.max)\
                       .then_inc(st.sem, 1)
                    eng.wait_ge(st.sem, st.at(f"{a}mx", i))
                    eng.tensor_scalar(sm3[a][:, 2:4], sm3[a][:, 0:2], -SC3, None, ALU.mult).then_inc(st.sem, 1)
                    eng.wait_ge(ac.sem, ac.at(f"{a}e1", i))
                    eng.reciprocal(sm3[a][:, 6:8], sm3[a][:, 4:6]).then_inc(st.sem, 1)
                    eng.wait_ge(st.sem, st.at(f"{a}rd", i))
                    for c in range(2):
                        eng.tensor_scalar(vs3[a][:, c * P:(c + 1) * P], v3[:, bass.ds(b * SEQ + c * P, P)],
                                          sm3[a][:, 6 + c:7 + c], None, ALU.mult).then_inc(st.sem, 1)
                    eng.wait_ge(pe.sem, pe.at(f"{a}o", i))
                    xt = x[:, bass.ds(b * SEQ, SEQ)]
                    eng.tensor_tensor(xt, xt, ps[:, 2 + a, 0:SEQ], ALU.add).then_inc(st.sem, 1)
            meet("dve", eng)

        PHASES = ["ln0", "a0", "r0", "f0", "ln1", "p1", "c1", "o1", "g1", "ln2", "t2", "c2", "o2", "r2", "e2",
                  "ln3", "p3", "c3", "r3", "f3"]
        WA_FREE = PHASES.index("o1") + 2
        ALL = len(PHASES) + 1

        filled = sem("filled")
        block = ctx.enter_context(nc.Block())

        @block.sync
        def _(eng):
            eng.dma_start(x[:, :], d["x"]).then_inc(ld_x, 16)
            eng.dma_start(tabs[:, :], d["tabs"]).then_inc(ld_x, 16)
            eng.dma_start(mats[:, :], d["mats"]).then_inc(ld_small, 16)
            eng.dma_start(cols[:, :], d["cols"]).then_inc(ld_small, 16)
            eng.dma_start(work[:, 0:(E + 2) * P], d["bft"]).then_inc(ld_small, 16)
            eng.dma_start(b2rows[:, :], d["b2rows"]).then_inc(ld_small, 16)
            eng.dma_start(wa[:, :], d["w0"]).then_inc(ld_w0, 16)
            eng.dma_start(wb[:, :], d["w1"]).then_inc(ld_w1, 16)
            r_sync(0, eng)
            for n in met:
                eng.wait_ge(met[n], WA_FREE)
            eng.dma_start(wa[:, 0:14336], d["w23"]).then_inc(ld_w23, 16)
            r_sync(2, eng)
            r_sync(3, eng)
            for n in met:
                eng.wait_ge(met[n], ALL)
            eng.dma_start(d["out"], x[:, :]).then_inc(stored, 16)
            eng.wait_ge(stored, 16)

        def idle(name, eng, n):
            for _ in range(n):
                meet(name, eng)

        @block.gpsimd
        def _(eng):
            for q in started:
                eng.sem_inc(q, 1)
            for k, v in enumerate(EPSV):
                eng.memset(epst[:, k:k + 1], v * DOWN)
            eng.memset(epst[:, 4:5], 0.5 * math.log(DOWN))
            eng.memset(ones16[:, :], 1.0)
            eng.wait_ge(ld_x, 32)
            eng.wait_ge(ld_small, 64)
            meet("pool", eng)
            meet("pool", eng)
            a0_pool(eng)
            idle("pool", eng, PHASES.index("c3") - PHASES.index("a0") - 1)
            c3_pool(eng)
            idle("pool", eng, len(PHASES) - PHASES.index("c3") - 1)

        @block.tensor
        def _(eng):
            meet("pe", eng)
            ln_pe(0, eng)
            a0_pe(eng)
            r_pe(0, eng)
            eng.wait_ge(ld_w0, 16)
            f_pe(0, eng)
            ln_pe(1, eng)
            p1_pe(eng)
            c1_pe(eng)
            o1_pe(eng)
            g1_pe(eng)
            ln_pe(2, eng)
            p2_pe(eng)
            c2_pe(eng)
            o2_pe(eng)
            r_pe(2, eng)
            eng.wait_ge(ld_w23, 16)
            e2_pe(eng)
            ln_pe(3, eng)
            p3_pe(eng)
            c3_pe(eng)
            r_pe(3, eng)
            f_pe(3, eng)

        @block.scalar
        def _(eng):
            meet("act", eng)
            ln_act(0, eng)
            a0_act(eng)
            r_act(0, eng)
            f_act(0, eng)
            ln_act(1, eng)
            meet("act", eng)
            c1_act(eng)
            meet("act", eng)
            g1_act(eng)
            ln_act(2, eng)
            t2_act(eng)
            p2_act(eng)
            c2_act(eng)
            o2_act(eng)
            r_act(2, eng)
            e2_act(eng)
            ln_act(3, eng)
            meet("act", eng)
            c3_act(eng)
            r_act(3, eng)
            f_act(3, eng)

        @block.vector
        def _(eng):
            eng.wait_ge(ld_small, 64)
            eng.tensor_copy(bft[:, :], work[:, 0:(E + 2) * P])
            meet("dve", eng)
            ln_dve(0, eng)
            a0_dve(eng)
            eng.memset(onesrow, 1.0).then_inc(filled, 1)
            eng.wait_ge(filled, 1)
            r_dve(0, eng)
            f_dve(0, eng)
            ln_dve(1, eng)
            p1_dve(eng)
            c1_dve(eng)
            o1_dve(eng)
            g1_dve(eng)
            ln_dve(2, eng)
            t2_dve(eng)
            p2_dve(eng)
            c2_dve(eng)
            o2_dve(eng)
            r_dve(2, eng)
            e2_dve(eng)
            ln_dve(3, eng)
            p3_dve(eng)
            c3_dve(eng)
            r_dve(3, eng)
            f_dve(3, eng)


def tables():
    import numpy as np
    f = np.float64
    t = {}
    t["ones_d"] = np.full((P, P), 1.0 / P)
    t["ident"] = np.eye(P)
    w = np.power(0.001, np.linspace(0.0, 1.0, P))[:, None]
    a = 1e-5
    s = np.arange(SEQ, dtype=f)[None, :]
    t["dec_c"], t["dec_s"] = np.exp(-a * s) * np.cos(w * s), np.exp(-a * s) * np.sin(w * s)
    t["gro_c"], t["gro_s"] = np.exp(a * s) * np.cos(w * s), np.exp(a * s) * np.sin(w * s)
    t["nxt_c"], t["nxt_s"] = np.exp(a * (s + 1)) * np.cos(w * (s + 1)), -np.exp(a * (s + 1)) * np.sin(w * (s + 1))
    keep = np.ones((P, T))
    keep[:, ::SEQ] = 0
    t["keep"] = keep
    th = 1.0 / 10000.0 ** (np.arange(0, HD, 2) / HD)
    p = np.arange(P)
    ang = (p // HD * th[(p % HD) // 2])[:, None] + 0 * s
    sign = np.where(p % 2 == 0, -1.0, 1.0)[:, None]
    t["cosk"], t["sink"] = np.cos(ang), sign * np.sin(ang)
    t["cosq"], t["sinq"] = t["cosk"] / HD ** 0.5, t["sink"] / HD ** 0.5
    t["hmask"] = (p[:, None] // HD == np.arange(H)[None, :])
    t["code"] = np.tile(E - np.arange(E), (P, 1))
    j, q = p[:, None], p[None, :]
    t["lag"] = np.maximum(q - j - 1, 0)
    t["before"] = j < q
    t["iota_q"] = np.tile(p, (P, 1))
    t["rev_j"] = (P - 1 - p)[:, None]
    t["grp"] = (j // HD == q // HD) / HD
    t["sel16"] = (j == q // HD)
    tabs = np.concatenate([np.asarray(t[n], np.float32).reshape(P, -1) for n, _ in TABS], axis=1)
    bft = np.zeros((P, E * P + 2 * P), np.float32)
    for e in range(E):
        for k in range(3):
            bft[k * E + e, e * P:(e + 1) * P] = 1.0
    bft[:, E * P:E * P + P] = np.eye(P)
    bft[:, E * P + P:] = np.where(q > j, NEG, 0.0)
    return tabs, bft


def kernel(**inputs):
    import numpy as _np
    import concourse.bacc as _bacc
    from concourse import mybir as _mybir
    from concourse.bass_utils import run_bass_kernel_spmd as _run

    a = {k: _np.asarray(v) for k, v in inputs.items()}
    cat = _np.concatenate
    swap = _np.arange(P) ^ 1
    wa1, ba1 = a["L1_attn_W_attn"], a["L1_attn_b_attn"]
    wq, wk, wv = wa1[:, 0:P], wa1[:, P:2 * P], wa1[:, 2 * P:]
    bq, bk, bv = ba1[0:P], ba1[P:2 * P], ba1[2 * P:]
    w3 = a["L3_attn_W"]
    m = {"z0": a["L0_attn_Wz"].T, "za0": a["L0_attn_Wza"].T, "y0": a["L0_attn_Wy"].T, "ya0": a["L0_attn_Wya"].T,
         "q1": wq, "qs1": wq[:, swap], "k1": wk, "ks1": wk[:, swap], "v1": wv, "p1": a["L1_attn_W_proj"],
         "r2": a["L2_attn_w_r"].T, "k2": a["L2_attn_w_k"].T, "v2": a["L2_attn_w_v"].T, "g2": a["L2_attn_w_g"].T,
         "o2": a["L2_attn_w_o"].T, "q3": w3[:, 0:P], "k3": w3[:, P:2 * P], "v3": w3[:, 2 * P:]}
    mats = cat([m[n] for n in MATS], axis=1)

    def rows(v, n):
        return _np.tile(v[None, :], (P, 1)) if n is None else v.reshape(n, P).T

    def below(v):
        return cat([v, _np.zeros((P - v.shape[0], v.shape[1]), v.dtype)], axis=0)

    c = {"bz": rows(a["L0_attn_bz"], 1), "bza": rows(a["L0_attn_bza"], 1), "by": rows(a["L0_attn_by"], 1),
         "bya": rows(a["L0_attn_bya"], 1), "norm_w": rows(a["L0_attn_norm_w"], 1),
         "lc_re": rows(a["L0_attn_lc_re"], 1), "lc_im": rows(a["L0_attn_lc_im"], 1),
         "bq": rows(bq, 1), "bqs": rows(bq[swap], 1), "bk": rows(bk, 1), "bks": rows(bk[swap], 1),
         "bv": rows(bv, 1), "bp": rows(a["L1_attn_b_proj"], 1),
         "w1_s": rows(a["L1_ffn_w1_s"], 4), "w2_s": rows(a["L1_ffn_w2_s"], 4), "h1_s": rows(a["L1_ffn_h1_s"], 4),
         "h2_s": rows(a["L1_ffn_h2_s"], 4), "w3_s": rows(a["L1_ffn_w3_s"], 1),
         "maa_k": rows(a["L2_attn_time_maa_k"], 1), "maa_v": rows(a["L2_attn_time_maa_v"], 1),
         "maa_r": rows(a["L2_attn_time_maa_r"], 1), "maa_g": rows(a["L2_attn_time_maa_g"], 1),
         "td_ch": rows(_np.repeat(a["L2_attn_time_decay"], HD), 1), "ln_g": rows(a["L2_attn_ln_g"], 1),
         "ln_b": rows(a["L2_attn_ln_b"], 1), "td_bc": rows(a["L2_attn_time_decay"], None),
         "u_bc": rows(a["L2_attn_time_faaaa"], None), "b1_2": rows(a["L2_ffn_b1"].reshape(-1), E * 4),
         "router0": a["L0_ffn_router_w"].T, "wgred2": a["L2_ffn_wg_red"].T, "wg2": below(a["L2_ffn_wg"].T),
         "gate3": a["L3_ffn_w_gate"]}
    cols = cat([c[n] for n, _ in COLS], axis=1)

    def up(w):
        return w.transpose(1, 0, 2).reshape(P, -1)

    def down(w):
        return w.reshape(-1, P, w.shape[-1]).transpose(1, 0, 2).reshape(P, -1)

    w0 = cat([up(a["L0_ffn_rg"]), up(a["L0_ffn_ru"]), down(a["L0_ffn_rd"]), a["L0_ffn_sg"], a["L0_ffn_su"],
              down(a["L0_ffn_sd"])], axis=1)
    w1 = cat([a["L1_ffn_w1_w"].T, a["L1_ffn_w2_w"].T, down(a["L1_ffn_h1_w"].T), down(a["L1_ffn_h2_w"].T),
              down(a["L1_ffn_w3_w"].T)], axis=1)
    w23 = cat([up(a["L2_ffn_w1"]), down(a["L2_ffn_w2"]), up(a["L3_ffn_w1"]), up(a["L3_ffn_w3"]),
               down(a["L3_ffn_w2"])], axis=1)
    tabs, bft = tables()
    arrays = {"x": a["L0_attn_x"].reshape(N, P).T, "mats": mats, "cols": cols, "tabs": tabs, "bft": bft,
              "b2rows": a["L2_ffn_b2"], "w0": w0, "w1": w1, "w23": w23}
    arrays = {k: _np.ascontiguousarray(v) for k, v in arrays.items()}

    nc = _bacc.Bacc("TRN2", target_bir_lowering=False, num_devices=1)
    d = {k: nc.dram_tensor(f"in_{k}", v.shape, _mybir.dt.from_np(v.dtype), kind="ExternalInput").ap()
         for k, v in arrays.items()}
    d["out"] = nc.dram_tensor("out", (P, N), F32, kind="ExternalOutput").ap()
    build(nc, d)
    r = _run(nc, [{f"in_{k}": v for k, v in arrays.items()}], core_ids=[0])
    return _np.ascontiguousarray(r.results[0]["out"].T).reshape(B, SEQ, P)
```

```python
import math
from contextlib import ExitStack

import concourse.bass as bass
from concourse import mybir

F32 = mybir.dt.float32
BF16 = mybir.dt.bfloat16
I32 = mybir.dt.int32
U32 = mybir.dt.uint32
ALU = mybir.AluOpType
ACT = mybir.ActivationFunctionType
AX_X = mybir.AxisListType.X

P = 128
B, SEQ = 8, 256
N = B * SEQ
T = 512
NT = N // T
NTOK = N // P
SPT = T // SEQ
E = 8
CAP = int(1.25 * N / E)
H, HD = 16, 8
HID0, SH0 = 512, 1024
HID1 = 512
HID2 = 512
HID3 = 256
EPS_LN = 1e-5
EPS_RMS = 1e-6
EPS_GN = 1e-5 * 64
EPS_GATE = 1e-4
EPS_F32 = 1.1920928955078125e-07
NEG = -1e30
DOWN = 2.0 ** -16

MATS = ["z0", "za0", "y0", "ya0", "q1", "qs1", "k1", "ks1", "v1", "p1",
        "r2", "k2", "v2", "g2", "o2", "q3", "k3", "v3"]
COLS = [("bz", 1), ("bza", 1), ("by", 1), ("bya", 1), ("norm_w", 1), ("lc_re", 1), ("lc_im", 1),
        ("bq", 1), ("bqs", 1), ("bk", 1), ("bks", 1), ("bv", 1), ("bp", 1),
        ("w1_s", 4), ("w2_s", 4), ("h1_s", 4), ("h2_s", 4), ("w3_s", 1),
        ("maa_k", 1), ("maa_v", 1), ("maa_r", 1), ("maa_g", 1), ("td_ch", 1), ("ln_g", 1), ("ln_b", 1),
        ("td_bc", H), ("u_bc", H), ("b1_2", E * 4),
        ("router0", E), ("wgred2", P), ("wg2", E), ("gate3", E)]
TABS = [("ones_d", P), ("ident", P), ("dec_c", SEQ), ("dec_s", SEQ), ("gro_c", SEQ), ("gro_s", SEQ),
        ("nxt_c", SEQ), ("nxt_s", SEQ), ("keep", T), ("cosq", 1), ("sinq", 1), ("cosk", 1), ("sink", 1),
        ("hmask", H), ("code", E), ("lag", P), ("before", P), ("iota_q", P), ("rev_j", 1), ("grp", P), ("sel16", P),
        ("keep_t", P), ("first_slot", E), ("tiles", 42), ("places", 42), ("starts", NTOK)]


def offsets(items):
    at, out = 0, {}
    for name, n in items:
        out[name] = (at, n)
        at += n
    return out, at


COL_AT, COL_N = offsets(COLS)
TAB_AT, TAB_N = offsets(TABS)


class Steps:

    def __init__(self, sem, names, turns=1, base=0):
        self.sem, self.names, self.base = sem, {n: k + 1 for k, n in enumerate(names)}, base
        self.per = len(names)
        self.end = base + turns * self.per

    def at(self, name, turn=0):
        return turn * self.per + (self.base + self.names[name])

    def turn_end(self, turn=0):
        return turn * self.per + (self.base + self.per)


def build(nc, d):
    ctx = ExitStack()
    with ctx:
        def sb(name, shape, dt=F32):
            return ctx.enter_context(nc.sbuf_tensor(name, shape, dt))

        def sem(name):
            return ctx.enter_context(nc.semaphore(name))

        x = sb("x", [P, N])
        xn = sb("xn", [P, N])
        mats = sb("mats", [P, len(MATS) * P])
        cols = sb("cols", [P, COL_N])
        tabs = sb("tabs", [P, TAB_N])
        bft = sb("bft", [P, 4 * P], BF16)
        wa = sb("wa", [P, 15360])
        wb = sb("wb", [P, 5632])
        work = sb("work", [P, 19968])
        rt = work[:, 10240:11520].rearrange("p (a b) -> p a b", b=NTOK * E)
        ps = ctx.enter_context(nc.psum_tensor("ps", [P, 8, T], F32))

        def mat(name):
            k = MATS.index(name)
            return mats[:, k * P:(k + 1) * P]

        def col(name, k=0, rows=P):
            return cols[0:rows, COL_AT[name][0] + k:COL_AT[name][0] + k + 1]

        def colv(name, rows=P):
            a, n = COL_AT[name]
            return cols[0:rows, a:a + n]

        def tab(name, rows=P):
            a, n = TAB_AT[name]
            return tabs[0:rows, a:a + n]

        def tabseq(name):
            return tab(name).rearrange("p (o s) -> p o s", o=1).broadcast_to([P, SPT, SEQ])

        def two(ap):
            return ap.rearrange("p (o s) -> p o s", s=SEQ)

        identb, causalb, upto, onesb = [bft[:, k * P:(k + 1) * P] for k in range(4)]
        ident = tab("ident")

        def tile(ap, i):
            return ap[:, bass.ds(i * T, T)]

        def bank(k):
            return ps[:, k, :] if isinstance(k, int) else ps[:, bass.ds(k, 1), :].rearrange("p o t -> p (o t)")

        ld_x, ld_small, ld_w0, ld_w1, ld_w23, stored = [sem(n) for n in
            ("ld_x", "ld_small", "ld_w0", "ld_w1", "ld_w23", "stored")]
        met = {n: sem(f"met_{n}") for n in ("pe", "act", "dve")}
        passed = {n: [0] for n in met}

        def meet(name, eng):
            passed[name][0] += 1
            eng.drain().then_inc(met[name], 1)
            for other in met:
                if other != name:
                    eng.wait_ge(met[other], passed[name][0])

        s = {}
        started = []

        def steps(key, names, turns=1, after=None):
            if after is None:
                s[key] = Steps(sem(key), names, turns, 1)
                started.append(s[key].sem)
            else:
                s[key] = Steps(s[after].sem, names, turns, s[after].end)
            return s[key]

        for L in range(4):
            prev = (lambda k: None if L == 0 else f"ln{L - 1}_{k}")
            steps(f"ln{L}_pe1", ["mean"], NT, f"ln{L-1}_pe2" if L else None)
            steps(f"ln{L}_pe2", ["var"], NT, f"ln{L}_pe1")
            steps(f"ln{L}_dve1", ["centred"], NT, f"ln{L-1}_dve2" if L else None)
            steps(f"ln{L}_dve2", ["normed"], NT, f"ln{L}_dve1")
            steps(f"ln{L}_act1", ["sq"], NT, f"ln{L-1}_act3" if L else None)
            steps(f"ln{L}_act2", ["log"], NT, f"ln{L}_act1")
            steps(f"ln{L}_act3", ["rstd"], NT, f"ln{L}_act2")

        ln_sq = work[:, 0:2048]
        ln_rs = work[:, 2048:4096]

        def ln_pe(L, eng):
            a, b = s[f"ln{L}_pe1"], s[f"ln{L}_pe2"]
            with eng.Fori(0, NT) as i:
                eng.matmul(bank(i), tab("ones_d"), tile(x, i), start=True, stop=True).then_inc(a.sem, 1)
            with eng.Fori(0, NT) as i:
                q = s[f"ln{L}_act1"]
                eng.wait_ge(q.sem, q.at("sq", i))
                eng.matmul(bank(i + 4), tab("ones_d"), tile(ln_sq, i), start=True, stop=True).then_inc(b.sem, 1)
            meet("pe", eng)

        def ln_dve(L, eng):
            a, b = s[f"ln{L}_dve1"], s[f"ln{L}_dve2"]
            with eng.Fori(0, NT) as i:
                q = s[f"ln{L}_pe1"]
                eng.wait_ge(q.sem, q.at("mean", i))
                eng.tensor_tensor(tile(xn, i), tile(x, i), bank(i), ALU.subtract).then_inc(a.sem, 1)
            with eng.Fori(0, NT) as i:
                q = s[f"ln{L}_act3"]
                eng.wait_ge(q.sem, q.at("rstd", i))
                eng.tensor_tensor(tile(xn, i), tile(xn, i), tile(ln_rs, i), ALU.mult).then_inc(b.sem, 1)
            meet("dve", eng)

        def ln_act(L, eng):
            a, b, c = s[f"ln{L}_act1"], s[f"ln{L}_act2"], s[f"ln{L}_act3"]
            eng.preload_act_table(ACT.Ln)
            with eng.Fori(0, NT) as i:
                q = s[f"ln{L}_dve1"]
                eng.wait_ge(q.sem, q.at("centred", i))
                eng.activation(tile(ln_sq, i), tile(xn, i), ACT.Square).then_inc(a.sem, 1)
            with eng.Fori(0, NT) as i:
                q = s[f"ln{L}_pe2"]
                eng.wait_ge(q.sem, q.at("var", i))
                eng.activation(tile(ln_rs, i), bank(i + 4), ACT.Ln, bias=eps_ap(EPS_LN), scale=DOWN).then_inc(b.sem, 1)
            eng.preload_act_table(ACT.Exp)
            with eng.Fori(0, NT) as i:
                eng.wait_ge(b.sem, b.at("log", i))
                eng.activation(tile(ln_rs, i), tile(ln_rs, i), ACT.Exp, bias=epst[:, 4:5], scale=-0.5).then_inc(c.sem, 1)
            meet("act", eng)

        epst = sb("epst", [P, 5])
        EPSV = [EPS_LN, EPS_RMS, EPS_GN, EPS_F32]

        def eps_ap(v):
            k = EPSV.index(v)
            return epst[:, k:k + 1]

        a0 = dict(sz=0, zc=2048, zs=4096, h=6144, rs=8192, hc=10240)
        A0 = {k: work[:, v:v + 2048] for k, v in a0.items()}
        A0["hc"] = work[:, 10240:10496]
        A0["h2"] = work[:, 10496:10496 + 2048]
        steps("a0_pe1", ["z"], NT)
        steps("a0_pe2", ["ms"], NT, "a0_pe1")
        steps("a0_pe3", ["y"], NT, "a0_pe2")
        steps("a0_act1", ["silu_z"], NT)
        steps("a0_act2", ["sq"], NT, "a0_act1")
        steps("a0_act3", ["log"], NT, "a0_act2")
        steps("a0_act4", ["rstd"], NT, "a0_act3")
        steps("a0_act5", ["silu_y"], NT, "a0_act4")
        steps("a0_dve0", ["cross_re", "cross"])
        steps("a0_dve1", ["z", "zc", "zs", "cc", "cs", "hc", "hs", "h", "hx"], NT, "a0_dve0")
        steps("a0_dve2", ["normed"], NT, "a0_dve1")
        steps("a0_dve3", ["y", "x"], NT, "a0_dve2")

        def a0_pe(eng):
            with eng.Fori(0, NT) as i:
                eng.matmul(bank(i), mat("z0"), tile(xn, i), start=True, stop=True)
                eng.matmul(bank(i + 4), mat("za0"), tile(xn, i), start=True, stop=True)\
                   .then_inc(s["a0_pe1"].sem, 1)
            with eng.Fori(0, NT) as i:
                q = s["a0_act2"]
                eng.wait_ge(q.sem, q.at("sq", i))
                eng.matmul(bank(i), tab("ones_d"), tile(A0["sz"], i), start=True, stop=True)\
                   .then_inc(s["a0_pe2"].sem, 1)
            with eng.Fori(0, NT) as i:
                q = s["a0_dve2"]
                eng.wait_ge(q.sem, q.at("normed", i))
                eng.matmul(bank(i), mat("y0"), tile(A0["h2"], i), start=True, stop=True)
                eng.matmul(bank(i + 4), mat("ya0"), tile(xn, i), start=True, stop=True)\
                   .then_inc(s["a0_pe3"].sem, 1)
            meet("pe", eng)

        def a0_act(eng):
            eng.preload_act_table(ACT.Silu)
            with eng.Fori(0, NT) as i:
                q = s["a0_pe1"]
                eng.wait_ge(q.sem, q.at("z", i))
                eng.activation(tile(A0["sz"], i), bank(i + 4), ACT.Silu, bias=col("bza"))\
                   .then_inc(s["a0_act1"].sem, 1)
            eng.preload_act_table(ACT.Ln)
            with eng.Fori(0, NT) as i:
                q = s["a0_dve1"]
                eng.wait_ge(q.sem, q.at("hx", i))
                eng.activation(tile(A0["sz"], i), tile(A0["h"], i), ACT.Square).then_inc(s["a0_act2"].sem, 1)
            with eng.Fori(0, NT) as i:
                q = s["a0_pe2"]
                eng.wait_ge(q.sem, q.at("ms", i))
                eng.activation(tile(A0["rs"], i), bank(i), ACT.Ln, bias=eps_ap(EPS_RMS), scale=DOWN)\
                   .then_inc(s["a0_act3"].sem, 1)
            eng.preload_act_table(ACT.Exp)
            with eng.Fori(0, NT) as i:
                q = s["a0_act3"]
                eng.wait_ge(q.sem, q.at("log", i))
                eng.activation(tile(A0["rs"], i), tile(A0["rs"], i), ACT.Exp, bias=epst[:, 4:5], scale=-0.5)\
                   .then_inc(s["a0_act4"].sem, 1)
            eng.preload_act_table(ACT.Silu)
            with eng.Fori(0, NT) as i:
                q = s["a0_pe3"]
                eng.wait_ge(q.sem, q.at("y", i))
                eng.activation(tile(A0["sz"], i), bank(i + 4), ACT.Silu, bias=col("bya"))\
                   .then_inc(s["a0_act5"].sem, 1)
            meet("act", eng)

        def a0_dve(eng):
            c = s["a0_dve0"]
            eng.tensor_scalar(A0["hc"], tab("nxt_c"), col("lc_re"), None, ALU.mult).then_inc(c.sem, 1)
            eng.wait_ge(c.sem, c.at("cross_re"))
            eng.scalar_tensor_tensor(out=A0["hc"], in0=tab("nxt_s"), scalar=col("lc_im"), in1=A0["hc"],
                                     op0=ALU.mult, op1=ALU.add).then_inc(c.sem, 1)
            eng.wait_ge(c.sem, c.at("cross"))
            hc = A0["hc"].rearrange("p (o s) -> p o s", o=1).broadcast_to([P, SPT, SEQ])
            st = s["a0_dve1"]
            with eng.Fori(0, NT) as i:
                q = s["a0_act1"]
                eng.wait_ge(q.sem, q.at("silu_z", i))
                eng.scalar_tensor_tensor(out=tile(A0["h2"], i), in0=bank(i), scalar=col("bz"),
                                         in1=tile(A0["sz"], i), op0=ALU.add, op1=ALU.mult).then_inc(st.sem, 1)
                eng.wait_ge(st.sem, st.at("z", i))
                eng.tensor_tensor(two(tile(A0["zc"], i)), two(tile(A0["h2"], i)), tabseq("dec_c"), ALU.mult)\
                   .then_inc(st.sem, 1)
                eng.tensor_tensor(two(tile(A0["zs"], i)), two(tile(A0["h2"], i)), tabseq("dec_s"), ALU.mult)\
                   .then_inc(st.sem, 1)
                eng.wait_ge(st.sem, st.at("zc", i))
                eng.tensor_tensor_scan(tile(A0["h"], i), tab("keep"), tile(A0["zc"], i), 0.0,
                                       ALU.mult, ALU.add).then_inc(st.sem, 1)
                eng.wait_ge(st.sem, st.at("cc", i))
                eng.tensor_tensor_scan(tile(A0["rs"], i), tab("keep"), tile(A0["zs"], i), 0.0,
                                       ALU.mult, ALU.add).then_inc(st.sem, 1)
                eng.tensor_tensor(two(tile(A0["zc"], i)), two(tile(A0["h"], i)), tabseq("gro_c"), ALU.mult)\
                   .then_inc(st.sem, 1)
                eng.wait_ge(st.sem, st.at("cs", i))
                eng.tensor_tensor(two(tile(A0["zs"], i)), two(tile(A0["rs"], i)), tabseq("gro_s"), ALU.mult)\
                   .then_inc(st.sem, 1)
                eng.wait_ge(st.sem, st.at("hs", i))
                eng.tensor_tensor(tile(A0["h"], i), tile(A0["zc"], i), tile(A0["zs"], i), ALU.add)\
                   .then_inc(st.sem, 1)
                eng.wait_ge(st.sem, st.at("h", i))
                eng.tensor_tensor(two(tile(A0["h"], i)), two(tile(A0["h"], i)), hc, ALU.add)\
                   .then_inc(st.sem, 1)
            with eng.Fori(0, NT) as i:
                q = s["a0_act4"]
                eng.wait_ge(q.sem, q.at("rstd", i))
                eng.scalar_tensor_tensor(out=tile(A0["h2"], i), in0=tile(A0["h"], i), scalar=col("norm_w"),
                                         in1=tile(A0["rs"], i), op0=ALU.mult, op1=ALU.mult)\
                   .then_inc(s["a0_dve2"].sem, 1)
            st = s["a0_dve3"]
            with eng.Fori(0, NT) as i:
                q = s["a0_act5"]
                eng.wait_ge(q.sem, q.at("silu_y", i))
                eng.scalar_tensor_tensor(out=tile(A0["zc"], i), in0=bank(i), scalar=col("by"),
                                         in1=tile(A0["sz"], i), op0=ALU.add, op1=ALU.mult).then_inc(st.sem, 1)
                eng.wait_ge(st.sem, st.at("y", i))
                eng.tensor_tensor(tile(x, i), tile(x, i), tile(A0["zc"], i), ALU.add).then_inc(st.sem, 1)
            meet("dve", eng)

        R = {k: rt[:, n, :].rearrange("p (t e) -> p t e", e=E) for n, k in enumerate(
            ("lg", "eq", "oh1", "lg2", "oh2", "t1", "t2", "cum", "cumb"))}
        flat = {k: rt[:, n, :] for n, k in enumerate(
            ("lg", "eq", "oh1", "lg2", "oh2", "t1", "t2", "cum", "cumb", "tt"))}
        rk = sb("rk", [P, 12, NTOK])
        Q = {k: rk[:, n, :] for n, k in enumerate(
            ("m1", "cm", "m2", "d", "e2", "w1", "w2", "rms", "p1", "p2", "k1", "k2"))}
        slots = sb("slots", [P, 2, NTOK], U32)
        ex = sb("ex", [P, 4, E])
        etab = sb("etab", [1, 14], I32)
        selb = sb("selb", [P, NTOK * E], BF16)
        wgn = sb("wgn", [16, 3, E])
        ones16 = sb("ones16", [16, 16])
        inc = work[:, 11520:11776].rearrange("p (a b) -> p a b", a=2)
        XT = {0: 16384, 2: 16640, 3: 16384}
        xtok = {L: work[:, a:a + N] for L, a in XT.items()}
        xsq = work[:, 0:N]
        NTILES = {2: 24, 3: 39}
        assert NTILES[2] >= (N + E * (P - 1)) // P and NTILES[3] >= (2 * N + E * (P - 1)) // P
        SLOTS = {0: E * CAP, 2: (NTILES[2] + 3) * P, 3: (NTILES[3] + 3) * P}
        xg = {L: nc.dram_tensor(f"xg{L}", (SLOTS[L], P), F32, kind="Internal").ap() for L in SLOTS}
        yg = {L: nc.dram_tensor(f"yg{L}", (SLOTS[L] + P if L == 0 else NTILES[L] * P, P), F32, kind="Internal").ap()
              for L in SLOTS}
        zeroed = {L: sem(f"zeroed{L}") for L in SLOTS}
        scattered = {L: sem(f"scattered{L}") for L in SLOTS}
        gathered = {L: sem(f"gathered{L}") for L in SLOTS}
        CH = {0: 2, 2: 1, 3: 2}
        GOT = {0: work[:, 14336:18432], 2: wa[:, 0:2048], 3: wa[:, 0:4096]}

        zeros = work[:, 19456:19968]
        ZEROS = {L: -(-SLOTS[L] // T) + (L == 0) for L in SLOTS}
        zeros_made = sem("zeros_made")

        def chunk0(table, c):
            return table[c * T:(c + 1) * T, :].rearrange("(a p) d -> p a d", p=P)

        def chunk0_sb(ap, c):
            return ap[:, c * T:(c + 1) * T].rearrange("p (a d) -> p a d", d=P)

        def bce(ap):
            return ap.rearrange("p (t o) -> p t o", o=1).broadcast_to([P, NTOK, E])

        code = tab("code").rearrange("p (o e) -> p o e", o=1).broadcast_to([P, NTOK, E])

        best1 = ["m1", "eq", "cd", "cm", "oh1"]
        best2 = ["lg2", "m2", "eq2", "cd2", "cm2", "oh2"]
        where = ["tt", "inc", "exc", "cum"]
        spans = ["sp", "nt", "end", "st", "base", "cmp", "cnt", "min", "pl", "pk", "etab"]
        DVE_R = {
            0: [f"x{g}" for g in range(6)] + ["rms", "lg"] + best1 + best2 + ["sel", "d"] + where + ["base"]
               + [f"{w}{k}" for k in (1, 2) for w in "apksfdzi"] + ["den", "w1", "w2", "w1k", "w2k"],
            2: ["nmax", "wginv", "wgu", "wc"] + [f"x{g}" for g in range(6)] + ["lg"] + best1 + ["sel", "lgm"]
               + where + spans + ["s1", "f1", "f1b", "g1", "den", "w1"],
            3: [f"x{g}" for g in range(6)] + ["lg"] + best1 + best2 + ["sel", "d"] + where + spans
               + ["s1", "f1", "f1b", "g1", "s2", "f2", "f2b", "g2", "den", "w1", "w2"]}
        PE_R = {0: [f"t{g}" for g in range(6)] + ["cnt"], 2: ["nrm", "wc"] + [f"t{g}" for g in range(6)] + ["cnt"],
                3: [f"t{g}" for g in range(6)] + ["cnt"]}
        ACT_R = {0: [f"q{g}" for g in range(NTOK)] + ["log", "rms", "e2"], 2: ["sqw", "root", "e2"], 3: ["e2"]}
        for L in (0, 2, 3):
            steps(f"r{L}_dve", DVE_R[L])
            steps(f"r{L}_pe", PE_R[L])
            steps(f"r{L}_act", ACT_R[L])
        TW = P + E
        wc = sb("wc", [P, E])

        def group(g):
            return range(3 * g, min(3 * g + 3, NTOK))

        def r_pe(L, eng):
            st, dv, ac = s[f"r{L}_pe"], s[f"r{L}_dve"], s[f"r{L}_act"]
            rw = {0: colv("router0"), 2: wc[:, :], 3: colv("gate3")}[L]
            if L == 2:
                eng.wait_ge(ac.sem, ac.at("sqw"))
                eng.matmul(ps[0:16, 7, 0:E], ones16[:, :], wgn[:, 0, :], start=True, stop=True).then_inc(st.sem, 1)
                eng.wait_ge(dv.sem, dv.at("wgu"))
                eng.matmul(ps[:, 7, E:2 * E], colv("wgred2", 16), wgn[:, 2, :], start=True, stop=True)\
                   .then_inc(st.sem, 1)
                eng.wait_ge(dv.sem, dv.at("wc"))
            for g in range(6):
                for n, t in enumerate(group(g)):
                    xt = xn[:, t * P:(t + 1) * P]
                    eng.matmul(ps[:, g, n * TW:n * TW + P], xt, ident, start=True, stop=True)
                    mm = eng.matmul(ps[:, g, n * TW + P:(n + 1) * TW], xt, rw, start=True, stop=True)
                mm.then_inc(st.sem, 1)
            eng.wait_ge(dv.sem, dv.at("sel"))
            eng.matmul(ps[:, 6, 0:P], upto, selb[:, :], start=True, stop=True)
            eng.matmul(ps[:, 6, P:2 * P], onesb, selb[:, :], start=True, stop=True).then_inc(st.sem, 1)
            meet("pe", eng)

        def r_act(L, eng):
            st, dv, pe = s[f"r{L}_act"], s[f"r{L}_dve"], s[f"r{L}_pe"]
            if L == 0:
                for t in range(NTOK):
                    eng.wait_ge(dv.sem, dv.at(f"x{t // 3}"))
                    eng.activation(xsq[:, t * P:(t + 1) * P], xtok[0][:, t * P:(t + 1) * P], ACT.Square,
                                   accum_out=Q["rms"][:, t:t + 1]).then_inc(st.sem, 1)
                eng.wait_ge(st.sem, st.at(f"q{NTOK - 1}"))
                eng.activation(Q["d"], Q["rms"], ACT.Ln, bias=eps_ap(EPS_F32), scale=DOWN / P).then_inc(st.sem, 1)
                eng.wait_ge(st.sem, st.at("log"))
                eng.activation(Q["rms"], Q["d"], ACT.Exp, bias=epst[:, 4:5], scale=-0.5).then_inc(st.sem, 1)
            if L == 2:
                eng.activation(wgn[:, 0, :], colv("wg2", 16), ACT.Square).then_inc(st.sem, 1)
                eng.wait_ge(pe.sem, pe.at("nrm"))
                eng.activation(wgn[:, 1, :], ps[0:16, 7, 0:E], ACT.Sqrt).then_inc(st.sem, 1)
                eng.wait_ge(dv.sem, dv.at("lgm"))
                eng.activation(R["t1"], R["eq"], ACT.Exp).then_inc(st.sem, 1)
            else:
                eng.wait_ge(dv.sem, dv.at("d"))
                eng.activation(Q["e2"], Q["d"], ACT.Exp).then_inc(st.sem, 1)
            meet("act", eng)

        def r_dve(L, eng):
            st, pe, ac = s[f"r{L}_dve"], s[f"r{L}_pe"], s[f"r{L}_act"]
            n = [0]

            def did(ins, name):
                ins.then_inc(st.sem, 1)
                n[0] += 1
                assert st.names[name] == n[0], (L, name, n[0])
                eng.wait_ge(st.sem, st.at(name))

            if L == 2:
                eng.wait_ge(ac.sem, ac.at("root"))
                did(eng.tensor_scalar(wgn[:, 1, :], wgn[:, 1, :], EPS_GATE, None, ALU.max), "nmax")
                did(eng.reciprocal(wgn[:, 0, :], wgn[:, 1, :]), "wginv")
                did(eng.tensor_tensor(wgn[:, 2, :], wgn[:, 0, :], colv("wg2", 16), ALU.mult), "wgu")
                eng.wait_ge(pe.sem, pe.at("wc"))
                did(eng.tensor_copy(wc[:, :], ps[:, 7, E:2 * E]), "wc")
            for g in range(6):
                k = len(group(g))
                eng.wait_ge(pe.sem, pe.at(f"t{g}"))
                v = ps[:, g, 0:k * TW].rearrange("p (t c) -> p t c", c=TW)
                eng.tensor_copy(R["lg2"][:, 3 * g:3 * g + k, :], v[:, :, P:TW])
                did(eng.tensor_copy(xtok[L][:, 3 * g * P:(3 * g + k) * P].rearrange("p (t c) -> p t c", c=P),
                                    v[:, :, 0:P]), f"x{g}")
            if L == 0:
                eng.wait_ge(ac.sem, ac.at("rms"))
                did(eng.tensor_copy(R["t1"], bce(Q["rms"])), "rms")
                did(eng.tensor_tensor(R["lg"], R["lg2"], R["t1"], ALU.mult), "lg")
            else:
                did(eng.tensor_copy(R["lg"], R["lg2"]), "lg")

            def best(lg, names, m, oh):
                did(eng.tensor_reduce(Q[m], lg, AX_X, ALU.max), names[0])
                did(eng.tensor_tensor(R["eq"], lg, bce(Q[m]), ALU.is_equal), names[1])
                did(eng.tensor_tensor(R["eq"], R["eq"], code, ALU.mult), names[2])
                did(eng.tensor_reduce(Q["cm"], R["eq"], AX_X, ALU.max), names[3])
                did(eng.tensor_tensor(R[oh], R["eq"], bce(Q["cm"]), ALU.is_equal), names[4])

            best(R["lg"], best1, "m1", "oh1")
            if L == 2:
                did(eng.tensor_copy(selb[:, :], flat["oh1"]), "sel")
                did(eng.tensor_tensor(R["eq"], R["lg"], bce(Q["m1"]), ALU.subtract), "lgm")
            else:
                did(eng.scalar_tensor_tensor(out=R["lg2"], in0=R["oh1"], scalar=NEG, in1=R["lg"],
                                             op0=ALU.mult, op1=ALU.add), "lg2")
                best(R["lg2"], best2[1:], "m2", "oh2")
                did(eng.tensor_tensor(selb[:, :], flat["oh1"], flat["oh2"], ALU.add), "sel")
                did(eng.tensor_tensor(Q["d"], Q["m2"], Q["m1"], ALU.subtract), "d")
            eng.wait_ge(pe.sem, pe.at("cnt"))
            e_t = lambda ap: ap.rearrange("p (e t) -> p e t", t=NTOK)
            did(eng.tensor_copy(e_t(flat["tt"]), ps[:, 6, P:2 * P].rearrange("p (t e) -> p e t", e=E)), "tt")
            did(eng.tensor_tensor_scan(inc[:, 0, :], tab("keep_t"), flat["tt"], 0.0, ALU.mult, ALU.add), "inc")
            did(eng.tensor_tensor(inc[:, 1, :], inc[:, 0, :], flat["tt"], ALU.subtract), "exc")
            did(eng.tensor_tensor(R["cum"], ps[:, 6, 0:P].rearrange("p (t e) -> p t e", e=E),
                                  inc[:, 1, :].rearrange("p (e t) -> p t e", t=NTOK), ALU.add), "cum")

            def of_choice(k, what, name, out):
                oh = R[f"oh{k}"]
                did(eng.tensor_tensor(R["t2"], oh, R[what], ALU.mult), name[0])
                did(eng.tensor_reduce(out, R["t2"], AX_X, ALU.add), name[1])

            if L == 0:
                fs = tab("first_slot").rearrange("p (o e) -> p o e", o=1).broadcast_to([P, NTOK, E])
                did(eng.tensor_tensor(R["cumb"], R["cum"], fs, ALU.add), "base")
                for k in (1, 2):
                    of_choice(k, "cum", (f"a{k}", f"p{k}"), Q[f"p{k}"])
                    did(eng.tensor_scalar(Q[f"k{k}"], Q[f"p{k}"], float(CAP), None, ALU.is_le), f"k{k}")
                    of_choice(k, "cumb", (f"s{k}", f"f{k}"), Q[f"p{k}"])
                    did(eng.tensor_scalar(Q["cm"], Q[f"k{k}"], -float(E * CAP), float(E * CAP), ALU.mult, ALU.add),
                        f"d{k}")
                    did(eng.tensor_tensor(Q[f"p{k}"], Q[f"p{k}"], Q[f"k{k}"], ALU.mult), f"z{k}")
                    did(eng.tensor_tensor(slots[:, k - 1, :], Q[f"p{k}"], Q["cm"], ALU.add), f"i{k}")
            else:
                c = {k: ex[:, n, :] for n, k in enumerate(("nt", "end", "st", "base"))}
                last = e_t(inc[:, 0, :])[:, :, NTOK - 1:NTOK].rearrange("p e o -> p (e o)")
                starts = tab("starts").rearrange("p (o t) -> p o t", o=1).broadcast_to([P, E, NTOK])
                did(eng.tensor_tensor(e_t(flat["cumb"]), starts,
                                      last.rearrange("p (e o) -> p e o", o=1).broadcast_to([P, E, NTOK]),
                                      ALU.is_lt), "sp")
                did(eng.tensor_reduce(c["nt"], e_t(flat["cumb"]), AX_X, ALU.add), "nt")
                did(eng.tensor_tensor_scan(c["end"], one8[:, :], c["nt"], 0.0,
                                           ALU.mult, ALU.add), "end")
                did(eng.tensor_tensor(c["st"], c["end"], c["nt"], ALU.subtract), "st")
                did(eng.tensor_scalar(c["base"], c["st"], float(P), -1.0, ALU.mult, ALU.add), "base")
                ctmp = xn1[0:1, 0:42 * E].rearrange("p (t e) -> p t e", e=E)
                did(eng.tensor_tensor(ctmp, c["end"][0:1, :].rearrange("p (o e) -> p o e", o=1).broadcast_to([1, 42, E]),
                                      tab("tiles", 1).rearrange("p (t o) -> p t o", o=1).broadcast_to([1, 42, E]),
                                      ALU.is_le), "cmp")
                exps = xn1[0:1, 42 * E:42 * E + 42]
                did(eng.tensor_reduce(exps, ctmp, AX_X, ALU.add), "cnt")
                did(eng.tensor_scalar(exps, exps, float(E - 1), None, ALU.min), "min")
                did(eng.tensor_tensor(exps, exps, tab("places", 1), ALU.mult), "pl")
                did(eng.tensor_reduce(xn1[0:1, 0:14], exps.rearrange("p (t k) -> p t k", k=3), AX_X, ALU.add), "pk")
                did(eng.tensor_copy(etab[:, :], xn1[0:1, 0:14]), "etab")
                bb = c["base"].rearrange("p (o e) -> p o e", o=1).broadcast_to([P, NTOK, E])
                for k in range(1, CH[L] + 1):
                    did(eng.tensor_tensor(R["cumb"], R["cum"], bb, ALU.add), f"s{k}")
                    did(eng.tensor_tensor(R["t2"], R[f"oh{k}"], R["cumb"], ALU.mult), f"f{k}")
                    did(eng.tensor_reduce(Q[f"p{k}"], R["t2"], AX_X, ALU.add), f"f{k}b")
                    did(eng.tensor_copy(slots[:, k - 1, :], Q[f"p{k}"]), f"g{k}")
            eng.wait_ge(ac.sem, ac.at("e2"))
            if L == 2:
                did(eng.tensor_reduce(Q["d"], R["t1"], AX_X, ALU.add), "den")
                did(eng.reciprocal(Q["w1"], Q["d"]), "w1")
            else:
                did(eng.tensor_scalar(Q["w2"], Q["e2"], 1.0, None, ALU.add), "den")
                did(eng.reciprocal(Q["w1"], Q["w2"]), "w1")
                did(eng.tensor_tensor(Q["w2"], Q["e2"], Q["w1"], ALU.mult), "w2")
                if L == 0:
                    did(eng.tensor_tensor(Q["w1"], Q["w1"], Q["k1"], ALU.mult), "w1k")
                    did(eng.tensor_tensor(Q["w2"], Q["w2"], Q["k2"], ALU.mult), "w2k")
            assert n[0] == st.per, (L, n[0], st.per)
            meet("dve", eng)

        one8 = sb("one8", [P, E])
        xn1 = sb("xn1", [1, 42 * (E + 1)])

        def scatter(L, eng):
            dv = s[f"r{L}_dve"]
            eng.wait_ge(dv.sem, dv.end)
            eng.wait_ge(zeroed[L], 16 * ZEROS[L])
            for k in range(CH[L]):
                for t in range(NTOK):
                    eng.indirect_dma_start(xg[L], bass.IndirectOffsetOnAxis(ap=slots[:, k, t:t + 1], axis=0),
                                           xtok[L][:, t * P:(t + 1) * P], None, bounds_check=SLOTS[L] - 1,
                                           oob_is_err=False).then_inc(scattered[L], 16)

        def gather(L, eng):
            rows = yg[L].shape[0]
            if L == 0:
                eng.wait_ge(yg0_stored, 16 * NCH0)
            else:
                for k in range(3):
                    eng.wait_ge(s[f"x{L}_stored{k}"].sem, 16 * TURNS[L] + 1)
            for k in range(CH[L]):
                for t in range(NTOK):
                    eng.indirect_dma_start(GOT[L][:, k * N + t * P:k * N + (t + 1) * P], None, yg[L],
                                           bass.IndirectOffsetOnAxis(ap=slots[:, k, t:t + 1], axis=0),
                                           bounds_check=rows - 1, oob_is_err=False).then_inc(gathered[L], 16)

        for L in (0, 2, 3):
            steps(f"b{L}_act", [f"a{t}" for t in range(NTOK)])
            steps(f"b{L}_dve", ([f"m{t}" for t in range(NTOK)] if CH[L] == 2 else []) + [f"x{i}" for i in range(NT)])
            steps(f"b{L}_pe", [f"t{i}" for i in range(NT)])

        def b_act(L, eng):
            st = s[f"b{L}_act"]
            eng.wait_ge(gathered[L], 16 * NTOK * CH[L])
            for t in range(NTOK):
                g = GOT[L][:, t * P:(t + 1) * P]
                eng.activation(g, g, ACT.Copy, scale=Q["w1"][:, t:t + 1]).then_inc(st.sem, 1)
            meet("act", eng)

        def b_dve(L, eng):
            st, ac, pe = s[f"b{L}_dve"], s[f"b{L}_act"], s[f"b{L}_pe"]
            if CH[L] == 2:
                eng.wait_ge(gathered[L], 16 * NTOK * CH[L])
                for t in range(NTOK):
                    g, h2_ = GOT[L][:, t * P:(t + 1) * P], GOT[L][:, N + t * P:N + (t + 1) * P]
                    eng.wait_ge(ac.sem, ac.at(f"a{t}"))
                    eng.scalar_tensor_tensor(out=g, in0=h2_, scalar=Q["w2"][:, t:t + 1], in1=g,
                                             op0=ALU.mult, op1=ALU.add).then_inc(st.sem, 1)
            for i in range(NT):
                eng.wait_ge(pe.sem, pe.at(f"t{i}"))
                xt = x[:, i * T:(i + 1) * T]
                eng.tensor_tensor(xt, xt, bank(i), ALU.add).then_inc(st.sem, 1)
            meet("dve", eng)

        def b_pe(L, eng):
            st, ac, dv = s[f"b{L}_pe"], s[f"b{L}_act"], s[f"b{L}_dve"]
            for t in range(NTOK):
                if CH[L] == 2:
                    eng.wait_ge(dv.sem, dv.at(f"m{t}"))
                else:
                    eng.wait_ge(ac.sem, ac.at(f"a{t}"))
                mm = eng.transpose(ps[:, t // 4, (t % 4) * P:(t % 4 + 1) * P], GOT[L][:, t * P:(t + 1) * P], ident)
                if t % 4 == 3:
                    mm.then_inc(st.sem, 1)
            meet("pe", eng)


        SW0 = 3 * E * HID0
        NS = SH0 // P
        sf_w = [[wa[:, SW0 + m * SH0 + j * P:SW0 + m * SH0 + (j + 1) * P] for m in range(3)] for j in range(NS)]
        names = []
        for k in range(NS + 2):
            names += ([f"g{k}", f"u{k}"] if k < NS else []) + ([f"d{k - 2}"] if k >= 2 else [])
        steps("sf0_pe", names, NT)
        steps("sf0_act", [f"s{k}" for k in range(NS)], NT)
        steps("sf0_dve", [f"h{k}" for k in range(NS)] + ["x"], NT)
        sf_sg = [work[:, k * T:(k + 1) * T] for k in range(2)]
        sf_h = [work[:, (2 + k) * T:(3 + k) * T] for k in range(3)]

        def sf0_pe(eng):
            st, dv = s["sf0_pe"], s["sf0_dve"]
            with eng.Fori(0, NT) as i:
                for k in range(NS + 2):
                    if k < NS:
                        if k >= 2:
                            eng.wait_ge(dv.sem, dv.at(f"h{k - 2}", i))
                        eng.matmul(bank(k % 2), sf_w[k][0], tile(xn, i), start=True, stop=True).then_inc(st.sem, 1)
                        eng.matmul(bank(2 + k % 2), sf_w[k][1], tile(xn, i), start=True, stop=True)\
                           .then_inc(st.sem, 1)
                    if k >= 2:
                        j = k - 2
                        if j == 0:
                            eng.wait_ge(dv.sem, i * dv.per + dv.base)
                        eng.wait_ge(dv.sem, dv.at(f"h{j}", i))
                        eng.matmul(bank(6), sf_w[j][2], sf_h[j % 3], start=(j == 0), stop=(j == NS - 1))\
                           .then_inc(st.sem, 1)
            meet("pe", eng)

        def sf0_act(eng):
            st, pe, dv = s["sf0_act"], s["sf0_pe"], s["sf0_dve"]
            eng.preload_act_table(ACT.Silu)
            with eng.Fori(0, NT) as i:
                for k in range(NS):
                    eng.wait_ge(pe.sem, pe.at(f"g{k}", i))
                    if k >= 2:
                        eng.wait_ge(dv.sem, dv.at(f"h{k - 2}", i))
                    eng.activation(sf_sg[k % 2], bank(k % 2), ACT.Silu).then_inc(st.sem, 1)
            meet("act", eng)

        def sf0_dve(eng):
            st, pe, ac = s["sf0_dve"], s["sf0_pe"], s["sf0_act"]
            with eng.Fori(0, NT) as i:
                for k in range(NS):
                    eng.wait_ge(pe.sem, pe.at(f"u{k}", i))
                    eng.wait_ge(ac.sem, ac.at(f"s{k}", i))
                    if k >= 3:
                        eng.wait_ge(pe.sem, pe.at(f"d{k - 3}", i))
                    eng.tensor_tensor(sf_h[k % 3], sf_sg[k % 2], bank(2 + k % 2), ALU.mult).then_inc(st.sem, 1)
                eng.wait_ge(pe.sem, pe.at(f"d{NS - 1}", i))
                eng.tensor_tensor(tile(x, i), tile(x, i), bank(6), ALU.add).then_inc(st.sem, 1)
            meet("dve", eng)

        NCH0 = E * CAP // T
        xin0 = work[:, 12544:12544 + E * CAP]
        xgT = work[:, 5120:5120 + E * CAP]
        ef_sg = [work[:, 7680 + k * CAP:7680 + (k + 1) * CAP] for k in range(2)]
        ef_h = [work[:, 7680 + (2 + k) * CAP:7680 + (3 + k) * CAP] for k in range(3)]
        xg0_loaded, yg0_stored = sem("xg0_loaded"), sem("yg0_stored")
        NB0 = HID0 // P
        NK0 = E * NB0
        outs0 = {}
        for c in range(NCH0):
            last = ((c + 1) * T - 1) // CAP
            outs0.setdefault(NB0 * last + NB0 + 2, []).append(c)
        pe_names = [f"in{c}" for c in range(NCH0)]
        for k in range(NK0 + 3):
            pe_names += ([f"g{k}", f"u{k}"] if k < NK0 else []) + ([f"d{k - 2}"] if 2 <= k < NK0 + 2 else [])
            pe_names += [f"out{c}" for c in outs0.get(k, [])]
        act_names = [f"in{c}" for c in range(NCH0)]
        dve_names = []
        for k in range(NK0 + 3):
            act_names += ([f"s{k}"] if k < NK0 else []) + [f"out{c}" for c in outs0.get(k, [])]
            dve_names += ([f"h{k}"] if k < NK0 else [])
            dve_names += [f"y{(k - 2) // NB0}"] if 2 <= k < NK0 + 2 and (k - 2) % NB0 == NB0 - 1 else []
        steps("ef0_pe", pe_names)
        steps("ef0_act", act_names)
        steps("ef0_dve", dve_names)

        def ef0_sync(eng):
            ac = s["ef0_act"]
            eng.wait_ge(scattered[0], 16 * NTOK * CH[0])
            for c in range(NCH0):
                eng.dma_start(chunk0_sb(xin0, c), chunk0(xg[0], c)).then_inc(xg0_loaded, 16)
            for c in range(NCH0):
                eng.wait_ge(ac.sem, ac.at(f"out{c}"))
                eng.dma_start(chunk0(yg[0], c), chunk0_sb(xin0, c)).then_inc(yg0_stored, 16)

        def ef0_pe(eng):
            st, ac, dv = s["ef0_pe"], s["ef0_act"], s["ef0_dve"]

            def turn_tiles(c, src, name):
                for n in range(4):
                    a = c * T + n * P
                    mm = eng.transpose(ps[:, 6 + c % 2, n * P:(n + 1) * P], src[:, a:a + P], ident)
                mm.then_inc(st.sem, 1)

            eng.wait_ge(xg0_loaded, 16 * NCH0)
            for c in range(NCH0):
                if c >= 2:
                    eng.wait_ge(ac.sem, ac.at(f"in{c - 2}"))
                turn_tiles(c, xin0, f"in{c}")
            for k in range(NK0 + 3):
                if k < NK0:
                    e, j = divmod(k, NB0)
                    slot = xgT[:, e * CAP:(e + 1) * CAP]
                    if j == 0:
                        eng.wait_ge(ac.sem, ac.at(f"in{((e + 1) * CAP - 1) // T}"))
                    if k >= 2:
                        eng.wait_ge(dv.sem, dv.at(f"h{k - 2}"))
                    eng.matmul(ps[:, k % 2, 0:CAP], wa[:, k * P:(k + 1) * P], slot, start=True, stop=True)\
                       .then_inc(st.sem, 1)
                    eng.matmul(ps[:, 2 + k % 2, 0:CAP], wa[:, E * HID0 + k * P:E * HID0 + (k + 1) * P], slot,
                               start=True, stop=True).then_inc(st.sem, 1)
                if 2 <= k < NK0 + 2:
                    e, j = divmod(k - 2, NB0)
                    if j == 0 and e >= 2:
                        eng.wait_ge(dv.sem, dv.at(f"y{e - 2}"))
                    eng.wait_ge(dv.sem, dv.at(f"h{k - 2}"))
                    a = 2 * E * HID0 + (k - 2) * P
                    eng.matmul(ps[:, 4 + e % 2, 0:CAP], wa[:, a:a + P], ef_h[(k - 2) % 3],
                               start=(j == 0), stop=(j == NB0 - 1)).then_inc(st.sem, 1)
                for c in outs0.get(k, []):
                    eng.wait_ge(dv.sem, dv.at(f"y{((c + 1) * T - 1) // CAP}"))
                    eng.wait_ge(ac.sem, ac.at(f"out{c - 2}" if c >= 2 else f"in{NCH0 - 1}"))
                    turn_tiles(c, xgT, f"out{c}")
            meet("pe", eng)

        def ef0_act(eng):
            st, pe, dv = s["ef0_act"], s["ef0_pe"], s["ef0_dve"]
            for c in range(NCH0):
                eng.wait_ge(pe.sem, pe.at(f"in{c}"))
                eng.activation(xgT[:, c * T:(c + 1) * T], bank(6 + c % 2), ACT.Copy).then_inc(st.sem, 1)
            for k in range(NK0 + 3):
                if k < NK0:
                    eng.wait_ge(pe.sem, pe.at(f"g{k}"))
                    if k >= 2:
                        eng.wait_ge(dv.sem, dv.at(f"h{k - 2}"))
                    eng.activation(ef_sg[k % 2], ps[:, k % 2, 0:CAP], ACT.Silu).then_inc(st.sem, 1)
                for c in outs0.get(k, []):
                    eng.wait_ge(pe.sem, pe.at(f"out{c}"))
                    eng.activation(xin0[:, c * T:(c + 1) * T], bank(6 + c % 2), ACT.Copy).then_inc(st.sem, 1)
            meet("act", eng)

        def ef0_dve(eng):
            st, pe, ac = s["ef0_dve"], s["ef0_pe"], s["ef0_act"]
            for k in range(NK0 + 3):
                if k < NK0:
                    eng.wait_ge(pe.sem, pe.at(f"u{k}"))
                    eng.wait_ge(ac.sem, ac.at(f"s{k}"))
                    if k >= 3:
                        eng.wait_ge(pe.sem, pe.at(f"d{k - 3}"))
                    eng.tensor_tensor(ef_h[k % 3], ef_sg[k % 2], ps[:, 2 + k % 2, 0:CAP], ALU.mult)\
                       .then_inc(st.sem, 1)
                if 2 <= k < NK0 + 2 and (k - 2) % NB0 == NB0 - 1:
                    e = (k - 2) // NB0
                    eng.wait_ge(pe.sem, pe.at(f"d{k - 2}"))
                    eng.tensor_copy(xgT[:, e * CAP:(e + 1) * CAP], ps[:, 4 + e % 2, 0:CAP]).then_inc(st.sem, 1)
            meet("dve", eng)

        TURNS = {2: NTILES[2] // 3, 3: NTILES[3] // 3}
        EW = {2: 2 * HID2 + P, 3: 3 * HID3}
        EBASE = {2: 0, 3: E * (2 * HID2 + P)}
        NBX = {2: HID2 // P, 3: HID3 // P}
        slot_mem = [work[:, 6144 + k * 1408:6144 + (k + 1) * 1408] for k in range(3)]
        x_w = [m[:, 0:512] for m in slot_mem]
        x_h = [m[:, 512:1024] for m in slot_mem]
        x_T = [m[:, 1024:1152] for m in slot_mem]
        x_sg = [m[:, 1024 + 128:1408] for m in slot_mem]
        x_in = [work[:, 18688 + k * P:18688 + (k + 1) * P] for k in range(3)]
        x_out = [work[:, 19072 + k * P:19072 + (k + 1) * P] for k in range(3)]
        x_b1 = [work[:, 11400 + k * 4:11404 + k * 4] for k in range(3)]
        T_BANK, Y_BANK = [0, 6, 7], [4, 5, 4]
        XO = ["g0", "g1", "y0", "g2", "y1", "y2"]
        for L in (2, 3):
            steps(f"x{L}_pe", XO, TURNS[L])
            steps(f"x{L}_turned", ["t0", "t1", "t2"], TURNS[L] + 1)
            steps(f"x{L}_act", ["a0", "a1", "a2"], TURNS[L])
            steps(f"x{L}_ready", ["r0", "r1", "r2"], TURNS[L] + 1)
            steps(f"x{L}_dve", (["h0", "h1"] if L == 3 else []) + ["y0"] + (["h2"] if L == 3 else []) + ["y1", "y2"],
                  TURNS[L])
            for k in range(3):
                steps(f"x{L}_loaded{k}", ["l"] * 1)
                steps(f"x{L}_stored{k}", ["l"] * 1)

        def experts_of(eng, j):
            v = eng.value_load(etab[0:1, bass.ds(j, 1) if not isinstance(j, int) else slice(j, j + 1)],
                               min_val=0, max_val=E ** 3 - 1)
            return [v % E, v // E % E, v // (E * E)]

        def weights_at(L, e):
            return e * EW[L] + EBASE[L]

        def x_sync(L, eng):
            pe, tn, dv = s[f"x{L}_pe"], s[f"x{L}_turned"], s[f"x{L}_dve"]
            ld = [s[f"x{L}_loaded{k}"].sem for k in range(3)]
            sd = [s[f"x{L}_stored{k}"].sem for k in range(3)]

            def load(t, k):
                eng.dma_start(x_in[k], xg[L][bass.ds(t * P, P), :]).then_inc(ld[k], 16)

            def store(t, k):
                eng.dma_start(yg[L][bass.ds(t * P, P), :], x_out[k]).then_inc(sd[k], 16)

            eng.wait_ge(scattered[L], 16 * NTOK * CH[L])
            for k in range(3):
                load(k, k)
            for k in range(3):
                eng.wait_ge(tn.sem, tn.at(f"t{k}"))
                load(3 + k, k)
            with eng.Fori(0, TURNS[L] - 1) as i:
                for k in range(3):
                    eng.wait_ge(dv.sem, dv.at(f"y{k}", i))
                    store(i * 3 + k, k)
                    eng.wait_ge(tn.sem, tn.at(f"t{k}", i + 1))
                    load(i * 3 + 6 + k, k)
            for k in range(3):
                eng.wait_ge(dv.sem, dv.at(f"y{k}", TURNS[L] - 1))
                store((TURNS[L] - 1) * 3 + k, k)

        def x_pe(L, eng):
            st, tn, ac, rd, dv = [s[f"x{L}_{n}"] for n in ("pe", "turned", "act", "ready", "dve")]
            ld = [s[f"x{L}_loaded{k}"].sem for k in range(3)]
            nb = NBX[L]

            def turn(k, j):
                eng.wait_ge(ld[k], j * 16 + 17)
                eng.transpose(ps[:, T_BANK[k], 0:P], x_in[k], ident).then_inc(tn.sem, 1)

            def first(k, i):
                eng.wait_ge(rd.sem, rd.at(f"r{k}", i))
                for n in range(4):
                    mm = eng.matmul(ps[:, 1 + k, n * P:(n + 1) * P], x_w[k][:, n * P:(n + 1) * P], x_T[k],
                                    start=True, stop=True)
                mm.then_inc(st.sem, 1)

            def second(k, i, at):
                q, nm = (ac, f"a{k}") if L == 2 else (dv, f"h{k}")
                eng.wait_ge(ld_w23, 16)
                eng.wait_ge(q.sem, q.at(nm, i))
                eng.wait_ge(dv.sem, dv.at("y0", i) if k == 2 else i * dv.per + dv.base)
                for n in range(nb):
                    mm = eng.matmul(ps[:, Y_BANK[k], 0:P], x_h[k][:, n * P:(n + 1) * P],
                                    wa[:, bass.ds(at + 512 + n * P, P)], start=(n == 0), stop=(n == nb - 1))
                mm.then_inc(st.sem, 1)

            for k in range(3):
                turn(k, 0)
            with eng.Fori(0, TURNS[L]) as i:
                at = [weights_at(L, e) for e in experts_of(eng, i)]
                first(0, i)
                first(1, i)
                second(0, i, at[0])
                turn(0, i + 1)
                first(2, i)
                second(1, i, at[1])
                turn(1, i + 1)
                turn(2, i + 1)
                second(2, i, at[2])
            meet("pe", eng)

        def x_act(L, eng):
            st, pe = s[f"x{L}_act"], s[f"x{L}_pe"]
            eng.preload_act_table(ACT.Gelu if L == 2 else ACT.Silu)
            with eng.Fori(0, TURNS[L]) as i:
                for k in range(3):
                    eng.wait_ge(pe.sem, pe.at(f"g{k}", i))
                    if L == 2:
                        for n in range(4):
                            a = eng.activation(x_h[k][:, n * P:(n + 1) * P], ps[:, 1 + k, n * P:(n + 1) * P],
                                               ACT.Gelu, bias=x_b1[k][:, n:n + 1])
                    else:
                        a = eng.activation(x_sg[k], ps[:, 1 + k, 0:2 * P], ACT.Silu)
                    a.then_inc(st.sem, 1)
            meet("act", eng)

        def x_dve(L, eng):
            st, pe, ac, tn, rd = [s[f"x{L}_{n}"] for n in ("dve", "pe", "act", "turned", "ready")]
            sd = [s[f"x{L}_stored{k}"].sem for k in range(3)]

            def fetch(k, j, e, last=None):
                eng.wait_ge(tn.sem, tn.at(f"t{k}", j))
                eng.tensor_copy(x_w[k], wa[:, bass.ds(weights_at(L, e), 512)])
                if L == 2:
                    b = COL_AT["b1_2"][0]
                    if last is not None:
                        eng.wait_ge(ac.sem, ac.at(f"a{k}", last))
                    eng.tensor_copy(x_b1[k], cols[:, bass.ds(e * 4 + b, 4)])
                eng.tensor_copy(x_T[k], ps[:, T_BANK[k], 0:P]).then_inc(rd.sem, 1)

            def hidden(k, i):
                eng.wait_ge(ac.sem, ac.at(f"a{k}", i))
                eng.tensor_tensor(x_h[k][:, 0:2 * P], x_sg[k], ps[:, 1 + k, 2 * P:4 * P], ALU.mult)\
                   .then_inc(st.sem, 1)

            def result(k, i, e):
                eng.wait_ge(sd[k], i * 16 + 1)
                eng.wait_ge(pe.sem, pe.at(f"y{k}", i))
                if L == 2:
                    eng.tensor_tensor(x_out[k], ps[:, Y_BANK[k], 0:P], wa[:, bass.ds(weights_at(L, e) + 2 * HID2, P)], ALU.add)\
                       .then_inc(st.sem, 1)
                else:
                    eng.tensor_copy(x_out[k], ps[:, Y_BANK[k], 0:P]).then_inc(st.sem, 1)

            eng.wait_ge(ld_w23, 16)
            for k, e in enumerate(experts_of(eng, 0)):
                fetch(k, 0, e)
            with eng.Fori(0, TURNS[L]) as i:
                here = experts_of(eng, i) if L == 2 else [None] * 3
                ahead = experts_of(eng, i + 1)
                if L == 3:
                    hidden(0, i)
                    hidden(1, i)
                result(0, i, here[0])
                fetch(0, i + 1, ahead[0], i)
                if L == 3:
                    hidden(2, i)
                result(1, i, here[1])
                fetch(1, i + 1, ahead[1], i)
                fetch(2, i + 1, ahead[2], i)
                result(2, i, here[2])
            meet("dve", eng)

        VP = 16 * 136
        q1, k1, v1 = [work[:, k * N:(k + 1) * N] for k in range(3)]
        y1 = q1
        kpad = [wa[:, k * 4096:(k + 1) * 4096] for k in range(2)]
        vpad = [[work[:, 6144 + (2 * k + c) * VP:6144 + (2 * k + c + 1) * VP] for c in range(2)] for k in range(2)]
        o = 6144 + 4 * VP
        qst = [work[:, o + k * SEQ:o + (k + 1) * SEQ] for k in range(2)]
        o += 2 * SEQ
        p0 = [work[:, o + k * 512:o + (k + 1) * 512] for k in range(2)]
        o += 1024
        p1 = [wa[:, 8192 + k * 1024:8192 + (k + 1) * 1024] for k in range(2)]
        pT = [wa[:, 10240 + k * 384:10240 + (k + 1) * 384] for k in range(3)]
        nmx = wa[:, 11392:11392 + 64]
        den1 = wa[:, 11456:11456 + 64]
        den_all = wa[:, 11520:11520 + 256]
        rden_all = wa[:, 11776:11776 + 256]
        rT = wa[0:16, 12032:12032 + 2048]
        tmpa = [wa[:, k * 2048:(k + 1) * 2048] for k in range(4)]
        assert o <= 19968

        steps("p1_pe", ["q", "k"], NT)
        steps("p1_pe_v", ["v"], NTOK // 4, "p1_pe")
        steps("p1_dve0", ["z0", "z1", "z2", "z3"])
        steps("p1_dve", ["qa", "qb", "q", "ka", "kb", "k"], NT, "p1_dve0")
        steps("p1_dve_v", ["v"], NT, "p1_dve")

        def p1_pe(eng):
            st = s["p1_pe"]
            with eng.Fori(0, NT) as i:
                dv = s["p1_dve"]
                eng.wait_ge(dv.sem, i * dv.per + dv.base)
                eng.matmul(bank(0), mat("q1"), tile(xn, i), start=True, stop=True)
                eng.matmul(bank(1), mat("qs1"), tile(xn, i), start=True, stop=True).then_inc(st.sem, 1)
                eng.matmul(bank(2), mat("k1"), tile(xn, i), start=True, stop=True)
                eng.matmul(bank(3), mat("ks1"), tile(xn, i), start=True, stop=True).then_inc(st.sem, 1)
            for t in range(NTOK):
                mm = eng.matmul(ps[:, 4 + t // 4, (t % 4) * P:(t % 4 + 1) * P], xn[:, t * P:(t + 1) * P], mat("v1"),
                                start=True, stop=True)
                if t % 4 == 3:
                    mm.then_inc(s["p1_pe_v"].sem, 1)
            meet("pe", eng)

        def p1_dve(eng):
            z = s["p1_dve0"]
            for k in range(2):
                for c in range(2):
                    eng.memset(vpad[k][c], 0.0).then_inc(z.sem, 1)
            st = s["p1_dve"]
            pe = s["p1_pe"]
            with eng.Fori(0, NT) as i:
                for dst, b0, bb, cs, sn, nm in ((q1, 0, ("bq", "bqs"), "cosq", "sinq", "q"),
                                                (k1, 2, ("bk", "bks"), "cosk", "sink", "k")):
                    eng.wait_ge(pe.sem, pe.at(nm, i))
                    eng.scalar_tensor_tensor(out=two(tile(tmpa[0], i)), in0=two(bank(b0)), scalar=col(bb[0]),
                                             in1=tabseq(cs), op0=ALU.add, op1=ALU.mult).then_inc(st.sem, 1)
                    eng.scalar_tensor_tensor(out=two(tile(tmpa[1], i)), in0=two(bank(b0 + 1)), scalar=col(bb[1]),
                                             in1=tabseq(sn), op0=ALU.add, op1=ALU.mult).then_inc(st.sem, 1)
                    eng.wait_ge(st.sem, st.at(nm + "b", i))
                    eng.tensor_tensor(tile(dst, i), tile(tmpa[0], i), tile(tmpa[1], i), ALU.add)\
                       .then_inc(st.sem, 1)
                    eng.wait_ge(st.sem, st.at(nm, i))
            sv, pv = s["p1_dve_v"], s["p1_pe_v"]
            for i in range(NT):
                eng.wait_ge(pv.sem, pv.at("v", i))
                eng.tensor_copy(v1[:, i * T:(i + 1) * T], bank(4 + i)).then_inc(sv.sem, 1)
            meet("dve", eng)

        def dve_names(a):
            out = [f"{a}qs"] + [f"{a}kp{h}" for h in range(H)] + [f"{a}v0", f"{a}v1"]
            out += [f"{a}mx{n}" for n in range(3)]
            for u in range(4):
                for h in range(4 * u, 4 * u + 4):
                    out += [f"{a}c{h}"]
                    if u < 3 and h % 4 != 1:
                        out += [f"{a}mx{3 * (u + 1) + (0, None, 1, 2)[h % 4]}"]
            return out + [f"{a}den"]

        def pe_names1(a):
            out = [f"{a}S{n}" for n in range(3)]
            for h in range(H):
                if h < 12 and h % 4 != 1:
                    out += [f"{a}S{3 * (h // 4 + 1) + (0, None, 1, 2)[h % 4]}"]
                out += [f"{a}T{h}"]
                if h:
                    out += [f"{a}Y{h - 1}"]
            return out + [f"{a}Y{H - 1}"]

        def act_names1(a):
            out = []
            for u in range(4):
                out += [f"{a}e0_{h}" for h in range(4 * u, 4 * u + 4)] + [f"{a}e1_{h}" for h in range(4 * u, 4 * u + 4)]
            return out + [f"{a}y"]

        steps("c1_dve", dve_names(0) + dve_names(1), B // 2)
        steps("c1_pe", pe_names1(0) + pe_names1(1), B // 2)
        steps("c1_act", act_names1(0) + act_names1(1), B // 2)

        def c1_pe(eng):
            st, dv, ac = s["c1_pe"], s["c1_dve"], s["c1_act"]
            with eng.Fori(0, B // 2) as i:
                for a in range(2):
                    kp = kpad[a].rearrange("p (h k) -> p h k", h=H)

                    def S(n):
                        u, w = n // 3, n % 3
                        bk = ps[:, n % 4, :]
                        if n == 0:
                            eng.wait_ge(dv.sem, dv.at(f"{a}qs", i))
                        need = 4 * u + 4 if w == 0 else 4 * u + 2 * w
                        eng.wait_ge(dv.sem, dv.at(f"{a}kp{need - 1}", i))
                        if n >= 4:
                            m = n - 4
                            hl = 4 * (m // 3) + (3 if m % 3 == 0 else 2 * (m % 3) - 1)
                            eng.wait_ge(ac.sem, ac.at(f"{a}e{0 if m % 3 == 0 else 1}_{hl}", i))
                        if w == 0:
                            eng.matmul(bk.rearrange("p (h k) -> p h k", h=4), qst[a][:, 0:P],
                                       kp[:, 4 * u:4 * u + 4, 0:P], start=True, stop=False)
                            eng.matmul(bk.rearrange("p (h k) -> p h k", h=4), identb,
                                       causalb.rearrange("p (o k) -> p o k", o=1).broadcast_to([P, 4, P]),
                                       start=False, stop=True).then_inc(st.sem, 1)
                        else:
                            h0 = 4 * u + 2 * (w - 1)
                            o2 = bk.rearrange("p (h k) -> p h k", h=2)
                            eng.matmul(o2, qst[a][:, P:SEQ], kp[:, h0:h0 + 2, :], start=True, stop=False)
                            eng.matmul(o2[:, :, P:SEQ], identb,
                                       causalb.rearrange("p (o k) -> p o k", o=1).broadcast_to([P, 2, P]),
                                       start=False, stop=True).then_inc(st.sem, 1)

                    def tr(h):
                        u = h // 4
                        eng.wait_ge(ac.sem, ac.at(f"{a}e1_{h}", i))
                        if h >= 2:
                            eng.wait_ge(dv.sem, dv.at(f"{a}c{h - 2}", i))
                        pp0 = p0[u % 2][:, (h % 4) * P:(h % 4 + 1) * P]
                        pp1 = p1[u % 2][:, (h % 4) * SEQ:(h % 4 + 1) * SEQ]
                        bk = ps[:, 4 + h % 2, :]
                        eng.transpose(bk[:, 0:P], pp0, ident)
                        eng.transpose(bk[:, P:2 * P], pp1[:, 0:P], ident)
                        eng.transpose(bk[:, 2 * P:3 * P], pp1[:, P:SEQ], ident).then_inc(st.sem, 1)

                    def pv(h):
                        eng.wait_ge(dv.sem, dv.at(f"{a}c{h}", i))
                        if h == 0 and a == 0:
                            eng.wait_ge(ac.sem, i * ac.per + ac.base)
                        yy = ps[:, 6 + a, 0:SEQ]
                        eng.matmul(yy, vpad[a][0][:, h * P:(h + 1) * P], pT[h % 3][:, 0:SEQ],
                                   start=(h == 0), stop=False, skip_group_check=True)
                        eng.matmul(yy[:, P:SEQ], vpad[a][1][:, h * P:(h + 1) * P], pT[h % 3][:, SEQ:SEQ + P],
                                   start=False, stop=(h == H - 1), skip_group_check=True).then_inc(st.sem, 1)

                    for n in range(3):
                        S(n)
                    for h in range(H):
                        if h < 12 and h % 4 != 1:
                            S(3 * (h // 4 + 1) + (0, None, 1, 2)[h % 4])
                        tr(h)
                        if h:
                            pv(h - 1)
                    pv(H - 1)
            meet("pe", eng)

        def c1_act(eng):
            st, pe, dv = s["c1_act"], s["c1_pe"], s["c1_dve"]
            eng.preload_act_table(ACT.Exp)
            with eng.Fori(0, B // 2) as i:
                for a in range(2):
                    for u in range(4):
                        for h in range(4 * u, 4 * u + 4):
                            n = 3 * u
                            if h == 4 * u:
                                eng.wait_ge(dv.sem, dv.at(f"{a}mx{n}", i))
                                if u >= 2:
                                    eng.wait_ge(pe.sem, pe.at(f"{a}T{4 * u - 5}", i))
                            eng.activation(p0[u % 2][:, (h % 4) * P:(h % 4 + 1) * P],
                                           ps[:, n % 4, (h % 4) * P:(h % 4 + 1) * P], ACT.Exp,
                                           bias=nmx[:, 32 * a + h:32 * a + h + 1],
                                           accum_out=den1[:, 32 * a + h:32 * a + h + 1]).then_inc(st.sem, 1)
                        for h in range(4 * u, 4 * u + 4):
                            n = 3 * u + 1 + (h % 4) // 2
                            if h % 2 == 0:
                                eng.wait_ge(dv.sem, dv.at(f"{a}mx{n}", i))
                            eng.activation(p1[u % 2][:, (h % 4) * SEQ:(h % 4 + 1) * SEQ],
                                           ps[:, n % 4, (h % 2) * SEQ:(h % 2 + 1) * SEQ], ACT.Exp,
                                           bias=nmx[:, 32 * a + 16 + h:32 * a + 17 + h],
                                           accum_out=den1[:, 32 * a + 16 + h:32 * a + 17 + h]).then_inc(st.sem, 1)
                    eng.wait_ge(pe.sem, pe.at(f"{a}Y{H - 1}", i))
                    eng.activation(y1[:, bass.ds((i * 2 + a) * SEQ, SEQ)], ps[:, 6 + a, 0:SEQ], ACT.Copy)\
                       .then_inc(st.sem, 1)
            meet("act", eng)

        def c1_dve(eng):
            st, pe, ac = s["c1_dve"], s["c1_pe"], s["c1_act"]
            with eng.Fori(0, B // 2) as i:
                for a in range(2):
                    b = i * 2 + a
                    eng.tensor_copy(qst[a], q1[:, bass.ds(b * SEQ, SEQ)]).then_inc(st.sem, 1)
                    for h in range(H):
                        eng.tensor_scalar(kpad[a][:, h * SEQ:(h + 1) * SEQ], k1[:, bass.ds(b * SEQ, SEQ)],
                                          tab("hmask")[:, h:h + 1], None, ALU.mult).then_inc(st.sem, 1)
                    for c in range(2):
                        eng.tensor_copy(vpad[a][c].rearrange("p (h c) -> p h c", c=136)[:, :, 0:HD],
                                        v1[:, bass.ds(b * SEQ + c * P, P)].rearrange("p (h c) -> p h c", c=HD))\
                           .then_inc(st.sem, 1)

                    def mx(n):
                        u, w = n // 3, n % 3
                        eng.wait_ge(pe.sem, pe.at(f"{a}S{n}", i))
                        if w == 0:
                            eng.tensor_reduce(nmx[:, 32 * a + 4 * u:32 * a + 4 * u + 4],
                                              ps[:, n % 4, :].rearrange("p (h k) -> p h k", h=4), AX_X, ALU.max,
                                              negate=True).then_inc(st.sem, 1)
                        else:
                            h0 = 32 * a + 16 + 4 * u + 2 * (w - 1)
                            eng.tensor_reduce(nmx[:, h0:h0 + 2], ps[:, n % 4, :].rearrange("p (h k) -> p h k", h=2),
                                              AX_X, ALU.max, negate=True).then_inc(st.sem, 1)

                    for n in range(3):
                        mx(n)
                    for h in range(H):
                        eng.wait_ge(pe.sem, pe.at(f"{a}T{h}", i))
                        if h >= 3:
                            eng.wait_ge(pe.sem, pe.at(f"{a}Y{h - 3}", i))
                        eng.tensor_copy(pT[h % 3], ps[:, 4 + h % 2, 0:3 * P]).then_inc(st.sem, 1)
                        if h < 12 and h % 4 != 1:
                            mx(3 * (h // 4 + 1) + (0, None, 1, 2)[h % 4])
                    eng.wait_ge(ac.sem, ac.at(f"{a}e1_{H - 1}", i))
                    eng.tensor_copy(den_all[:, bass.ds(b * 32, 32)], den1[:, 32 * a:32 * a + 32])\
                       .then_inc(st.sem, 1)
            meet("dve", eng)

        steps("o1_dve0", ["rden", "rT"])
        steps("o1_dve", ["y", "yb"], NT, "o1_dve0")
        steps("o1_dve2", ["x"], NT, "o1_dve")
        steps("o1_pe0", ["rT"])
        steps("o1_pe", ["bc"], NT, "o1_pe0")
        steps("o1_pe2", ["o"], NT, "o1_pe")

        def o1_pe(eng):
            dz = s["o1_dve0"]
            eng.wait_ge(dz.sem, dz.at("rden"))
            for t in range(NTOK):
                mm = eng.transpose(ps[0:16, 4 + t // 4, (t % 4) * P:(t % 4 + 1) * P],
                                   rden_all[:, t * H:(t + 1) * H], ident)
            mm.then_inc(s["o1_pe0"].sem, 1)
            eng.wait_ge(dz.sem, dz.at("rT"))
            with eng.Fori(0, NT) as i:
                eng.matmul(bank(i), tab("sel16", 16), tile(rT, i), start=True, stop=True)\
                   .then_inc(s["o1_pe"].sem, 1)
            with eng.Fori(0, NT) as i:
                q = s["o1_dve"]
                eng.wait_ge(q.sem, q.at("yb", i))
                eng.matmul(bank(i + 4), mat("p1"), tile(y1, i), start=True, stop=True)\
                   .then_inc(s["o1_pe2"].sem, 1)
            meet("pe", eng)

        def o1_dve(eng):
            dz = s["o1_dve0"]
            eng.reciprocal(rden_all, den_all).then_inc(dz.sem, 1)
            q = s["o1_pe0"]
            eng.wait_ge(q.sem, q.at("rT"))
            eng.tensor_copy(rT, ps[0:16, 4:8, :].rearrange("p a t -> p (a t)")).then_inc(dz.sem, 1)
            st = s["o1_dve"]
            with eng.Fori(0, NT) as i:
                q = s["o1_pe"]
                eng.wait_ge(q.sem, q.at("bc", i))
                eng.tensor_tensor(tile(y1, i), tile(y1, i), bank(i), ALU.mult).then_inc(st.sem, 1)
                eng.wait_ge(st.sem, st.at("y", i))
                eng.tensor_scalar(tile(y1, i), tile(y1, i), col("bv"), None, ALU.add).then_inc(st.sem, 1)
            with eng.Fori(0, NT) as i:
                q = s["o1_pe2"]
                eng.wait_ge(q.sem, q.at("o", i))
                eng.scalar_tensor_tensor(out=tile(x, i), in0=bank(i + 4), scalar=col("bp"), in1=tile(x, i),
                                         op0=ALU.add, op1=ALU.add).then_inc(s["o1_dve2"].sem, 1)
            meet("dve", eng)

        ha = [work[:, k * N:(k + 1) * N] for k in range(4)]
        hb = [work[:, (4 + k) * N:(5 + k) * N] for k in range(4)]
        tern = {}
        at = 0
        for nm, n in (("w1", 512), ("w2", 512), ("h1", 2048), ("h2", 2048), ("w3", 512)):
            tern[nm] = wb[:, at:at + n]
            at += n
        sgl = [work[:, 16384 + k * T:16384 + (k + 1) * T] for k in range(2)]
        steps("g1_pe_a", [f"{w}{j}" for j in range(4) for w in "gu"], NT)
        steps("g1_pe_b", [f"o{j}" for j in range(4)], NT, "g1_pe_a")
        steps("g1_pe_c", [f"o{j}" for j in range(4)], NT, "g1_pe_b")
        steps("g1_pe_d", ["y"], NT, "g1_pe_c")
        steps("g1_act_a", [f"s{j}" for j in range(4)], NT)
        steps("g1_act_b", [f"h{j}" for j in range(4)], NT, "g1_act_a")
        steps("g1_act_c", [f"h{j}" for j in range(4)], NT, "g1_act_b")
        steps("g1_dve_a", [f"h{j}" for j in range(4)], NT)
        steps("g1_dve_d", ["x"], NT, "g1_dve_a")

        def g1_pe(eng):
            st, dv = s["g1_pe_a"], s["g1_dve_a"]
            eng.wait_ge(ld_w1, 16)
            with eng.Fori(0, NT) as i:
                for j in range(4):
                    if j >= 2:
                        eng.wait_ge(dv.sem, dv.at(f"h{j - 2}", i))
                    else:
                        eng.wait_ge(dv.sem, i * dv.per + dv.base)
                    eng.matmul(bank(j % 2), tern["w1"][:, j * P:(j + 1) * P], tile(xn, i), start=True, stop=True)\
                       .then_inc(st.sem, 1)
                    eng.matmul(bank(2 + j % 2), tern["w2"][:, j * P:(j + 1) * P], tile(xn, i), start=True, stop=True)\
                       .then_inc(st.sem, 1)
            for nm, src, key, akey in (("h1", ha, "g1_pe_b", "g1_act_b"), ("h2", hb, "g1_pe_c", "g1_act_c")):
                st, ac = s[key], s[akey]
                with eng.Fori(0, NT) as i:
                    if nm == "h1":
                        eng.wait_ge(dv.sem, dv.turn_end(i))
                    else:
                        pa = s["g1_act_b"]
                        eng.wait_ge(pa.sem, pa.turn_end(i))
                    for o in range(4):
                        eng.wait_ge(ac.sem, i * ac.per + (ac.base - ac.per + o + 1))
                        for k in range(4):
                            mm = eng.matmul(bank(4 + o), tern[nm][:, k * 512 + o * P:k * 512 + (o + 1) * P],
                                            tile(src[k], i), start=(k == 0), stop=(k == 3))
                        mm.then_inc(st.sem, 1)
            st, ac, dv = s["g1_pe_d"], s["g1_act_c"], s["g1_dve_d"]
            with eng.Fori(0, NT) as i:
                eng.wait_ge(ac.sem, ac.turn_end(i))
                for k in range(4):
                    mm = eng.matmul(bank(i), tern["w3"][:, k * P:(k + 1) * P], tile(ha[k], i),
                                    start=(k == 0), stop=(k == 3))
                mm.then_inc(st.sem, 1)
            meet("pe", eng)

        def g1_act(eng):
            st, pe, dv = s["g1_act_a"], s["g1_pe_a"], s["g1_dve_a"]
            eng.preload_act_table(ACT.Silu)
            with eng.Fori(0, NT) as i:
                for j in range(4):
                    eng.wait_ge(pe.sem, pe.at(f"g{j}", i))
                    if j >= 2:
                        eng.wait_ge(dv.sem, dv.at(f"h{j - 2}", i))
                    else:
                        eng.wait_ge(dv.sem, i * dv.per + dv.base)
                    eng.activation(sgl[j % 2], bank(j % 2), ACT.Silu, scale=col("w1_s", j)).then_inc(st.sem, 1)
            eng.preload_act_table(ACT.Gelu)
            for key, pkey, dst, sc in (("g1_act_b", "g1_pe_b", hb, "h1_s"), ("g1_act_c", "g1_pe_c", ha, "h2_s")):
                st, pe = s[key], s[pkey]
                with eng.Fori(0, NT) as i:
                    for o in range(4):
                        eng.wait_ge(pe.sem, pe.at(f"o{o}", i))
                        eng.activation(tile(dst[o], i), bank(4 + o), ACT.Gelu, scale=col(sc, o)).then_inc(st.sem, 1)
            meet("act", eng)

        def g1_dve(eng):
            st, pe, ac = s["g1_dve_a"], s["g1_pe_a"], s["g1_act_a"]
            with eng.Fori(0, NT) as i:
                for j in range(4):
                    eng.wait_ge(pe.sem, pe.at(f"u{j}", i))
                    eng.wait_ge(ac.sem, ac.at(f"s{j}", i))
                    eng.scalar_tensor_tensor(out=tile(ha[j], i), in0=bank(2 + j % 2), scalar=col("w2_s", j),
                                             in1=sgl[j % 2], op0=ALU.mult, op1=ALU.mult).then_inc(st.sem, 1)
            st, pe = s["g1_dve_d"], s["g1_pe_d"]
            with eng.Fori(0, NT) as i:
                eng.wait_ge(pe.sem, pe.at("y", i))
                eng.scalar_tensor_tensor(out=tile(x, i), in0=bank(i), scalar=col("w3_s"), in1=tile(x, i),
                                         op0=ALU.mult, op1=ALU.add).then_inc(st.sem, 1)
            meet("dve", eng)

        r2, k2, v2 = [work[:, k * N:(k + 1) * N] for k in range(3)]
        y2 = r2
        rpad = [work[:, 6144 + k * 4096:6144 + (k + 1) * 4096] for k in range(1)] * 2
        vp2 = [work[:, 10240 + c * VP:10240 + (c + 1) * VP] for c in range(2)]
        decay = work[:, 14592:14592 + 2048]
        kst = work[:, 16640:16640 + SEQ]
        aT = [work[:, 16896 + k * 512:16896 + (k + 1) * 512] for k in range(3)]
        kw = wb[:, 0:1024]
        s0 = wb[:, 1024:2048]
        wkt = wb[:, 2048:2064]
        wbt = wb[:, 2064:2192]
        lam = wb[:, 2192:2192 + 16]
        lamc = wb[:, 2208:2209]
        expo = wb[:, 2216:2232]
        g2 = wb[:, 2304:4352]
        steps("t2_act0", ["lam", "lamc", "wk", "wb"] + [f"d{h}" for h in range(H)])
        steps("t2_dve0", ["lamm", "lamcm", "ex"] + [f"m{h}" for h in range(H)] + [f"u{h}" for h in range(H)]
              )
        mix = {"r": work[:, 6144:8192], "k": work[:, 8192:10240], "v": work[:, 10240:12288],
               "g": work[:, 12288:14336]}
        xxs = g2
        steps("p2_dve", ["xx", "xx0", "xr", "xk", "xv", "xg"], 1, "t2_dve0")
        steps("p2_dve1", ["r", "k"], NT, "p2_dve")
        steps("p2_dve2", ["v"], NT, "p2_dve1")
        steps("p2_dve3", ["kw0", "kw1", "s00", "s01"], 1, "p2_dve2")
        steps("p2_act", ["g"], NT, "t2_act0")
        steps("p2_pe", ["r", "k", "g"], NT)
        steps("p2_pe_v", ["v"], NT, "p2_pe")
        steps("p2_pe_k", ["k0", "k1", "s0"], 1, "p2_pe_v")

        def t2_act(eng):
            st, dv = s["t2_act0"], s["t2_dve0"]
            eng.activation(lam, colv("td_bc"), ACT.Exp).then_inc(st.sem, 1)
            eng.activation(lamc, col("td_ch"), ACT.Exp).then_inc(st.sem, 1)
            eng.wait_ge(dv.sem, dv.at("ex"))
            eng.activation(wkt, expo, ACT.Exp).then_inc(st.sem, 1)
            eng.activation(wbt, tab("iota_q"), ACT.Exp, scale=lamc).then_inc(st.sem, 1)
            for h in range(H):
                eng.activation(decay[:, h * P:(h + 1) * P], tab("lag"), ACT.Exp, scale=lam[:, h:h + 1])\
                   .then_inc(st.sem, 1)

        def t2_dve(eng):
            st, ac = s["t2_dve0"], s["t2_act0"]
            eng.wait_ge(ac.sem, ac.at("lamc"))
            eng.tensor_scalar(lam, lam, 1e30, -1.0, ALU.min, ALU.mult).then_inc(st.sem, 1)
            eng.tensor_scalar(lamc, lamc, 1e30, -1.0, ALU.min, ALU.mult).then_inc(st.sem, 1)
            eng.wait_ge(st.sem, st.at("lamm"))
            eng.tensor_scalar(expo, lam, tab("rev_j"), None, ALU.mult).then_inc(st.sem, 1)
            for h in range(H):
                dh = decay[:, h * P:(h + 1) * P]
                eng.wait_ge(ac.sem, ac.at(f"d{h}"))
                eng.tensor_tensor(dh, dh, tab("before"), ALU.mult).then_inc(st.sem, 1)
            for h in range(H):
                dh = decay[:, h * P:(h + 1) * P]
                eng.wait_ge(st.sem, st.at(f"m{h}"))
                eng.scalar_tensor_tensor(out=dh, in0=ident, scalar=cols[:, COL_AT["u_bc"][0] + h:COL_AT["u_bc"][0] + h + 1],
                                         in1=dh, op0=ALU.mult, op1=ALU.add).then_inc(st.sem, 1)
            eng.wait_ge(st.sem, st.at(f"u{H - 1}"))

        def p2_pe(eng):
            st, dv = s["p2_pe"], s["p2_dve"]
            d1, ac = s["p2_dve1"], s["p2_act"]
            eng.wait_ge(dv.sem, dv.at("xg"))
            with eng.Fori(0, NT) as i:
                eng.wait_ge(d1.sem, i * d1.per + d1.base)
                eng.matmul(bank(0), mat("r2"), tile(mix["r"], i), start=True, stop=True).then_inc(st.sem, 1)
                eng.matmul(bank(1), mat("k2"), tile(mix["k"], i), start=True, stop=True).then_inc(st.sem, 1)
                eng.wait_ge(ac.sem, i * ac.per + ac.base)
                eng.matmul(bank(2), mat("g2"), tile(mix["g"], i), start=True, stop=True).then_inc(st.sem, 1)
            sv = s["p2_pe_v"]
            for t in range(NTOK):
                mm = eng.matmul(ps[:, 4 + t // 4, (t % 4) * P:(t % 4 + 1) * P], mix["v"][:, t * P:(t + 1) * P],
                                mat("v2"), start=True, stop=True)
                if t % 4 == 3:
                    mm.then_inc(sv.sem, 1)
            sk = s["p2_pe_k"]
            eng.wait_ge(d1.sem, d1.end)
            for b in range(B):
                mm = eng.matmul(ps[:, b // 4, (b % 4) * P:(b % 4 + 1) * P], mix["k"][:, b * SEQ:b * SEQ + P],
                                mat("k2"), start=True, stop=True)
                if b % 4 == 3:
                    mm.then_inc(sk.sem, 1)
            d3, d2 = s["p2_dve3"], s["p2_dve2"]
            eng.wait_ge(ac.sem, ac.end)
            eng.wait_ge(d3.sem, d3.at("kw1"))
            for b in range(B):
                mm = eng.matmul(ps[:, 2 + b // 4, (b % 4) * P:(b % 4 + 1) * P], kw[:, b * P:(b + 1) * P],
                                v2[:, b * SEQ:b * SEQ + P], start=True, stop=True)
            mm.then_inc(sk.sem, 1)
            meet("pe", eng)

        def p2_act(eng):
            eng.preload_act_table(ACT.Silu)
            st, pe = s["p2_act"], s["p2_pe"]
            dv = s["p2_dve"]
            eng.wait_ge(dv.sem, dv.at("xg"))
            with eng.Fori(0, NT) as i:
                eng.wait_ge(pe.sem, pe.at("g", i))
                eng.activation(tile(g2, i), bank(2), ACT.Silu).then_inc(st.sem, 1)
            meet("act", eng)

        def p2_dve(eng):
            st = s["p2_dve"]
            x3 = xn[:, :].rearrange("p (b t) -> p b t", t=SEQ)
            d3 = xxs.rearrange("p (b t) -> p b t", t=SEQ)
            eng.tensor_tensor(d3[:, :, 1:SEQ], x3[:, :, 0:SEQ - 1], x3[:, :, 1:SEQ], ALU.subtract)\
               .then_inc(st.sem, 1)
            eng.tensor_scalar(d3[:, :, 0:1], x3[:, :, 0:1], -1.0, None, ALU.mult).then_inc(st.sem, 1)
            eng.wait_ge(st.sem, st.at("xx0"))
            for k in "rkvg":
                eng.scalar_tensor_tensor(out=mix[k], in0=xxs, scalar=col("maa_" + k), in1=xn[:, :],
                                         op0=ALU.mult, op1=ALU.add).then_inc(st.sem, 1)
            pe, d1 = s["p2_pe"], s["p2_dve1"]
            with eng.Fori(0, NT) as i:
                eng.wait_ge(pe.sem, pe.at("r", i))
                eng.tensor_copy(tile(r2, i), bank(0)).then_inc(d1.sem, 1)
                eng.wait_ge(pe.sem, pe.at("k", i))
                eng.tensor_copy(tile(k2, i), bank(1)).then_inc(d1.sem, 1)
            pv, d2 = s["p2_pe_v"], s["p2_dve2"]
            for i in range(NT):
                eng.wait_ge(pv.sem, pv.at("v", i))
                eng.tensor_copy(v2[:, i * T:(i + 1) * T], bank(4 + i)).then_inc(d2.sem, 1)
            pk, d3s = s["p2_pe_k"], s["p2_dve3"]
            wk = wkt.rearrange("p (o h c) -> p o h c", o=1, c=1).broadcast_to([P, 4, H, HD])
            for n in range(2):
                eng.wait_ge(pk.sem, pk.at(f"k{n}"))
                eng.tensor_tensor(kw[:, n * T:(n + 1) * T].rearrange("p (b h c) -> p b h c", h=H, c=HD),
                                  bank(n).rearrange("p (b h c) -> p b h c", h=H, c=HD), wk, ALU.mult)\
                   .then_inc(d3s.sem, 1)
            eng.wait_ge(pk.sem, pk.at("s0"))
            same = tab("grp").rearrange("p (o c) -> p o c", o=1).broadcast_to([P, 4, P])
            for n in range(2):
                eng.scalar_tensor_tensor(out=s0[:, n * T:(n + 1) * T].rearrange("p (b c) -> p b c", c=P),
                                         in0=bank(2 + n).rearrange("p (b c) -> p b c", c=P), scalar=float(HD),
                                         in1=same, op0=ALU.mult, op1=ALU.mult).then_inc(d3s.sem, 1)
            meet("dve", eng)

        steps("c2_dve0", ["z0", "z1"])
        steps("c2_dve", ["ks"] + [f"rp{h}" for h in range(H)] + ["v0", "v1"] + [f"a{n}" for n in range(8)], B, "c2_dve0")
        steps("c2_act", ["y"], B)
        steps("c2_pe", [f"S{n}" for n in range(3)] + [x_ for n in range(8) for x_ in
              ([f"S{n + 3}"] if n + 3 < 8 else []) + [f"Y{n}"]], B)

        def c2_pe(eng):
            st, dv, ac = s["c2_pe"], s["c2_dve"], s["c2_act"]
            rp = rpad[0].rearrange("p (h q) -> p h q", h=H)
            eng.wait_ge(dv.sem, dv.base)
            with eng.Fori(0, B) as b:
                def S(n):
                    c, u = n // 4, n % 4
                    eng.wait_ge(dv.sem, dv.at(f"rp{4 * u + 3}", b))
                    if n >= 4:
                        eng.wait_ge(dv.sem, dv.at(f"a{n - 4}", b))
                    eng.matmul(ps[:, n % 4, :].rearrange("p (h q) -> p h q", h=4), kst[:, c * P:(c + 1) * P],
                               rp[:, 4 * u:4 * u + 4, c * P:(c + 1) * P], start=True, stop=True).then_inc(st.sem, 1)

                def Y(n):
                    c, u = n // 4, n % 4
                    eng.wait_ge(dv.sem, dv.at(f"a{n}", b))
                    if n == 0:
                        eng.wait_ge(ac.sem, b * ac.per + ac.base)
                    for h in range(4 * u, 4 * u + 4):
                        mm = eng.matmul(ps[:, 4, c * P:(c + 1) * P], vp2[c][:, h * P:(h + 1) * P],
                                        aT[n % 3][:, (h % 4) * P:(h % 4 + 1) * P],
                                        start=(h == 0), stop=(h == H - 1), skip_group_check=True)
                    mm.then_inc(st.sem, 1)

                for n in range(3):
                    S(n)
                for n in range(8):
                    if n + 3 < 8:
                        S(n + 3)
                    Y(n)
            meet("pe", eng)

        def c2_act(eng):
            st, pe = s["c2_act"], s["c2_pe"]
            with eng.Fori(0, B) as b:
                eng.wait_ge(pe.sem, pe.turn_end(b))
                eng.activation(y2q[:, bass.ds(b * SEQ, SEQ)], ps[:, 4, 0:SEQ], ACT.Copy).then_inc(st.sem, 1)
            meet("act", eng)

        def c2_dve(eng):
            z, st, pe = s["c2_dve0"], s["c2_dve"], s["c2_pe"]
            for c in range(2):
                eng.memset(vp2[c], 0.0).then_inc(z.sem, 1)
            eng.wait_ge(z.sem, z.end)
            with eng.Fori(0, B) as b:
                eng.wait_ge(pe.sem, b * pe.per + pe.base)
                eng.tensor_copy(kst, k2[:, bass.ds(b * SEQ, SEQ)]).then_inc(st.sem, 1)
                for h in range(H):
                    eng.tensor_scalar(rpad[0][:, h * SEQ:(h + 1) * SEQ], r2[:, bass.ds(b * SEQ, SEQ)],
                                      tab("hmask")[:, h:h + 1], None, ALU.mult).then_inc(st.sem, 1)
                for c in range(2):
                    eng.tensor_copy(vp2[c].rearrange("p (h c) -> p h c", c=136)[:, :, 0:HD],
                                    v2[:, bass.ds(b * SEQ + c * P, P)].rearrange("p (h c) -> p h c", c=HD))\
                       .then_inc(st.sem, 1)
                for n in range(8):
                    u = n % 4
                    eng.wait_ge(pe.sem, pe.at(f"S{n}", b))
                    if n >= 3:
                        eng.wait_ge(pe.sem, pe.at(f"Y{n - 3}", b))
                    eng.tensor_tensor(aT[n % 3], ps[:, n % 4, :], decay[:, u * 4 * P:(u + 1) * 4 * P], ALU.mult)\
                       .then_inc(st.sem, 1)
            meet("dve", eng)

        y2q = k2
        gn = {"c": work[:, 6144:8192], "q": work[:, 8192:10240], "r": work[:, 10240:12288]}
        rwb = work[:, 12288:13312]
        steps("o2_dve0", ["rw", "x0", "x1"])
        steps("o2_dve1", ["c"], NT, "o2_dve0")
        steps("o2_dve2", ["n", "b", "g"], NT, "o2_dve1")
        steps("o2_dve3", ["x"], NT, "o2_dve2")
        steps("o2_act1", ["sq"], NT)
        steps("o2_act2", ["log"], NT, "o2_act1")
        steps("o2_act3", ["rstd"], NT, "o2_act2")
        steps("o2_pe0", ["x"])
        steps("o2_pe1", ["mean"], NT, "o2_pe0")
        steps("o2_pe2", ["var"], NT, "o2_pe1")
        steps("o2_pe3", ["o"], NT, "o2_pe2")

        def o2_pe(eng):
            dz = s["o2_dve0"]
            eng.wait_ge(dz.sem, dz.at("rw"))
            for b in range(B):
                mm = eng.matmul(ps[:, b // 4, (b % 4) * P:(b % 4 + 1) * P], s0[:, b * P:(b + 1) * P],
                                rwb[:, b * P:(b + 1) * P], start=True, stop=True)
            mm.then_inc(s["o2_pe0"].sem, 1)
            eng.wait_ge(dz.sem, dz.at("x1"))
            with eng.Fori(0, NT) as i:
                eng.matmul(bank(i), tab("grp"), tile(y2q, i), start=True, stop=True).then_inc(s["o2_pe1"].sem, 1)
            with eng.Fori(0, NT) as i:
                q = s["o2_act1"]
                eng.wait_ge(q.sem, q.at("sq", i))
                eng.matmul(bank(i + 4), tab("grp"), tile(gn["q"], i), start=True, stop=True)\
                   .then_inc(s["o2_pe2"].sem, 1)
            with eng.Fori(0, NT) as i:
                q = s["o2_dve2"]
                eng.wait_ge(q.sem, q.at("g", i))
                eng.matmul(bank(i), mat("o2"), tile(gn["c"], i), start=True, stop=True).then_inc(s["o2_pe3"].sem, 1)
            meet("pe", eng)

        def o2_act(eng):
            eng.preload_act_table(ACT.Ln)
            with eng.Fori(0, NT) as i:
                q = s["o2_dve1"]
                eng.wait_ge(q.sem, q.at("c", i))
                eng.activation(tile(gn["q"], i), tile(gn["c"], i), ACT.Square).then_inc(s["o2_act1"].sem, 1)
            with eng.Fori(0, NT) as i:
                q = s["o2_pe2"]
                eng.wait_ge(q.sem, q.at("var", i))
                eng.activation(tile(gn["r"], i), bank(i + 4), ACT.Ln, bias=eps_ap(EPS_GN), scale=DOWN)\
                   .then_inc(s["o2_act2"].sem, 1)
            eng.preload_act_table(ACT.Exp)
            with eng.Fori(0, NT) as i:
                q = s["o2_act2"]
                eng.wait_ge(q.sem, q.at("log", i))
                eng.activation(tile(gn["r"], i), tile(gn["r"], i), ACT.Exp, bias=epst[:, 4:5], scale=-0.5)\
                   .then_inc(s["o2_act3"].sem, 1)
            meet("act", eng)

        def o2_dve(eng):
            st = s["o2_dve0"]
            r3 = r2.rearrange("p (b t) -> p b t", t=SEQ)
            y3 = y2q.rearrange("p (b t) -> p b t", t=SEQ)
            eng.tensor_tensor(rwb.rearrange("p (b q) -> p b q", q=P), r3[:, :, P:SEQ],
                              wbt.rearrange("p (o q) -> p o q", o=1).broadcast_to([P, B, P]), ALU.mult)\
               .then_inc(st.sem, 1)
            q = s["o2_pe0"]
            eng.wait_ge(q.sem, q.at("x"))
            for n in range(2):
                yy = y3[:, 4 * n:4 * n + 4, P:SEQ]
                eng.tensor_tensor(yy, yy, bank(n).rearrange("p (b q) -> p b q", q=P), ALU.add).then_inc(st.sem, 1)
            with eng.Fori(0, NT) as i:
                q = s["o2_pe1"]
                eng.wait_ge(q.sem, q.at("mean", i))
                eng.tensor_tensor(tile(gn["c"], i), tile(y2q, i), bank(i), ALU.subtract)\
                   .then_inc(s["o2_dve1"].sem, 1)
            st = s["o2_dve2"]
            with eng.Fori(0, NT) as i:
                q = s["o2_act3"]
                eng.wait_ge(q.sem, q.at("rstd", i))
                eng.scalar_tensor_tensor(out=tile(gn["c"], i), in0=tile(gn["c"], i), scalar=col("ln_g"),
                                         in1=tile(gn["r"], i), op0=ALU.mult, op1=ALU.mult).then_inc(st.sem, 1)
                eng.wait_ge(st.sem, st.at("n", i))
                eng.tensor_scalar(tile(gn["c"], i), tile(gn["c"], i), col("ln_b"), None, ALU.add)\
                   .then_inc(st.sem, 1)
                eng.wait_ge(st.sem, st.at("b", i))
                eng.tensor_tensor(tile(gn["c"], i), tile(gn["c"], i), tile(g2, i), ALU.mult).then_inc(st.sem, 1)
            with eng.Fori(0, NT) as i:
                q = s["o2_pe3"]
                eng.wait_ge(q.sem, q.at("o", i))
                eng.tensor_tensor(tile(x, i), tile(x, i), bank(i), ALU.add).then_inc(s["o2_dve3"].sem, 1)
            meet("dve", eng)

        q3, k3, v3 = [work[:, k * N:(k + 1) * N] for k in range(3)]
        SC3 = 1.0 / float(P) ** 0.5
        steps("p3_pe", ["q", "k"], NT)
        steps("p3_pe_v", ["v"], NT, "p3_pe")
        steps("p3_dve", ["q", "k"], NT)
        steps("p3_dve_v", ["v"], NT, "p3_dve")

        def p3_pe(eng):
            st, dv = s["p3_pe"], s["p3_dve"]
            with eng.Fori(0, NT) as i:
                eng.wait_ge(dv.sem, i * dv.per + dv.base)
                eng.matmul(bank(0), mat("q3"), tile(xn, i), start=True, stop=True).then_inc(st.sem, 1)
                eng.matmul(bank(1), mat("k3"), tile(xn, i), start=True, stop=True).then_inc(st.sem, 1)
            for t in range(NTOK):
                mm = eng.matmul(ps[:, 4 + t // 4, (t % 4) * P:(t % 4 + 1) * P], xn[:, t * P:(t + 1) * P], mat("v3"),
                                start=True, stop=True)
                if t % 4 == 3:
                    mm.then_inc(s["p3_pe_v"].sem, 1)
            meet("pe", eng)

        def p3_dve(eng):
            st, pe = s["p3_dve"], s["p3_pe"]
            with eng.Fori(0, NT) as i:
                for nm, dst, k in (("q", q3, 0), ("k", k3, 1)):
                    eng.wait_ge(pe.sem, pe.at(nm, i))
                    eng.tensor_copy(tile(dst, i), bank(k)).then_inc(st.sem, 1)
            for i in range(NT):
                q = s["p3_pe_v"]
                eng.wait_ge(q.sem, q.at("v", i))
                eng.tensor_copy(v3[:, i * T:(i + 1) * T], bank(4 + i)).then_inc(s["p3_dve_v"].sem, 1)
            meet("dve", eng)

        c3 = 6144
        pr3 = [work[:, c3 + k * 512:c3 + (k + 1) * 512] for k in range(2)]
        vs3 = [work[:, c3 + 1024 + k * SEQ:c3 + 1024 + (k + 1) * SEQ] for k in range(2)]
        sm3 = [work[:, c3 + 2048 + k * 16:c3 + 2048 + (k + 1) * 16] for k in range(2)]
        steps("c3_pe", [f"{a}{w}" for a in range(2) for w in ("S", "o")], B // 2)
        steps("c3_act", [f"{a}{w}" for a in range(2) for w in ("k", "e0", "e1")], B // 2)
        steps("c3_dve", [f"{a}{w}" for a in range(2) for w in ("mx", "nb", "rd", "v0", "v1", "x")], B // 2)

        kst3 = [work[:, c3 + 3072 + k * SEQ:c3 + 3072 + (k + 1) * SEQ] for k in range(2)]
        def c3_pe(eng):
            st, dv, ac = s["c3_pe"], s["c3_dve"], s["c3_act"]
            with eng.Fori(0, B // 2) as i:
                for a in range(2):
                    b = i * 2 + a
                    eng.wait_ge(ac.sem, ac.at(f"{a}k", i))
                    eng.wait_ge(dv.sem, i * dv.per + dv.base)
                    for c in range(2):
                        mm = eng.matmul(ps[:, a, c * SEQ:(c + 1) * SEQ], kst3[a][:, c * P:(c + 1) * P],
                                        q3[:, bass.ds(b * SEQ, SEQ)], start=True, stop=True)
                    mm.then_inc(st.sem, 1)
                    eng.wait_ge(dv.sem, dv.at(f"{a}v1", i))
                    for c in range(2):
                        mm = eng.matmul(ps[:, 2 + a, 0:SEQ], vs3[a][:, c * P:(c + 1) * P],
                                        pr3[a][:, c * SEQ:(c + 1) * SEQ], start=(c == 0), stop=(c == 1))
                    mm.then_inc(st.sem, 1)
            meet("pe", eng)

        def c3_act(eng):
            st, dv, pe = s["c3_act"], s["c3_dve"], s["c3_pe"]
            eng.preload_act_table(ACT.Exp)
            with eng.Fori(0, B // 2) as i:
                for a in range(2):
                    eng.wait_ge(pe.sem, i * pe.per + pe.base)
                    eng.activation(kst3[a], k3[:, bass.ds((i * 2 + a) * SEQ, SEQ)], ACT.Copy).then_inc(st.sem, 1)
                    eng.wait_ge(dv.sem, dv.at(f"{a}nb", i))
                    for c in range(2):
                        eng.activation(pr3[a][:, c * SEQ:(c + 1) * SEQ], ps[:, a, c * SEQ:(c + 1) * SEQ], ACT.Exp,
                                       bias=sm3[a][:, 2 + c:3 + c], scale=SC3,
                                       accum_out=sm3[a][:, 4 + c:5 + c]).then_inc(st.sem, 1)
            meet("act", eng)

        def c3_dve(eng):
            st, pe, ac = s["c3_dve"], s["c3_pe"], s["c3_act"]
            with eng.Fori(0, B // 2) as i:
                for a in range(2):
                    b = i * 2 + a
                    eng.wait_ge(pe.sem, pe.at(f"{a}S", i))
                    eng.tensor_reduce(sm3[a][:, 0:2], ps[:, a, :].rearrange("p (c q) -> p c q", c=2), AX_X, ALU.max)\
                       .then_inc(st.sem, 1)
                    eng.wait_ge(st.sem, st.at(f"{a}mx", i))
                    eng.tensor_scalar(sm3[a][:, 2:4], sm3[a][:, 0:2], -SC3, None, ALU.mult).then_inc(st.sem, 1)
                    eng.wait_ge(ac.sem, ac.at(f"{a}e1", i))
                    eng.reciprocal(sm3[a][:, 6:8], sm3[a][:, 4:6]).then_inc(st.sem, 1)
                    eng.wait_ge(st.sem, st.at(f"{a}rd", i))
                    for c in range(2):
                        eng.tensor_scalar(vs3[a][:, c * P:(c + 1) * P], v3[:, bass.ds(b * SEQ + c * P, P)],
                                          sm3[a][:, 6 + c:7 + c], None, ALU.mult).then_inc(st.sem, 1)
                    eng.wait_ge(pe.sem, pe.at(f"{a}o", i))
                    xt = x[:, bass.ds(b * SEQ, SEQ)]
                    eng.tensor_tensor(xt, xt, ps[:, 2 + a, 0:SEQ], ALU.add).then_inc(st.sem, 1)
            meet("dve", eng)

        PHASES = ["ln0", "r0", "sf0", "ef0", "a0", "b0", "ln1", "p1", "c1", "o1", "g1", "ln2", "r2", "p2", "x2", "c2", "o2", "b2",
                  "ln3", "r3", "p3", "x3", "c3", "b3"]
        WA_FREE = PHASES.index("o1") + 2
        ALL = len(PHASES) + 1

        set_up = sem("set_up")

        def clear(L, eng):
            for a in range(0, SLOTS[L], T):
                n = min(T, SLOTS[L] - a)
                eng.dma_start(xg[L][a:a + n, :].rearrange("(a p) d -> p a d", p=P),
                              zeros[:, 0:n].rearrange("p (a d) -> p a d", d=P)).then_inc(zeroed[L], 16)

        block = ctx.enter_context(nc.Block())

        @block.sync
        def _(eng):
            eng.dma_start(x[:, :], d["x"]).then_inc(ld_x, 16)
            eng.dma_start(tabs[:, :], d["tabs"]).then_inc(ld_x, 16)
            eng.dma_start(mats[:, :], d["mats"]).then_inc(ld_small, 16)
            eng.dma_start(cols[:, :], d["cols"]).then_inc(ld_small, 16)
            eng.dma_start(work[:, 0:4 * P], d["bft"]).then_inc(ld_small, 16)
            eng.wait_ge(zeros_made, 1)
            clear(0, eng)
            eng.dma_start(yg[0][E * CAP:E * CAP + P, :], zeros[:, 0:P]).then_inc(zeroed[0], 16)
            eng.dma_start(wa[:, :], d["w0"]).then_inc(ld_w0, 16)
            eng.dma_start(wb[:, :], d["w1"]).then_inc(ld_w1, 16)
            clear(2, eng)
            clear(3, eng)
            ef0_sync(eng)
            for n in met:
                eng.wait_ge(met[n], WA_FREE)
            eng.dma_start(wa[:, :], d["w23"]).then_inc(ld_w23, 16)
            x_sync(2, eng)
            x_sync(3, eng)
            for n in met:
                eng.wait_ge(met[n], ALL)
            eng.dma_start(d["out"], x[:, :]).then_inc(stored, 16)
            eng.wait_ge(stored, 16)

        @block.gpsimd
        def _(eng):
            eng.memset(zeros[:, :], 0.0).then_inc(zeros_made, 1)
            for q in started:
                eng.sem_inc(q, 1)
            for k, v in enumerate(EPSV):
                eng.memset(epst[:, k:k + 1], v * DOWN)
            eng.memset(ones16[:, :], 1.0)
            eng.memset(one8[:, :], 1.0)
            eng.memset(epst[:, 4:5], 0.5 * math.log(DOWN)).then_inc(set_up, 1)
            for L in (0, 2, 3):
                scatter(L, eng)
                gather(L, eng)

        @block.tensor
        def _(eng):
            eng.wait_ge(set_up, 1)
            eng.wait_ge(ld_x, 32)
            meet("pe", eng)
            ln_pe(0, eng)
            eng.wait_ge(ld_small, 48)
            r_pe(0, eng)
            eng.wait_ge(ld_w0, 16)
            sf0_pe(eng)
            ef0_pe(eng)
            a0_pe(eng)
            b_pe(0, eng)
            ln_pe(1, eng)
            p1_pe(eng)
            c1_pe(eng)
            o1_pe(eng)
            g1_pe(eng)
            ln_pe(2, eng)
            r_pe(2, eng)
            p2_pe(eng)
            x_pe(2, eng)
            c2_pe(eng)
            o2_pe(eng)
            b_pe(2, eng)
            ln_pe(3, eng)
            r_pe(3, eng)
            p3_pe(eng)
            x_pe(3, eng)
            c3_pe(eng)
            b_pe(3, eng)

        @block.scalar
        def _(eng):
            eng.wait_ge(set_up, 1)
            meet("act", eng)
            ln_act(0, eng)
            eng.wait_ge(ld_small, 48)
            r_act(0, eng)
            sf0_act(eng)
            ef0_act(eng)
            a0_act(eng)
            b_act(0, eng)
            ln_act(1, eng)
            meet("act", eng)
            c1_act(eng)
            meet("act", eng)
            g1_act(eng)
            ln_act(2, eng)
            r_act(2, eng)
            t2_act(eng)
            p2_act(eng)
            x_act(2, eng)
            c2_act(eng)
            o2_act(eng)
            b_act(2, eng)
            ln_act(3, eng)
            r_act(3, eng)
            meet("act", eng)
            x_act(3, eng)
            c3_act(eng)
            b_act(3, eng)

        @block.vector
        def _(eng):
            eng.wait_ge(set_up, 1)
            eng.wait_ge(ld_small, 48)
            eng.tensor_copy(bft[:, :], work[:, 0:4 * P])
            meet("dve", eng)
            ln_dve(0, eng)
            r_dve(0, eng)
            sf0_dve(eng)
            ef0_dve(eng)
            a0_dve(eng)
            b_dve(0, eng)
            ln_dve(1, eng)
            p1_dve(eng)
            c1_dve(eng)
            o1_dve(eng)
            g1_dve(eng)
            ln_dve(2, eng)
            r_dve(2, eng)
            t2_dve(eng)
            p2_dve(eng)
            x_dve(2, eng)
            c2_dve(eng)
            o2_dve(eng)
            b_dve(2, eng)
            ln_dve(3, eng)
            r_dve(3, eng)
            p3_dve(eng)
            x_dve(3, eng)
            c3_dve(eng)
            b_dve(3, eng)


def tables():
    import numpy as np
    f = np.float64
    t = {}
    t["ones_d"] = np.full((P, P), 1.0 / P)
    t["ident"] = np.eye(P)
    w = np.power(0.001, np.linspace(0.0, 1.0, P))[:, None]
    a = 1e-5
    s = np.arange(SEQ, dtype=f)[None, :]
    t["dec_c"], t["dec_s"] = np.exp(-a * s) * np.cos(w * s), np.exp(-a * s) * np.sin(w * s)
    t["gro_c"], t["gro_s"] = np.exp(a * s) * np.cos(w * s), np.exp(a * s) * np.sin(w * s)
    t["nxt_c"], t["nxt_s"] = np.exp(a * (s + 1)) * np.cos(w * (s + 1)), -np.exp(a * (s + 1)) * np.sin(w * (s + 1))
    keep = np.ones((P, T))
    keep[:, ::SEQ] = 0
    t["keep"] = keep
    th = 1.0 / 10000.0 ** (np.arange(0, HD, 2) / HD)
    p = np.arange(P)
    ang = (p // HD * th[(p % HD) // 2])[:, None]
    sign = np.where(p % 2 == 0, -1.0, 1.0)[:, None]
    t["cosk"], t["sink"] = np.cos(ang), sign * np.sin(ang)
    t["cosq"], t["sinq"] = t["cosk"] / HD ** 0.5, t["sink"] / HD ** 0.5
    t["hmask"] = (p[:, None] // HD == np.arange(H)[None, :])
    t["code"] = np.tile(E - np.arange(E), (P, 1))
    j, q = p[:, None], p[None, :]
    t["lag"] = np.maximum(q - j - 1, 0)
    t["before"] = j < q
    t["iota_q"] = np.tile(p, (P, 1))
    t["rev_j"] = (P - 1 - p)[:, None]
    t["grp"] = (j // HD == q // HD) / HD
    t["sel16"] = (j == q // HD)
    t["keep_t"] = np.tile(np.arange(P) % NTOK != 0, (P, 1))
    t["first_slot"] = np.tile(np.arange(E) * CAP - 1, (P, 1))
    t["starts"] = np.tile(P * np.arange(NTOK), (P, 1))
    t["tiles"] = np.tile(np.arange(42), (P, 1))
    t["places"] = np.tile([1, E, E * E], (P, 14))
    tabs = np.concatenate([np.asarray(t[n], np.float32).reshape(P, -1) for n, _ in TABS], axis=1)
    bft = [np.eye(P), np.where(q > j, NEG, 0.0), j <= q, np.ones((P, P))]
    return tabs, np.concatenate([np.asarray(b, np.float32) for b in bft], axis=1)


def kernel(**inputs):
    import numpy as _np
    import concourse.bacc as _bacc
    from concourse import mybir as _mybir
    from concourse.bass_utils import run_bass_kernel_spmd as _run

    a = {k: _np.asarray(v) for k, v in inputs.items()}
    cat = _np.concatenate
    swap = _np.arange(P) ^ 1
    wa1, ba1 = a["L1_attn_W_attn"], a["L1_attn_b_attn"]
    wq, wk, wv = wa1[:, 0:P], wa1[:, P:2 * P], wa1[:, 2 * P:]
    bq, bk, bv = ba1[0:P], ba1[P:2 * P], ba1[2 * P:]
    w3 = a["L3_attn_W"]
    m = {"z0": a["L0_attn_Wz"].T, "za0": a["L0_attn_Wza"].T, "y0": a["L0_attn_Wy"].T, "ya0": a["L0_attn_Wya"].T,
         "q1": wq, "qs1": wq[:, swap], "k1": wk, "ks1": wk[:, swap], "v1": wv, "p1": a["L1_attn_W_proj"],
         "r2": a["L2_attn_w_r"].T, "k2": a["L2_attn_w_k"].T, "v2": a["L2_attn_w_v"].T, "g2": a["L2_attn_w_g"].T,
         "o2": a["L2_attn_w_o"].T, "q3": w3[:, 0:P], "k3": w3[:, P:2 * P], "v3": w3[:, 2 * P:]}
    mats = cat([m[n] for n in MATS], axis=1)

    def rows(v, n):
        return _np.tile(v[None, :], (P, 1)) if n is None else v.reshape(n, P).T

    def below(v):
        return cat([v, _np.zeros((P - v.shape[0], v.shape[1]), v.dtype)], axis=0)

    c = {"bz": rows(a["L0_attn_bz"], 1), "bza": rows(a["L0_attn_bza"], 1), "by": rows(a["L0_attn_by"], 1),
         "bya": rows(a["L0_attn_bya"], 1), "norm_w": rows(a["L0_attn_norm_w"], 1),
         "lc_re": rows(a["L0_attn_lc_re"], 1), "lc_im": rows(a["L0_attn_lc_im"], 1),
         "bq": rows(bq, 1), "bqs": rows(bq[swap], 1), "bk": rows(bk, 1), "bks": rows(bk[swap], 1),
         "bv": rows(bv, 1), "bp": rows(a["L1_attn_b_proj"], 1),
         "w1_s": rows(a["L1_ffn_w1_s"], 4), "w2_s": rows(a["L1_ffn_w2_s"], 4), "h1_s": rows(a["L1_ffn_h1_s"], 4),
         "h2_s": rows(a["L1_ffn_h2_s"], 4), "w3_s": rows(a["L1_ffn_w3_s"], 1),
         "maa_k": rows(a["L2_attn_time_maa_k"], 1), "maa_v": rows(a["L2_attn_time_maa_v"], 1),
         "maa_r": rows(a["L2_attn_time_maa_r"], 1), "maa_g": rows(a["L2_attn_time_maa_g"], 1),
         "td_ch": rows(_np.repeat(a["L2_attn_time_decay"], HD), 1), "ln_g": rows(a["L2_attn_ln_g"], 1),
         "ln_b": rows(a["L2_attn_ln_b"], 1), "td_bc": rows(a["L2_attn_time_decay"], None),
         "u_bc": rows(a["L2_attn_time_faaaa"], None), "b1_2": rows(a["L2_ffn_b1"].reshape(-1), E * 4),
         "router0": a["L0_ffn_router_w"].T, "wgred2": below(a["L2_ffn_wg_red"]), "wg2": below(a["L2_ffn_wg"].T),
         "gate3": a["L3_ffn_w_gate"]}
    cols = cat([c[n] for n, _ in COLS], axis=1)

    def up(w):
        return w.transpose(1, 0, 2).reshape(P, -1)

    def down(w):
        return w.reshape(-1, P, w.shape[-1]).transpose(1, 0, 2).reshape(P, -1)

    w0 = cat([up(a["L0_ffn_rg"]), up(a["L0_ffn_ru"]), down(a["L0_ffn_rd"]), a["L0_ffn_sg"], a["L0_ffn_su"],
              down(a["L0_ffn_sd"])], axis=1)
    w1 = cat([a["L1_ffn_w1_w"].T, a["L1_ffn_w2_w"].T, down(a["L1_ffn_h1_w"].T), down(a["L1_ffn_h2_w"].T),
              down(a["L1_ffn_w3_w"].T)], axis=1)
    w23 = cat([cat([a["L2_ffn_w1"][e], down(a["L2_ffn_w2"][e]), rows(a["L2_ffn_b2"][e], None)], axis=1)
               for e in range(E)]
              + [cat([a["L3_ffn_w1"][e], a["L3_ffn_w3"][e], down(a["L3_ffn_w2"][e])], axis=1) for e in range(E)],
              axis=1)
    tabs, bft = tables()
    arrays = {"x": a["L0_attn_x"].reshape(N, P).T, "mats": mats, "cols": cols, "tabs": tabs, "bft": bft,
              "w0": w0, "w1": w1, "w23": w23}
    arrays = {k: _np.ascontiguousarray(v) for k, v in arrays.items()}

    nc = _bacc.Bacc("TRN2", target_bir_lowering=False, num_devices=1)
    d = {k: nc.dram_tensor(f"in_{k}", v.shape, _mybir.dt.from_np(v.dtype), kind="ExternalInput").ap()
         for k, v in arrays.items()}
    d["out"] = nc.dram_tensor("out", (P, N), F32, kind="ExternalOutput").ap()
    build(nc, d)
    r = _run(nc, [{f"in_{k}": v for k, v in arrays.items()}], core_ids=[0])
    return _np.ascontiguousarray(r.results[0]["out"].T).reshape(B, SEQ, P)
```

```python
import math
from contextlib import ExitStack

import concourse.bass as bass
from concourse import mybir

F32 = mybir.dt.float32
BF16 = mybir.dt.bfloat16
I32 = mybir.dt.int32
U32 = mybir.dt.uint32
ALU = mybir.AluOpType
ACT = mybir.ActivationFunctionType
AX_X = mybir.AxisListType.X

P = 128
B, SEQ = 8, 256
N = B * SEQ
T = 512
NT = N // T
NTOK = N // P
SPT = T // SEQ
E = 8
CAP = int(1.25 * N / E)
H, HD = 16, 8
HID0, SH0 = 512, 1024
HID2 = 512
HID3 = 256
NTILES = {2: 24, 3: 39}
MAX_TILES = NTILES[3] + 3
EPS_LN = 1e-5
EPS_RMS = 1e-6
EPS_GN = 1e-5 * 64
EPS_GATE = 1e-4
EPS_F32 = 1.1920928955078125e-07
NEG = -1e30
DOWN = 2.0 ** -16

MATS = ["z0", "za0", "y0", "ya0", "q1", "qs1", "k1", "ks1", "v1", "p1",
        "r2", "k2", "v2", "g2", "o2", "q3", "k3", "v3"]
COLS = [("bz", 1), ("bza", 1), ("by", 1), ("bya", 1), ("norm_w", 1), ("lc_re", 1), ("lc_im", 1),
        ("bq", 1), ("bqs", 1), ("bk", 1), ("bks", 1), ("bv", 1), ("bp", 1),
        ("w1_s", 4), ("w2_s", 4), ("h1_s", 4), ("h2_s", 4), ("w3_s", 1),
        ("maa_k", 1), ("maa_v", 1), ("maa_r", 1), ("maa_g", 1), ("td_ch", 1), ("ln_g", 1), ("ln_b", 1),
        ("td_bc", H), ("u_bc", H), ("b1_2", E * 4),
        ("wgred2", P), ("wg2", E),
        ("ident0", P), ("router0", E), ("ident2", P), ("gate2", E), ("ident3", P), ("gate3", E)]
TABS = [("ones_d", P), ("ident", P), ("dec_c", SEQ), ("dec_s", SEQ), ("gro_c", SEQ), ("gro_s", SEQ),
        ("nxt_c", SEQ), ("nxt_s", SEQ), ("keep", T), ("cosq", 1), ("sinq", 1), ("cosk", 1), ("sink", 1),
        ("cosq_row", P), ("sinq_row", P), ("cosk_row", P), ("sink_row", P),
        ("code", E), ("lag", P), ("before", P), ("iota_q", P), ("rev_j", 1), ("grp", P), ("sel16", P),
        ("keep_t", P), ("first_slot", E), ("tiles", MAX_TILES), ("places", MAX_TILES), ("starts", NTOK)]


def offsets(items):
    at, out = 0, {}
    for name, n in items:
        out[name] = (at, n)
        at += n
    return out, at


COL_AT, COL_N = offsets(COLS)
TAB_AT, TAB_N = offsets(TABS)


class Steps:

    def __init__(self, sem, names, turns=1, base=0):
        self.sem, self.names, self.base = sem, {n: k + 1 for k, n in enumerate(names)}, base
        self.per = len(names)
        self.end = base + turns * self.per

    def at(self, name, turn=0):
        return turn * self.per + (self.base + self.names[name])

    def turn_end(self, turn=0):
        return turn * self.per + (self.base + self.per)


def build(nc, d):
    ctx = ExitStack()
    with ctx:
        def sb(name, shape, dt=F32):
            return ctx.enter_context(nc.sbuf_tensor(name, shape, dt))

        def sem(name):
            return ctx.enter_context(nc.semaphore(name))

        x = sb("x", [P, N])
        xn = sb("xn", [P, N])
        mats = sb("mats", [P, len(MATS) * P])
        cols = sb("cols", [P, COL_N])
        tabs = sb("tabs", [P, TAB_N])
        bft = sb("bft", [P, 4 * P], BF16)
        wa = sb("wa", [P, 15360])
        wb = sb("wb", [P, 5632])
        work = sb("work", [P, 19968])
        rt = work[:, 10240:11520].rearrange("p (a b) -> p a b", b=NTOK * E)
        ps = ctx.enter_context(nc.psum_tensor("ps", [P, 8, T], F32))

        def mat(name):
            k = MATS.index(name)
            return mats[:, k * P:(k + 1) * P]

        def col(name, k=0, rows=P):
            return cols[0:rows, COL_AT[name][0] + k:COL_AT[name][0] + k + 1]

        def colv(name, rows=P):
            a, n = COL_AT[name]
            return cols[0:rows, a:a + n]

        def tab(name, rows=P):
            a, n = TAB_AT[name]
            return tabs[0:rows, a:a + n]

        def tabseq(name):
            return tab(name).rearrange("p (o s) -> p o s", o=1).broadcast_to([P, SPT, SEQ])

        def two(ap):
            return ap.rearrange("p (o s) -> p o s", s=SEQ)

        identb, causalb, upto, onesb = [bft[:, k * P:(k + 1) * P] for k in range(4)]
        ident = tab("ident")

        def tile(ap, i):
            return ap[:, bass.ds(i * T, T)]

        def bank(k):
            return ps[:, k, :] if isinstance(k, int) else ps[:, bass.ds(k, 1), :].rearrange("p o t -> p (o t)")

        ld_x, ld_small, ld_w0, ld_w1, ld_w23, stored = [sem(n) for n in
            ("ld_x", "ld_small", "ld_w0", "ld_w1", "ld_w23", "stored")]
        met = {n: sem(f"met_{n}") for n in ("pe", "act", "dve")}
        passed = {n: [0] for n in met}

        def meet(name, eng):
            passed[name][0] += 1
            eng.drain().then_inc(met[name], 1)
            for other in met:
                if other != name:
                    eng.wait_ge(met[other], passed[name][0])

        s = {}
        started = []

        def steps(key, names, turns=1, after=None):
            if after is None:
                s[key] = Steps(sem(key), names, turns, 1)
                started.append(s[key].sem)
            else:
                s[key] = Steps(s[after].sem, names, turns, s[after].end)
            return s[key]

        for L in range(4):
            prev = (lambda k: None if L == 0 else f"ln{L - 1}_{k}")
            steps(f"ln{L}_pe1", ["mean"], NT, f"ln{L-1}_pe2" if L else None)
            steps(f"ln{L}_pe2", ["var"], NT, f"ln{L}_pe1")
            steps(f"ln{L}_dve1", ["centred"], NT, f"ln{L-1}_dve2" if L else None)
            steps(f"ln{L}_dve2", ["normed"], NT, f"ln{L}_dve1")
            steps(f"ln{L}_act1", ["sq"], NT, f"ln{L-1}_act3" if L else None)
            steps(f"ln{L}_act2", ["log"], NT, f"ln{L}_act1")
            steps(f"ln{L}_act3", ["rstd"], NT, f"ln{L}_act2")

        ln_sq = work[:, 0:2048]
        ln_rs = work[:, 2048:4096]

        def ln_pe(L, eng):
            a, b = s[f"ln{L}_pe1"], s[f"ln{L}_pe2"]
            with eng.Fori(0, NT) as i:
                eng.matmul(bank(i), tab("ones_d"), tile(x, i), start=True, stop=True).then_inc(a.sem, 1)
            with eng.Fori(0, NT) as i:
                q = s[f"ln{L}_act1"]
                eng.wait_ge(q.sem, q.at("sq", i))
                eng.matmul(bank(i + 4), tab("ones_d"), tile(ln_sq, i), start=True, stop=True).then_inc(b.sem, 1)
            meet("pe", eng)

        def ln_dve(L, eng):
            a, b = s[f"ln{L}_dve1"], s[f"ln{L}_dve2"]
            with eng.Fori(0, NT) as i:
                q = s[f"ln{L}_pe1"]
                eng.wait_ge(q.sem, q.at("mean", i))
                eng.tensor_tensor(tile(xn, i), tile(x, i), bank(i), ALU.subtract).then_inc(a.sem, 1)
            with eng.Fori(0, NT) as i:
                q = s[f"ln{L}_act3"]
                eng.wait_ge(q.sem, q.at("rstd", i))
                eng.tensor_tensor(tile(xn, i), tile(xn, i), tile(ln_rs, i), ALU.mult).then_inc(b.sem, 1)
            meet("dve", eng)

        def ln_act(L, eng):
            a, b, c = s[f"ln{L}_act1"], s[f"ln{L}_act2"], s[f"ln{L}_act3"]
            eng.preload_act_table(ACT.Ln)
            with eng.Fori(0, NT) as i:
                q = s[f"ln{L}_dve1"]
                eng.wait_ge(q.sem, q.at("centred", i))
                eng.activation(tile(ln_sq, i), tile(xn, i), ACT.Square).then_inc(a.sem, 1)
            with eng.Fori(0, NT) as i:
                q = s[f"ln{L}_pe2"]
                eng.wait_ge(q.sem, q.at("var", i))
                eng.activation(tile(ln_rs, i), bank(i + 4), ACT.Ln, bias=eps_ap(EPS_LN), scale=DOWN).then_inc(b.sem, 1)
            eng.preload_act_table(ACT.Exp)
            with eng.Fori(0, NT) as i:
                eng.wait_ge(b.sem, b.at("log", i))
                eng.activation(tile(ln_rs, i), tile(ln_rs, i), ACT.Exp, bias=epst[:, 4:5], scale=-0.5)\
                   .then_inc(c.sem, 1)
            meet("act", eng)

        epst = sb("epst", [P, 5])
        EPSV = [EPS_LN, EPS_RMS, EPS_GN, EPS_F32]

        def eps_ap(v):
            k = EPSV.index(v)
            return epst[:, k:k + 1]

        a0 = dict(sz=0, zc=2048, zs=4096, h=6144, rs=8192, hc=10240)
        A0 = {k: work[:, v:v + 2048] for k, v in a0.items()}
        A0["hc"] = work[:, 10240:10496]
        A0["h2"] = work[:, 10496:10496 + 2048]
        steps("a0_pe1", ["z"], NT)
        steps("a0_pe2", ["ms"], NT, "a0_pe1")
        steps("a0_pe3", ["y"], NT, "a0_pe2")
        steps("a0_act1", ["silu_z"], NT)
        steps("a0_act2", ["sq"], NT, "a0_act1")
        steps("a0_act3", ["log"], NT, "a0_act2")
        steps("a0_act4", ["rstd"], NT, "a0_act3")
        steps("a0_act5", ["silu_y"], NT, "a0_act4")
        steps("a0_dve0", ["cross_re", "cross"])
        steps("a0_dve1", ["z", "zc", "zs", "cc", "cs", "hc", "hs", "h", "hx"], NT, "a0_dve0")
        steps("a0_dve2", ["normed"], NT, "a0_dve1")
        steps("a0_dve3", ["y", "x"], NT, "a0_dve2")

        def a0_pe(eng):
            with eng.Fori(0, NT) as i:
                eng.matmul(bank(i), mat("z0"), tile(xn, i), start=True, stop=True)
                eng.matmul(bank(i + 4), mat("za0"), tile(xn, i), start=True, stop=True)\
                   .then_inc(s["a0_pe1"].sem, 1)
            with eng.Fori(0, NT) as i:
                q = s["a0_act2"]
                eng.wait_ge(q.sem, q.at("sq", i))
                eng.matmul(bank(i), tab("ones_d"), tile(A0["sz"], i), start=True, stop=True)\
                   .then_inc(s["a0_pe2"].sem, 1)
            with eng.Fori(0, NT) as i:
                q = s["a0_dve2"]
                eng.wait_ge(q.sem, q.at("normed", i))
                eng.matmul(bank(i), mat("y0"), tile(A0["h2"], i), start=True, stop=True)
                eng.matmul(bank(i + 4), mat("ya0"), tile(xn, i), start=True, stop=True)\
                   .then_inc(s["a0_pe3"].sem, 1)
            meet("pe", eng)

        def a0_act(eng):
            eng.preload_act_table(ACT.Silu)
            with eng.Fori(0, NT) as i:
                q = s["a0_pe1"]
                eng.wait_ge(q.sem, q.at("z", i))
                eng.activation(tile(A0["sz"], i), bank(i + 4), ACT.Silu, bias=col("bza"))\
                   .then_inc(s["a0_act1"].sem, 1)
            eng.preload_act_table(ACT.Ln)
            with eng.Fori(0, NT) as i:
                q = s["a0_dve1"]
                eng.wait_ge(q.sem, q.at("hx", i))
                eng.activation(tile(A0["sz"], i), tile(A0["h"], i), ACT.Square).then_inc(s["a0_act2"].sem, 1)
            with eng.Fori(0, NT) as i:
                q = s["a0_pe2"]
                eng.wait_ge(q.sem, q.at("ms", i))
                eng.activation(tile(A0["rs"], i), bank(i), ACT.Ln, bias=eps_ap(EPS_RMS), scale=DOWN)\
                   .then_inc(s["a0_act3"].sem, 1)
            eng.preload_act_table(ACT.Exp)
            with eng.Fori(0, NT) as i:
                q = s["a0_act3"]
                eng.wait_ge(q.sem, q.at("log", i))
                eng.activation(tile(A0["rs"], i), tile(A0["rs"], i), ACT.Exp, bias=epst[:, 4:5], scale=-0.5)\
                   .then_inc(s["a0_act4"].sem, 1)
            eng.preload_act_table(ACT.Silu)
            with eng.Fori(0, NT) as i:
                q = s["a0_pe3"]
                eng.wait_ge(q.sem, q.at("y", i))
                eng.activation(tile(A0["sz"], i), bank(i + 4), ACT.Silu, bias=col("bya"))\
                   .then_inc(s["a0_act5"].sem, 1)
            meet("act", eng)

        def a0_dve(eng):
            c = s["a0_dve0"]
            eng.tensor_scalar(A0["hc"], tab("nxt_c"), col("lc_re"), None, ALU.mult).then_inc(c.sem, 1)
            eng.wait_ge(c.sem, c.at("cross_re"))
            eng.scalar_tensor_tensor(out=A0["hc"], in0=tab("nxt_s"), scalar=col("lc_im"), in1=A0["hc"],
                                     op0=ALU.mult, op1=ALU.add).then_inc(c.sem, 1)
            eng.wait_ge(c.sem, c.at("cross"))
            hc = A0["hc"].rearrange("p (o s) -> p o s", o=1).broadcast_to([P, SPT, SEQ])
            st = s["a0_dve1"]
            with eng.Fori(0, NT) as i:
                q = s["a0_act1"]
                eng.wait_ge(q.sem, q.at("silu_z", i))
                eng.scalar_tensor_tensor(out=tile(A0["h2"], i), in0=bank(i), scalar=col("bz"),
                                         in1=tile(A0["sz"], i), op0=ALU.add, op1=ALU.mult).then_inc(st.sem, 1)
                eng.wait_ge(st.sem, st.at("z", i))
                eng.tensor_tensor(two(tile(A0["zc"], i)), two(tile(A0["h2"], i)), tabseq("dec_c"), ALU.mult)\
                   .then_inc(st.sem, 1)
                eng.tensor_tensor(two(tile(A0["zs"], i)), two(tile(A0["h2"], i)), tabseq("dec_s"), ALU.mult)\
                   .then_inc(st.sem, 1)
                eng.wait_ge(st.sem, st.at("zc", i))
                eng.tensor_tensor_scan(tile(A0["h"], i), tab("keep"), tile(A0["zc"], i), 0.0,
                                       ALU.mult, ALU.add).then_inc(st.sem, 1)
                eng.wait_ge(st.sem, st.at("cc", i))
                eng.tensor_tensor_scan(tile(A0["rs"], i), tab("keep"), tile(A0["zs"], i), 0.0,
                                       ALU.mult, ALU.add).then_inc(st.sem, 1)
                eng.tensor_tensor(two(tile(A0["zc"], i)), two(tile(A0["h"], i)), tabseq("gro_c"), ALU.mult)\
                   .then_inc(st.sem, 1)
                eng.wait_ge(st.sem, st.at("cs", i))
                eng.tensor_tensor(two(tile(A0["zs"], i)), two(tile(A0["rs"], i)), tabseq("gro_s"), ALU.mult)\
                   .then_inc(st.sem, 1)
                eng.wait_ge(st.sem, st.at("hs", i))
                eng.tensor_tensor(tile(A0["h"], i), tile(A0["zc"], i), tile(A0["zs"], i), ALU.add)\
                   .then_inc(st.sem, 1)
                eng.wait_ge(st.sem, st.at("h", i))
                eng.tensor_tensor(two(tile(A0["h"], i)), two(tile(A0["h"], i)), hc, ALU.add)\
                   .then_inc(st.sem, 1)
            with eng.Fori(0, NT) as i:
                q = s["a0_act4"]
                eng.wait_ge(q.sem, q.at("rstd", i))
                eng.scalar_tensor_tensor(out=tile(A0["h2"], i), in0=tile(A0["h"], i), scalar=col("norm_w"),
                                         in1=tile(A0["rs"], i), op0=ALU.mult, op1=ALU.mult)\
                   .then_inc(s["a0_dve2"].sem, 1)
            st = s["a0_dve3"]
            with eng.Fori(0, NT) as i:
                q = s["a0_act5"]
                eng.wait_ge(q.sem, q.at("silu_y", i))
                eng.scalar_tensor_tensor(out=tile(A0["zc"], i), in0=bank(i), scalar=col("by"),
                                         in1=tile(A0["sz"], i), op0=ALU.add, op1=ALU.mult).then_inc(st.sem, 1)
                eng.wait_ge(st.sem, st.at("y", i))
                eng.tensor_tensor(tile(x, i), tile(x, i), tile(A0["zc"], i), ALU.add).then_inc(st.sem, 1)
            meet("dve", eng)

        R = {k: rt[:, n, :].rearrange("p (t e) -> p t e", e=E) for n, k in enumerate(
            ("lg", "eq", "oh1", "lg2", "oh2", "t1", "t2", "cum", "cumb"))}
        flat = {k: rt[:, n, :] for n, k in enumerate(
            ("lg", "eq", "oh1", "lg2", "oh2", "t1", "t2", "cum", "cumb", "tt"))}
        rk = sb("rk", [P, 12, NTOK])
        Q = {k: rk[:, n, :] for n, k in enumerate(
            ("m1", "cm", "m2", "d", "e2", "w1", "w2", "rms", "p1", "p2", "k1", "k2"))}
        slots = sb("slots", [P, 2, NTOK], U32)
        ex = sb("ex", [P, 4, E])
        etab = sb("etab", [1, MAX_TILES // 3], I32)
        selb = sb("selb", [P, NTOK * E], BF16)
        wgn = sb("wgn", [16, 3, E])
        ones16 = sb("ones16", [16, 16])
        inc = work[:, 11520:11776].rearrange("p (a b) -> p a b", a=2)
        XT = {0: 16384, 2: 16640, 3: 16384}
        xtok = {L: work[:, a:a + N] for L, a in XT.items()}
        xsq = work[:, 0:N]
        assert NTILES[2] >= (N + E * (P - 1)) // P and NTILES[3] >= (2 * N + E * (P - 1)) // P
        SLOTS = {0: E * CAP, 2: (NTILES[2] + 3) * P, 3: (NTILES[3] + 3) * P}
        xg = {L: nc.dram_tensor(f"xg{L}", (SLOTS[L], P), F32, kind="Internal").ap() for L in SLOTS}
        yg = {L: nc.dram_tensor(f"yg{L}", (SLOTS[L] + P if L == 0 else NTILES[L] * P, P), F32, kind="Internal").ap()
              for L in SLOTS}
        zeroed = {L: sem(f"zeroed{L}") for L in SLOTS}
        scattered = {L: sem(f"scattered{L}") for L in SLOTS}
        gathered = {(L, k): sem(f"gathered{L}_{k}") for L in SLOTS for k in range(2)}
        CH = {0: 2, 2: 1, 3: 2}
        GOT = {0: work[:, 14336:18432], 2: wa[:, 0:2048], 3: wa[:, 0:4096]}

        zeros = work[:, 19456:19968]
        ZEROS = {L: -(-SLOTS[L] // T) + (L == 0) for L in SLOTS}
        zeros_made = sem("zeros_made")

        def chunk0(table, c):
            return table[c * T:(c + 1) * T, :].rearrange("(a p) d -> p a d", p=P)

        def chunk0_sb(ap, c):
            return ap[:, c * T:(c + 1) * T].rearrange("p (a d) -> p a d", d=P)

        def bce(ap):
            return ap.rearrange("p (t o) -> p t o", o=1).broadcast_to([P, NTOK, E])

        code = tab("code").rearrange("p (o e) -> p o e", o=1).broadcast_to([P, NTOK, E])

        best1 = ["m1", "eq", "cd", "cm", "oh1"]
        best2 = ["lg2", "m2", "eq2", "cd2", "cm2", "oh2"]
        where = ["tt", "inc", "exc", "cum"]
        spans = ["sp", "nt", "end", "st", "base", "cmp", "cnt", "min", "pl", "pk", "etab"]
        DVE_R = {
            0: [f"x{g}" for g in range(6)] + ["rms", "lg"] + best1 + best2 + ["sel", "d"] + where + ["base"]
               + [f"{w}{k}" for k in (1, 2) for w in "apksfdzi"] + ["den", "w1", "w2", "w1k", "w2k"],
            2: ["nmax", "wginv", "wgu", "wc"] + [f"x{g}" for g in range(6)] + best1 + ["sel", "lgm"]
               + where + spans + ["s1", "f1", "f1b", "g1", "den", "w1"],
            3: [f"x{g}" for g in range(6)] + best1 + best2 + ["sel", "d"] + where + spans
               + ["s1", "f1", "f1b", "g1", "s2", "f2", "f2b", "g2", "den", "w1", "w2"]}
        PE_R = {0: [f"t{g}" for g in range(6)] + ["cnt"], 2: ["nrm", "wc"] + [f"t{g}" for g in range(6)] + ["cnt"],
                3: [f"t{g}" for g in range(6)] + ["cnt"]}
        rows_ = [f"c{g}" for g in range(6)]
        ACT_R = {0: [n for g in range(6) for n in [f"c{g}"] + [f"q{t}" for t in range(3 * g, min(3 * g + 3, NTOK))]]
                    + ["log", "rms", "e2"], 2: ["sqw", "root"] + rows_ + ["e2"], 3: rows_ + ["e2"]}
        for L in (0, 2, 3):
            steps(f"r{L}_dve", DVE_R[L])
            steps(f"r{L}_pe", PE_R[L])
            steps(f"r{L}_act", ACT_R[L])
        TW = P + E
        wc = cols[:, COL_AT["gate2"][0]:COL_AT["gate2"][0] + E]

        def group(g):
            return range(3 * g, min(3 * g + 3, NTOK))

        def r_pe(L, eng):
            st, dv, ac = s[f"r{L}_pe"], s[f"r{L}_dve"], s[f"r{L}_act"]
            at = COL_AT[f"ident{L}"][0]
            rw = cols[:, at:at + TW]
            if L == 2:
                eng.wait_ge(ac.sem, ac.at("sqw"))
                eng.matmul(ps[0:16, 7, 0:E], ones16[:, :], wgn[:, 0, :], start=True, stop=True).then_inc(st.sem, 1)
                eng.wait_ge(dv.sem, dv.at("wgu"))
                eng.matmul(ps[:, 7, E:2 * E], colv("wgred2", 16), wgn[:, 2, :], start=True, stop=True)\
                   .then_inc(st.sem, 1)
                eng.wait_ge(dv.sem, dv.at("wc"))
            for g in range(6):
                for n, t in enumerate(group(g)):
                    xt = xn[:, t * P:(t + 1) * P]
                    mm = eng.matmul(ps[:, g, n * TW:(n + 1) * TW], xt, rw, start=True, stop=True)
                mm.then_inc(st.sem, 1)
            eng.wait_ge(dv.sem, dv.at("sel"))
            eng.matmul(ps[:, 6, 0:P], upto, selb[:, :], start=True, stop=True)
            eng.matmul(ps[:, 6, P:2 * P], onesb, selb[:, :], start=True, stop=True).then_inc(st.sem, 1)
            meet("pe", eng)

        def r_act(L, eng):
            st, dv, pe = s[f"r{L}_act"], s[f"r{L}_dve"], s[f"r{L}_pe"]
            if L == 2:
                eng.activation(wgn[:, 0, :], colv("wg2", 16), ACT.Square).then_inc(st.sem, 1)
                eng.wait_ge(pe.sem, pe.at("nrm"))
                eng.activation(wgn[:, 1, :], ps[0:16, 7, 0:E], ACT.Sqrt).then_inc(st.sem, 1)
            for g in range(6):
                k = len(group(g))
                eng.wait_ge(dv.sem, dv.at(f"x{g}"))
                eng.activation(xtok[L][:, 3 * g * P:(3 * g + k) * P].rearrange("p (t c) -> p t c", c=P),
                               ps[:, g, 0:k * TW].rearrange("p (t c) -> p t c", c=TW)[:, :, 0:P], ACT.Copy)\
                   .then_inc(st.sem, 1)
                if L == 0:
                    eng.wait_ge(st.sem, st.at(f"c{g}"))
                    for t in group(g):
                        eng.activation(xsq[:, t * P:(t + 1) * P], xtok[0][:, t * P:(t + 1) * P], ACT.Square,
                                       accum_out=Q["rms"][:, t:t + 1]).then_inc(st.sem, 1)
            if L == 0:
                eng.wait_ge(st.sem, st.at(f"q{NTOK - 1}"))
                eng.activation(Q["d"], Q["rms"], ACT.Ln, bias=eps_ap(EPS_F32), scale=DOWN / P).then_inc(st.sem, 1)
                eng.wait_ge(st.sem, st.at("log"))
                eng.activation(Q["rms"], Q["d"], ACT.Exp, bias=epst[:, 4:5], scale=-0.5).then_inc(st.sem, 1)
            if L == 2:
                eng.wait_ge(dv.sem, dv.at("lgm"))
                eng.activation(R["t1"], R["eq"], ACT.Exp).then_inc(st.sem, 1)
            else:
                eng.wait_ge(dv.sem, dv.at("d"))
                eng.activation(Q["e2"], Q["d"], ACT.Exp).then_inc(st.sem, 1)
            meet("act", eng)

        def r_dve(L, eng):
            st, pe, ac = s[f"r{L}_dve"], s[f"r{L}_pe"], s[f"r{L}_act"]
            n = [0]

            def did(ins, name):
                ins.then_inc(st.sem, 1)
                n[0] += 1
                assert st.names[name] == n[0], (L, name, n[0])
                eng.wait_ge(st.sem, st.at(name))

            if L == 2:
                eng.wait_ge(ac.sem, ac.at("root"))
                did(eng.tensor_scalar(wgn[:, 1, :], wgn[:, 1, :], EPS_GATE, None, ALU.max), "nmax")
                did(eng.reciprocal(wgn[:, 0, :], wgn[:, 1, :]), "wginv")
                did(eng.tensor_tensor(wgn[:, 2, :], wgn[:, 0, :], colv("wg2", 16), ALU.mult), "wgu")
                eng.wait_ge(pe.sem, pe.at("wc"))
                did(eng.tensor_copy(wc[:, :], ps[:, 7, E:2 * E]), "wc")
            for g in range(6):
                k = len(group(g))
                eng.wait_ge(pe.sem, pe.at(f"t{g}"))
                v = ps[:, g, 0:k * TW].rearrange("p (t c) -> p t c", c=TW)
                eng.tensor_copy((R["lg2"] if L == 0 else R["lg"])[:, 3 * g:3 * g + k, :], v[:, :, P:TW])\
                   .then_inc(st.sem, 1)
                n[0] += 1
            eng.wait_ge(st.sem, st.at("x5"))
            if L == 0:
                eng.wait_ge(ac.sem, ac.at("rms"))
                did(eng.tensor_copy(R["t1"], bce(Q["rms"])), "rms")
                did(eng.tensor_tensor(R["lg"], R["lg2"], R["t1"], ALU.mult), "lg")

            def best(lg, names, m, oh):
                did(eng.tensor_reduce(Q[m], lg, AX_X, ALU.max), names[0])
                did(eng.tensor_tensor(R["eq"], lg, bce(Q[m]), ALU.is_equal), names[1])
                did(eng.tensor_tensor(R["eq"], R["eq"], code, ALU.mult), names[2])
                did(eng.tensor_reduce(Q["cm"], R["eq"], AX_X, ALU.max), names[3])
                did(eng.tensor_tensor(R[oh], R["eq"], bce(Q["cm"]), ALU.is_equal), names[4])

            best(R["lg"], best1, "m1", "oh1")
            if L == 2:
                did(eng.tensor_copy(selb[:, :], flat["oh1"]), "sel")
                did(eng.tensor_tensor(R["eq"], R["lg"], bce(Q["m1"]), ALU.subtract), "lgm")
            else:
                did(eng.scalar_tensor_tensor(out=R["lg2"], in0=R["oh1"], scalar=NEG, in1=R["lg"],
                                             op0=ALU.mult, op1=ALU.add), "lg2")
                best(R["lg2"], best2[1:], "m2", "oh2")
                did(eng.tensor_tensor(selb[:, :], flat["oh1"], flat["oh2"], ALU.add), "sel")
                did(eng.tensor_tensor(Q["d"], Q["m2"], Q["m1"], ALU.subtract), "d")
            eng.wait_ge(pe.sem, pe.at("cnt"))
            e_t = lambda ap: ap.rearrange("p (e t) -> p e t", t=NTOK)
            did(eng.tensor_copy(e_t(flat["tt"]), ps[:, 6, P:2 * P].rearrange("p (t e) -> p e t", e=E)), "tt")
            did(eng.tensor_tensor_scan(inc[:, 0, :], tab("keep_t"), flat["tt"], 0.0, ALU.mult, ALU.add), "inc")
            did(eng.tensor_tensor(inc[:, 1, :], inc[:, 0, :], flat["tt"], ALU.subtract), "exc")
            did(eng.tensor_tensor(R["cum"], ps[:, 6, 0:P].rearrange("p (t e) -> p t e", e=E),
                                  inc[:, 1, :].rearrange("p (e t) -> p t e", t=NTOK), ALU.add), "cum")

            def of_choice(k, what, name, out):
                oh = R[f"oh{k}"]
                did(eng.tensor_tensor(R["t2"], oh, R[what], ALU.mult), name[0])
                did(eng.tensor_reduce(out, R["t2"], AX_X, ALU.add), name[1])

            if L == 0:
                fs = tab("first_slot").rearrange("p (o e) -> p o e", o=1).broadcast_to([P, NTOK, E])
                did(eng.tensor_tensor(R["cumb"], R["cum"], fs, ALU.add), "base")
                for k in (1, 2):
                    of_choice(k, "cum", (f"a{k}", f"p{k}"), Q[f"p{k}"])
                    did(eng.tensor_scalar(Q[f"k{k}"], Q[f"p{k}"], float(CAP), None, ALU.is_le), f"k{k}")
                    of_choice(k, "cumb", (f"s{k}", f"f{k}"), Q[f"p{k}"])
                    did(eng.tensor_scalar(Q["cm"], Q[f"k{k}"], -float(E * CAP), float(E * CAP), ALU.mult, ALU.add),
                        f"d{k}")
                    did(eng.tensor_tensor(Q[f"p{k}"], Q[f"p{k}"], Q[f"k{k}"], ALU.mult), f"z{k}")
                    did(eng.tensor_tensor(slots[:, k - 1, :], Q[f"p{k}"], Q["cm"], ALU.add), f"i{k}")
            else:
                c = {k: ex[:, n, :] for n, k in enumerate(("nt", "end", "st", "base"))}
                last = e_t(inc[:, 0, :])[:, :, NTOK - 1:NTOK].rearrange("p e o -> p (e o)")
                starts = tab("starts").rearrange("p (o t) -> p o t", o=1).broadcast_to([P, E, NTOK])
                did(eng.tensor_tensor(e_t(flat["cumb"]), starts,
                                      last.rearrange("p (e o) -> p e o", o=1).broadcast_to([P, E, NTOK]),
                                      ALU.is_lt), "sp")
                did(eng.tensor_reduce(c["nt"], e_t(flat["cumb"]), AX_X, ALU.add), "nt")
                did(eng.tensor_tensor_scan(c["end"], one8[:, :], c["nt"], 0.0,
                                           ALU.mult, ALU.add), "end")
                did(eng.tensor_tensor(c["st"], c["end"], c["nt"], ALU.subtract), "st")
                did(eng.tensor_scalar(c["base"], c["st"], float(P), -1.0, ALU.mult, ALU.add), "base")
                ctmp = tile_ex[0:1, 0:MAX_TILES * E].rearrange("p (t e) -> p t e", e=E)
                did(eng.tensor_tensor(ctmp, c["end"][0:1, :].rearrange("p (o e) -> p o e", o=1)
                                      .broadcast_to([1, MAX_TILES, E]),
                                      tab("tiles", 1).rearrange("p (t o) -> p t o", o=1)
                                      .broadcast_to([1, MAX_TILES, E]),
                                      ALU.is_le), "cmp")
                exps = tile_ex[0:1, MAX_TILES * E:MAX_TILES * (E + 1)]
                did(eng.tensor_reduce(exps, ctmp, AX_X, ALU.add), "cnt")
                did(eng.tensor_scalar(exps, exps, float(E - 1), None, ALU.min), "min")
                did(eng.tensor_tensor(exps, exps, tab("places", 1), ALU.mult), "pl")
                did(eng.tensor_reduce(tile_ex[0:1, 0:MAX_TILES // 3], exps.rearrange("p (t k) -> p t k", k=3),
                                      AX_X, ALU.add), "pk")
                did(eng.tensor_copy(etab[:, :], tile_ex[0:1, 0:MAX_TILES // 3]), "etab")
                bb = c["base"].rearrange("p (o e) -> p o e", o=1).broadcast_to([P, NTOK, E])
                for k in range(1, CH[L] + 1):
                    did(eng.tensor_tensor(R["cumb"], R["cum"], bb, ALU.add), f"s{k}")
                    did(eng.tensor_tensor(R["t2"], R[f"oh{k}"], R["cumb"], ALU.mult), f"f{k}")
                    did(eng.tensor_reduce(Q[f"p{k}"], R["t2"], AX_X, ALU.add), f"f{k}b")
                    did(eng.tensor_copy(slots[:, k - 1, :], Q[f"p{k}"]), f"g{k}")
            eng.wait_ge(ac.sem, ac.at("e2"))
            if L == 2:
                did(eng.tensor_reduce(Q["d"], R["t1"], AX_X, ALU.add), "den")
                did(eng.reciprocal(Q["w1"], Q["d"]), "w1")
            else:
                did(eng.tensor_scalar(Q["w2"], Q["e2"], 1.0, None, ALU.add), "den")
                did(eng.reciprocal(Q["w1"], Q["w2"]), "w1")
                did(eng.tensor_tensor(Q["w2"], Q["e2"], Q["w1"], ALU.mult), "w2")
                if L == 0:
                    did(eng.tensor_tensor(Q["w1"], Q["w1"], Q["k1"], ALU.mult), "w1k")
                    did(eng.tensor_tensor(Q["w2"], Q["w2"], Q["k2"], ALU.mult), "w2k")
            assert n[0] == st.per, (L, n[0], st.per)
            meet("dve", eng)

        one8 = sb("one8", [P, E])
        tile_ex = sb("tile_ex", [1, MAX_TILES * (E + 1)])

        def scatter(L, eng):
            dv = s[f"r{L}_dve"]
            eng.wait_ge(dv.sem, dv.at("i2" if L == 0 else f"g{CH[L]}"))
            eng.wait_ge(s[f"r{L}_act"].sem, s[f"r{L}_act"].at("c5"))
            eng.wait_ge(zeroed[L], 16 * ZEROS[L])
            for k in range(CH[L]):
                for t in range(NTOK):
                    eng.indirect_dma_start(xg[L], bass.IndirectOffsetOnAxis(ap=slots[:, k, t:t + 1], axis=0),
                                           xtok[L][:, t * P:(t + 1) * P], None, bounds_check=SLOTS[L] - 1,
                                           oob_is_err=False).then_inc(scattered[L], 16)

        def gather(L, eng):
            rows = yg[L].shape[0]
            if L == 0:
                eng.wait_ge(yg0_stored, 16 * NCH0)
            else:
                for k in range(3):
                    eng.wait_ge(s[f"x{L}_stored{k}"].sem, 16 * TURNS[L] + 1)
            for k in range(CH[L]):
                for t in range(NTOK):
                    eng.indirect_dma_start(GOT[L][:, k * N + t * P:k * N + (t + 1) * P], None, yg[L],
                                           bass.IndirectOffsetOnAxis(ap=slots[:, k, t:t + 1], axis=0),
                                           bounds_check=rows - 1, oob_is_err=False).then_inc(gathered[L, k], 16)

        for L in (0, 2, 3):
            steps(f"b{L}_act", [f"a{t}" for t in range(NTOK)])
            steps(f"b{L}_dve", ([f"m{t}" for t in range(NTOK)] if CH[L] == 2 else []) + [f"x{i}" for i in range(NT)])
            steps(f"b{L}_pe", [f"t{i}" for i in range(NT)])

        def b_act(L, eng):
            st = s[f"b{L}_act"]
            eng.wait_ge(gathered[L, 0], 16 * NTOK)
            for t in range(NTOK):
                g = GOT[L][:, t * P:(t + 1) * P]
                eng.activation(g, g, ACT.Copy, scale=Q["w1"][:, t:t + 1]).then_inc(st.sem, 1)
            meet("act", eng)

        def b_dve(L, eng):
            st, ac, pe = s[f"b{L}_dve"], s[f"b{L}_act"], s[f"b{L}_pe"]
            if CH[L] == 2:
                eng.wait_ge(gathered[L, 1], 16 * NTOK)
                for t in range(NTOK):
                    g, h2_ = GOT[L][:, t * P:(t + 1) * P], GOT[L][:, N + t * P:N + (t + 1) * P]
                    eng.wait_ge(ac.sem, ac.at(f"a{t}"))
                    eng.scalar_tensor_tensor(out=g, in0=h2_, scalar=Q["w2"][:, t:t + 1], in1=g,
                                             op0=ALU.mult, op1=ALU.add).then_inc(st.sem, 1)
            for i in range(NT):
                eng.wait_ge(pe.sem, pe.at(f"t{i}"))
                xt = x[:, i * T:(i + 1) * T]
                eng.tensor_tensor(xt, xt, bank(i), ALU.add).then_inc(st.sem, 1)
            meet("dve", eng)

        def b_pe(L, eng):
            st, ac, dv = s[f"b{L}_pe"], s[f"b{L}_act"], s[f"b{L}_dve"]
            for t in range(NTOK):
                if CH[L] == 2:
                    eng.wait_ge(dv.sem, dv.at(f"m{t}"))
                else:
                    eng.wait_ge(ac.sem, ac.at(f"a{t}"))
                mm = eng.transpose(ps[:, t // 4, (t % 4) * P:(t % 4 + 1) * P], GOT[L][:, t * P:(t + 1) * P], ident)
                if t % 4 == 3:
                    mm.then_inc(st.sem, 1)
            meet("pe", eng)


        SW0 = 3 * E * HID0
        NS = SH0 // P
        sf_w = [[wa[:, SW0 + m * SH0 + j * P:SW0 + m * SH0 + (j + 1) * P] for m in range(3)] for j in range(NS)]
        names = []
        for k in range(NS + 2):
            names += ([f"g{k}", f"u{k}"] if k < NS else []) + ([f"d{k - 2}"] if k >= 2 else [])
        steps("sf0_pe", names, NT)
        steps("sf0_act", [f"s{k}" for k in range(NS)], NT)
        steps("sf0_dve", [f"h{k}" for k in range(NS)] + ["x"], NT)
        sf_sg = [work[:, k * T:(k + 1) * T] for k in range(2)]
        sf_h = [work[:, (2 + k) * T:(3 + k) * T] for k in range(3)]

        def sf0_pe(eng):
            st, dv = s["sf0_pe"], s["sf0_dve"]
            with eng.Fori(0, NT) as i:
                for k in range(NS + 2):
                    if k < NS:
                        if k >= 2:
                            eng.wait_ge(dv.sem, dv.at(f"h{k - 2}", i))
                        eng.matmul(bank(k % 2), sf_w[k][0], tile(xn, i), start=True, stop=True).then_inc(st.sem, 1)
                        eng.matmul(bank(2 + k % 2), sf_w[k][1], tile(xn, i), start=True, stop=True)\
                           .then_inc(st.sem, 1)
                    if k >= 2:
                        j = k - 2
                        if j == 0:
                            eng.wait_ge(dv.sem, i * dv.per + dv.base)
                        eng.wait_ge(dv.sem, dv.at(f"h{j}", i))
                        eng.matmul(bank(6), sf_w[j][2], sf_h[j % 3], start=(j == 0), stop=(j == NS - 1))\
                           .then_inc(st.sem, 1)
            meet("pe", eng)

        def sf0_act(eng):
            st, pe, dv = s["sf0_act"], s["sf0_pe"], s["sf0_dve"]
            eng.preload_act_table(ACT.Silu)
            with eng.Fori(0, NT) as i:
                for k in range(NS):
                    eng.wait_ge(pe.sem, pe.at(f"g{k}", i))
                    if k >= 2:
                        eng.wait_ge(dv.sem, dv.at(f"h{k - 2}", i))
                    eng.activation(sf_sg[k % 2], bank(k % 2), ACT.Silu).then_inc(st.sem, 1)
            meet("act", eng)

        def sf0_dve(eng):
            st, pe, ac = s["sf0_dve"], s["sf0_pe"], s["sf0_act"]
            with eng.Fori(0, NT) as i:
                for k in range(NS):
                    eng.wait_ge(pe.sem, pe.at(f"u{k}", i))
                    eng.wait_ge(ac.sem, ac.at(f"s{k}", i))
                    if k >= 3:
                        eng.wait_ge(pe.sem, pe.at(f"d{k - 3}", i))
                    eng.tensor_tensor(sf_h[k % 3], sf_sg[k % 2], bank(2 + k % 2), ALU.mult).then_inc(st.sem, 1)
                eng.wait_ge(pe.sem, pe.at(f"d{NS - 1}", i))
                eng.tensor_tensor(tile(x, i), tile(x, i), bank(6), ALU.add).then_inc(st.sem, 1)
            meet("dve", eng)

        NCH0 = E * CAP // T
        xin0 = work[:, 12544:12544 + E * CAP]
        xgT = work[:, 5120:5120 + E * CAP]
        ef_sg = [work[:, 7680 + k * CAP:7680 + (k + 1) * CAP] for k in range(2)]
        ef_h = [work[:, 7680 + (2 + k) * CAP:7680 + (3 + k) * CAP] for k in range(3)]
        xg0_loaded, yg0_stored = sem("xg0_loaded"), sem("yg0_stored")
        NB0 = HID0 // P
        NK0 = E * NB0
        outs0 = {}
        for c in range(NCH0):
            last = ((c + 1) * T - 1) // CAP
            outs0.setdefault(NB0 * last + NB0 + 2, []).append(c)
        pe_names = [f"in{c}" for c in range(NCH0)]
        for k in range(NK0 + 3):
            pe_names += ([f"g{k}", f"u{k}"] if k < NK0 else []) + ([f"d{k - 2}"] if 2 <= k < NK0 + 2 else [])
            pe_names += [f"out{c}" for c in outs0.get(k, [])]
        act_names = [f"in{c}" for c in range(NCH0)]
        dve_names = []
        for k in range(NK0 + 3):
            act_names += ([f"s{k}"] if k < NK0 else []) + [f"out{c}" for c in outs0.get(k, [])]
            dve_names += ([f"h{k}"] if k < NK0 else [])
            dve_names += [f"y{(k - 2) // NB0}"] if 2 <= k < NK0 + 2 and (k - 2) % NB0 == NB0 - 1 else []
        steps("ef0_pe", pe_names)
        steps("ef0_act", act_names)
        steps("ef0_dve", dve_names)

        def ef0_sync(eng):
            ac = s["ef0_act"]
            eng.wait_ge(scattered[0], 16 * NTOK * CH[0])
            for c in range(NCH0):
                eng.dma_start(chunk0_sb(xin0, c), chunk0(xg[0], c)).then_inc(xg0_loaded, 16)
            for c in range(NCH0):
                eng.wait_ge(ac.sem, ac.at(f"out{c}"))
                eng.dma_start(chunk0(yg[0], c), chunk0_sb(xin0, c)).then_inc(yg0_stored, 16)

        def ef0_pe(eng):
            st, ac, dv = s["ef0_pe"], s["ef0_act"], s["ef0_dve"]

            def turn_tiles(c, src):
                for n in range(4):
                    a = c * T + n * P
                    mm = eng.transpose(ps[:, 6 + c % 2, n * P:(n + 1) * P], src[:, a:a + P], ident)
                mm.then_inc(st.sem, 1)

            eng.wait_ge(xg0_loaded, 16 * NCH0)
            for c in range(NCH0):
                if c >= 2:
                    eng.wait_ge(ac.sem, ac.at(f"in{c - 2}"))
                turn_tiles(c, xin0)
            for k in range(NK0 + 3):
                if k < NK0:
                    e, j = divmod(k, NB0)
                    slot = xgT[:, e * CAP:(e + 1) * CAP]
                    if j == 0:
                        eng.wait_ge(ac.sem, ac.at(f"in{((e + 1) * CAP - 1) // T}"))
                    if k >= 2:
                        eng.wait_ge(dv.sem, dv.at(f"h{k - 2}"))
                    eng.matmul(ps[:, k % 2, 0:CAP], wa[:, k * P:(k + 1) * P], slot, start=True, stop=True)\
                       .then_inc(st.sem, 1)
                    eng.matmul(ps[:, 2 + k % 2, 0:CAP], wa[:, E * HID0 + k * P:E * HID0 + (k + 1) * P], slot,
                               start=True, stop=True).then_inc(st.sem, 1)
                if 2 <= k < NK0 + 2:
                    e, j = divmod(k - 2, NB0)
                    if j == 0 and e >= 2:
                        eng.wait_ge(dv.sem, dv.at(f"y{e - 2}"))
                    eng.wait_ge(dv.sem, dv.at(f"h{k - 2}"))
                    a = 2 * E * HID0 + (k - 2) * P
                    eng.matmul(ps[:, 4 + e % 2, 0:CAP], wa[:, a:a + P], ef_h[(k - 2) % 3],
                               start=(j == 0), stop=(j == NB0 - 1)).then_inc(st.sem, 1)
                for c in outs0.get(k, []):
                    eng.wait_ge(dv.sem, dv.at(f"y{((c + 1) * T - 1) // CAP}"))
                    eng.wait_ge(ac.sem, ac.at(f"out{c - 2}" if c >= 2 else f"in{NCH0 - 1}"))
                    turn_tiles(c, xgT)
            meet("pe", eng)

        def ef0_act(eng):
            st, pe, dv = s["ef0_act"], s["ef0_pe"], s["ef0_dve"]
            for c in range(NCH0):
                eng.wait_ge(pe.sem, pe.at(f"in{c}"))
                eng.activation(xgT[:, c * T:(c + 1) * T], bank(6 + c % 2), ACT.Copy).then_inc(st.sem, 1)
            for k in range(NK0 + 3):
                if k < NK0:
                    eng.wait_ge(pe.sem, pe.at(f"g{k}"))
                    if k >= 2:
                        eng.wait_ge(dv.sem, dv.at(f"h{k - 2}"))
                    eng.activation(ef_sg[k % 2], ps[:, k % 2, 0:CAP], ACT.Silu).then_inc(st.sem, 1)
                for c in outs0.get(k, []):
                    eng.wait_ge(pe.sem, pe.at(f"out{c}"))
                    eng.activation(xin0[:, c * T:(c + 1) * T], bank(6 + c % 2), ACT.Copy).then_inc(st.sem, 1)
            meet("act", eng)

        def ef0_dve(eng):
            st, pe, ac = s["ef0_dve"], s["ef0_pe"], s["ef0_act"]
            for k in range(NK0 + 3):
                if k < NK0:
                    eng.wait_ge(pe.sem, pe.at(f"u{k}"))
                    eng.wait_ge(ac.sem, ac.at(f"s{k}"))
                    if k >= 3:
                        eng.wait_ge(pe.sem, pe.at(f"d{k - 3}"))
                    eng.tensor_tensor(ef_h[k % 3], ef_sg[k % 2], ps[:, 2 + k % 2, 0:CAP], ALU.mult)\
                       .then_inc(st.sem, 1)
                if 2 <= k < NK0 + 2 and (k - 2) % NB0 == NB0 - 1:
                    e = (k - 2) // NB0
                    eng.wait_ge(pe.sem, pe.at(f"d{k - 2}"))
                    eng.tensor_copy(xgT[:, e * CAP:(e + 1) * CAP], ps[:, 4 + e % 2, 0:CAP]).then_inc(st.sem, 1)
            meet("dve", eng)

        TURNS = {2: NTILES[2] // 3, 3: NTILES[3] // 3}
        EW = {2: 2 * HID2 + P, 3: 3 * HID3}
        EBASE = {2: 0, 3: E * (2 * HID2 + P)}
        NBX = {2: HID2 // P, 3: HID3 // P}
        slot_mem = [work[:, 6144 + k * 1408:6144 + (k + 1) * 1408] for k in range(3)]
        x_w = [m[:, 0:512] for m in slot_mem]
        x_h = [m[:, 512:1024] for m in slot_mem]
        x_T = [m[:, 1024:1152] for m in slot_mem]
        x_sg = [m[:, 1024 + 128:1408] for m in slot_mem]
        x_in = [work[:, 18688 + k * P:18688 + (k + 1) * P] for k in range(3)]
        x_out = [work[:, 19072 + k * P:19072 + (k + 1) * P] for k in range(3)]
        x_b1 = [work[:, 11400 + k * 4:11404 + k * 4] for k in range(3)]
        T_BANK, Y_BANK = [0, 6, 7], [4, 5, 4]
        for L in (2, 3):
            steps(f"x{L}_pe", ["g0", "g1", "y0", "g2", "y1", "y2"], TURNS[L])
            steps(f"x{L}_turned", ["t0", "t1", "t2"], TURNS[L] + 1)
            steps(f"x{L}_act", ["a0", "a1", "a2"] if L == 3 else ["a0", "r1", "k1", "a1", "r2", "k2", "a2", "r3", "k3"],
                  TURNS[L])
            steps(f"x{L}_ready", ["r0", "r1", "r2"], TURNS[L] + 1)
            steps(f"x{L}_dve", ["h0", "h1", "y0", "h2", "y1", "y2"] if L == 3
                  else ["r1", "k1", "y0", "r2", "k2", "y1", "y2"], TURNS[L])
            for k in range(3):
                steps(f"x{L}_loaded{k}", ["l"])
                steps(f"x{L}_stored{k}", ["l"])

        assert TURNS[2] == B
        parts2_mem = work[:, 11500:13036].bitcast(BF16)

        def parts2(m, lo, hi, i):
            return parts2_mem[:, bass.ds(i % 2 * (6 * SEQ) + (3 * m + lo) * SEQ, (hi - lo) * SEQ)]

        left2 = work[:, 18432:18688]
        pd2 = {nm: nc.dram_tensor(f"parts2_{nm}", (n, P, N), BF16, kind="Internal").ap()
               for nm, n in (("r", 5), ("k", 3))}
        steps("parts2_out", ["l"])

        def part2(eng, n, m, i):
            seq = bass.ds(i * SEQ, SEQ)
            src = work[:, bass.ds(i * SEQ + 2048 * m, SEQ)] if m or n == 0 else left2
            return eng.activation(parts2(m, n, n + 1, i), src, ACT.Copy)

        def parts2_sync(eng, i):
            ac = s["x2_act"]
            eng.wait_ge(s["parts2_out"].sem, i * 48 + 49)
            eng.wait_ge(ac.sem, ac.at("k3", i))
            for nm, m, lo, hi in (("r", 0, 0, 3), ("r", 0, 3, 5), ("k", 1, 0, 3)):
                eng.dma_start(pd2[nm][lo:hi, :, bass.ds(i * SEQ, SEQ)].rearrange("n c t -> c n t"),
                              parts2(m, 0, hi - lo, i).rearrange("p (n t) -> p n t", t=SEQ))\
                   .then_inc(s["parts2_out"].sem, 16)

        def experts_of(eng, j):
            v = eng.value_load(etab[0:1, bass.ds(j, 1) if not isinstance(j, int) else slice(j, j + 1)],
                               min_val=0, max_val=E ** 3 - 1)
            return [v % E, v // E % E, v // (E * E)]

        def weights_at(L, e):
            return e * EW[L] + EBASE[L]

        def x_sync(L, eng):
            pe, tn, dv = s[f"x{L}_pe"], s[f"x{L}_turned"], s[f"x{L}_dve"]
            ld = [s[f"x{L}_loaded{k}"].sem for k in range(3)]
            sd = [s[f"x{L}_stored{k}"].sem for k in range(3)]

            def load(t, k):
                eng.dma_start(x_in[k], xg[L][bass.ds(t * P, P), :]).then_inc(ld[k], 16)

            def store(t, k):
                eng.dma_start(yg[L][bass.ds(t * P, P), :], x_out[k]).then_inc(sd[k], 16)

            eng.wait_ge(scattered[L], 16 * NTOK * CH[L])
            for k in range(3):
                load(k, k)
            for k in range(3):
                eng.wait_ge(tn.sem, tn.at(f"t{k}"))
                load(3 + k, k)
            with eng.Fori(0, TURNS[L] - 1) as i:
                for k in range(3):
                    eng.wait_ge(dv.sem, dv.at(f"y{k}", i))
                    store(i * 3 + k, k)
                    eng.wait_ge(tn.sem, tn.at(f"t{k}", i + 1))
                    load(i * 3 + 6 + k, k)
                if L == 2:
                    parts2_sync(eng, i)
            for k in range(3):
                eng.wait_ge(dv.sem, dv.at(f"y{k}", TURNS[L] - 1))
                store((TURNS[L] - 1) * 3 + k, k)
            if L == 2:
                parts2_sync(eng, TURNS[L] - 1)

        def x_pe(L, eng):
            st, tn, ac, rd, dv = [s[f"x{L}_{n}"] for n in ("pe", "turned", "act", "ready", "dve")]
            ld = [s[f"x{L}_loaded{k}"].sem for k in range(3)]
            nb = NBX[L]

            def turn(k, j):
                eng.wait_ge(ld[k], j * 16 + 17)
                eng.transpose(ps[:, T_BANK[k], 0:P], x_in[k], ident).then_inc(tn.sem, 1)

            def first(k, i):
                eng.wait_ge(rd.sem, rd.at(f"r{k}", i))
                for n in range(4):
                    mm = eng.matmul(ps[:, 1 + k, n * P:(n + 1) * P], x_w[k][:, n * P:(n + 1) * P], x_T[k],
                                    start=True, stop=True)
                mm.then_inc(st.sem, 1)

            def second(k, i, at):
                q, nm = (ac, f"a{k}") if L == 2 else (dv, f"h{k}")
                eng.wait_ge(ld_w23, 16)
                eng.wait_ge(q.sem, q.at(nm, i))
                eng.wait_ge(dv.sem, dv.at("y0", i) if k == 2 else i * dv.per + dv.base)
                for n in range(nb):
                    mm = eng.matmul(ps[:, Y_BANK[k], 0:P], x_h[k][:, n * P:(n + 1) * P],
                                    wa[:, bass.ds(at + 512 + n * P, P)], start=(n == 0), stop=(n == nb - 1))
                mm.then_inc(st.sem, 1)

            for k in range(3):
                turn(k, 0)
            with eng.Fori(0, TURNS[L]) as i:
                first(0, i)
                first(1, i)
                at = [weights_at(L, e) for e in experts_of(eng, i)]
                second(0, i, at[0])
                turn(0, i + 1)
                first(2, i)
                second(1, i, at[1])
                turn(1, i + 1)
                turn(2, i + 1)
                second(2, i, at[2])
            meet("pe", eng)

        def x_act(L, eng):
            st, pe, dv = s[f"x{L}_act"], s[f"x{L}_pe"], s[f"x{L}_dve"]
            eng.preload_act_table(ACT.Gelu if L == 2 else ACT.Silu)
            with eng.Fori(0, TURNS[L]) as i:
                for k in range(3):
                    eng.wait_ge(pe.sem, pe.at(f"g{k}", i))
                    if L == 2:
                        for n in range(4):
                            a = eng.activation(x_h[k][:, n * P:(n + 1) * P], ps[:, 1 + k, n * P:(n + 1) * P],
                                               ACT.Gelu, bias=x_b1[k][:, n:n + 1])
                    else:
                        a = eng.activation(x_sg[k], ps[:, 1 + k, 0:2 * P], ACT.Silu)
                    a.then_inc(st.sem, 1)
                    if L == 2:
                        if k == 0:
                            po = s["parts2_out"]
                            eng.wait_ge(po.sem, i * 48 + 1)
                        else:
                            eng.wait_ge(dv.sem, dv.at(f"k{k}", i))
                        for m in range(2):
                            part2(eng, k, m, i).then_inc(st.sem, 1)
            meet("act", eng)

        def x_dve(L, eng):
            st, pe, ac, tn, rd = [s[f"x{L}_{n}"] for n in ("dve", "pe", "act", "turned", "ready")]
            sd = [s[f"x{L}_stored{k}"].sem for k in range(3)]

            def fetch(k, j, e, last=None):
                eng.wait_ge(tn.sem, tn.at(f"t{k}", j))
                eng.tensor_copy(x_w[k], wa[:, bass.ds(weights_at(L, e), 512)])
                if L == 2:
                    b = COL_AT["b1_2"][0]
                    if last is not None:
                        eng.wait_ge(ac.sem, ac.at(f"a{k}", last))
                    eng.tensor_copy(x_b1[k], cols[:, bass.ds(e * 4 + b, 4)])
                eng.tensor_copy(x_T[k], ps[:, T_BANK[k], 0:P]).then_inc(rd.sem, 1)

            def less_part(n, i):
                eng.wait_ge(ac.sem, ac.at(f"k{n + 1}", i))
                r_, k_ = [work[:, bass.ds(i * SEQ + 2048 * m, SEQ)] for m in range(2)]
                eng.tensor_tensor(left2, r_ if n == 0 else left2, parts2(0, n, n + 1, i), ALU.subtract)\
                   .then_inc(st.sem, 1)
                eng.tensor_tensor(k_, k_, parts2(1, n, n + 1, i), ALU.subtract).then_inc(st.sem, 1)

            def hidden(k, i):
                eng.wait_ge(ac.sem, ac.at(f"a{k}", i))
                eng.tensor_tensor(x_h[k][:, 0:2 * P], x_sg[k], ps[:, 1 + k, 2 * P:4 * P], ALU.mult)\
                   .then_inc(st.sem, 1)

            def result(k, i, e):
                eng.wait_ge(sd[k], i * 16 + 1)
                eng.wait_ge(pe.sem, pe.at(f"y{k}", i))
                if L == 2:
                    eng.tensor_tensor(x_out[k], ps[:, Y_BANK[k], 0:P],
                                      wa[:, bass.ds(weights_at(L, e) + 2 * HID2, P)], ALU.add)\
                       .then_inc(st.sem, 1)
                else:
                    eng.tensor_copy(x_out[k], ps[:, Y_BANK[k], 0:P]).then_inc(st.sem, 1)

            eng.wait_ge(ld_w23, 16)
            for k, e in enumerate(experts_of(eng, 0)):
                fetch(k, 0, e)
            with eng.Fori(0, TURNS[L]) as i:
                here = experts_of(eng, i) if L == 2 else [None] * 3
                ahead = experts_of(eng, i + 1)
                if L == 3:
                    hidden(0, i)
                    hidden(1, i)
                else:
                    less_part(0, i)
                result(0, i, here[0])
                fetch(0, i + 1, ahead[0], i)
                if L == 2:
                    less_part(1, i)
                if L == 3:
                    hidden(2, i)
                result(1, i, here[1])
                fetch(1, i + 1, ahead[1], i)
                fetch(2, i + 1, ahead[2], i)
                result(2, i, here[2])
            meet("dve", eng)

        VP = 16 * 136
        q1, k1, v1 = [work[:, k * N:(k + 1) * N] for k in range(3)]
        y1 = q1
        PR = 9 * HD
        qpk = [wa[0:PR, k * 4096:k * 4096 + 2048].bitcast(BF16).rearrange("p (h t) -> p h t", h=H) for k in range(2)]
        kpk = [wa[0:PR, k * 4096 + 2048:(k + 1) * 4096].bitcast(BF16).rearrange("p (h t) -> p h t", h=H)
               for k in range(2)]
        vpad = [[work[:, 6144 + (2 * k + c) * VP:6144 + (2 * k + c + 1) * VP] for c in range(2)] for k in range(2)]
        o = 6144 + 4 * VP
        p0 = [work[:, o + k * 512:o + (k + 1) * 512] for k in range(2)]
        o += 1024
        p1 = [wa[:, 8192 + k * 1024:8192 + (k + 1) * 1024] for k in range(2)]
        pT = [wa[:, 10240 + k * 384:10240 + (k + 1) * 384] for k in range(3)]
        nmx = wa[:, 11392:11392 + 64]
        den1 = wa[:, 11456:11456 + 64]
        den_all = wa[:, 11520:11520 + 256]
        rden_all = wa[:, 11776:11776 + 256]
        rT = wa[0:16, 12032:12032 + 2048]
        rot = [work[:, o + k * P:o + (k + 1) * P] for k in range(2)]
        o += 2 * P
        parts1 = {}
        parts1["q"] = [work[:, 16384 + k * 1024:16384 + (k + 1) * 1024].bitcast(BF16) for k in range(3)]
        parts1["k"] = [wa[:, 12288 + k * 1024:12288 + (k + 1) * 1024].bitcast(BF16) for k in range(3)]
        pd1 = {nm: nc.dram_tensor(f"parts1_{nm}", (n, HD, H, N), BF16, kind="Internal").ap()
               for nm, n in (("q", 5), ("k", 3))}
        parts_out, v_zeroed = sem("parts_out"), sem("v_zeroed")
        packed1 = [f"c1_packed{a}" for a in range(2)]
        for nm in packed1:
            steps(nm, ["l"])
        assert o <= 19968

        steps("p1_pe", ["q", "k"], NT)
        steps("p1_pe_v", ["v"], NTOK // 4, "p1_pe")
        steps("p1_dve0", [f"{m}{w}" for m in "qk" for w in ("sin", "cos", "w", "bs", "b")])
        steps("p1_dve", ["q", "k", "qr", "kr", "qs", "ks"], NT, "p1_dve0")
        steps("p1_act", ["q1", "k1", "q2", "k2", "q3", "k3"], NT)
        steps("p1_act_v", ["v"], NT, "p1_act")

        def p1_pe(eng):
            st = s["p1_pe"]
            dz, dv = s["p1_dve0"], s["p1_dve"]
            eng.wait_ge(dz.sem, dz.at("kw"))
            with eng.Fori(0, NT) as i:
                eng.matmul(bank(i), mat("q1"), tile(xn, i), start=True, stop=True).then_inc(st.sem, 1)
                eng.matmul(bank(i + 4), mat("k1"), tile(xn, i), start=True, stop=True).then_inc(st.sem, 1)
            for i in range(NT):
                eng.wait_ge(dv.sem, dv.at("q", i))
                for t in range(4 * i, 4 * i + 4):
                    mm = eng.matmul(ps[:, i, (t % 4) * P:(t % 4 + 1) * P], xn[:, t * P:(t + 1) * P], mat("v1"),
                                    start=True, stop=True)
                mm.then_inc(s["p1_pe_v"].sem, 1)
            meet("pe", eng)

        def p1_act(eng):
            st, dv = s["p1_act"], s["p1_dve"]
            with eng.Fori(0, NT) as i:
                for n, src in enumerate(("", "r", "s")):
                    for m, t in (("q", q1), ("k", k1)):
                        eng.wait_ge(dv.sem, dv.at(m + src, i))
                        eng.activation(tile(parts1[m][n], i), tile(t, i), ACT.Copy).then_inc(st.sem, 1)
            pv = s["p1_pe_v"]
            for i in range(NT):
                eng.wait_ge(pv.sem, pv.at("v", i))
                eng.activation(v1[:, i * T:(i + 1) * T], bank(i), ACT.Copy).then_inc(st.sem, 1)
            meet("act", eng)

        def p1_dve(eng):
            st, dz = s["p1_dve"], s["p1_dve0"]
            pe, ac = s["p1_pe"], s["p1_act"]
            for n, m in enumerate("qk"):
                w, b, bs_ = mat(m + "1"), col("b" + m), col(f"b{m}s")
                eng.tensor_tensor(rot[n], mat(m + "s1"), tab(f"sin{m}_row"), ALU.mult).then_inc(dz.sem, 1)
                eng.tensor_tensor(w, w, tab(f"cos{m}_row"), ALU.mult).then_inc(dz.sem, 1)
                eng.wait_ge(dz.sem, dz.at(m + "cos"))
                eng.tensor_tensor(w, w, rot[n], ALU.add).then_inc(dz.sem, 1)
                eng.tensor_scalar(bs_, bs_, tab("sin" + m), None, ALU.mult).then_inc(dz.sem, 1)
                eng.wait_ge(dz.sem, dz.at(m + "bs"))
                eng.scalar_tensor_tensor(out=b, in0=b, scalar=tab("cos" + m), in1=bs_, op0=ALU.mult, op1=ALU.add)\
                   .then_inc(dz.sem, 1)
            eng.wait_ge(dz.sem, dz.at("kb"))
            with eng.Fori(0, NT) as i:
                for m, t, k in (("q", q1, 0), ("k", k1, 4)):
                    eng.wait_ge(pe.sem, pe.at(m, i))
                    eng.tensor_scalar(tile(t, i), bank(i + k), col("b" + m), None, ALU.add).then_inc(st.sem, 1)
                for n in (1, 2):
                    for m, t in (("q", q1), ("k", k1)):
                        eng.wait_ge(ac.sem, ac.at(f"{m}{n}", i))
                        eng.tensor_tensor(tile(t, i), tile(t, i), tile(parts1[m][n - 1], i), ALU.subtract)\
                           .then_inc(st.sem, 1)
            meet("dve", eng)

        def c1_sync(eng):
            ac, pe = s["p1_act"], s["c1_pe"]

            def out(m, n, at, i):
                eng.dma_start(pd1[m][at].rearrange("d h t -> h d t")[:, :, i * T:(i + 1) * T],
                              parts1[m][n][:, i * T:(i + 1) * T]).then_inc(parts_out, 16)

            def pack(b, a):
                for r in range(3):
                    rows = slice(r * 3 * HD, (r + 1) * 3 * HD)
                    eng.dma_start(qpk[a][rows], pd1["q"][r:r + 3, :, :, bass.ds(b * SEQ, SEQ)]
                                  .rearrange("j d h t -> (j d) h t")).then_inc(s[packed1[a]].sem, 16)
                    eng.dma_start(kpk[a][rows], pd1["k"][0:3, :, :, bass.ds(b * SEQ, SEQ)]
                                  .rearrange("j d h t -> (j d) h t")).then_inc(s[packed1[a]].sem, 16)

            for i in range(NT):
                for n in range(3):
                    for m in "qk":
                        eng.wait_ge(ac.sem, ac.at(f"{m}{n + 1}", i))
                        out(m, n, n, i)
                        if m == "q" and n < 2:
                            out(m, n, n + 3, i)
                if i == 0:
                    eng.wait_ge(parts_out, 16 * 8)
                    pack(0, 0)
                    pack(1, 1)
            eng.wait_ge(parts_out, 16 * 8 * NT)
            with eng.Fori(0, B // 2 - 1) as i:
                for a in range(2):
                    eng.wait_ge(pe.sem, pe.at(f"{a}S11", i))
                    pack(i * 2 + 2 + a, a)

        def dve_names(a):
            out = [f"{a}v0", f"{a}v1"]
            out += [f"{a}mx{n}" for n in range(3)]
            for u in range(4):
                for h in range(4 * u, 4 * u + 4):
                    out += [f"{a}c{h}"]
                    if u < 3 and h % 4 != 1:
                        out += [f"{a}mx{3 * (u + 1) + (0, None, 1, 2)[h % 4]}"]
            return out + [f"{a}den"]

        def pe_names1(a):
            out = [f"{a}S{n}" for n in range(3)]
            for h in range(H):
                if h < 12 and h % 4 != 1:
                    out += [f"{a}S{3 * (h // 4 + 1) + (0, None, 1, 2)[h % 4]}"]
                out += [f"{a}T{h}"]
                if h:
                    out += [f"{a}Y{h - 1}"]
            return out + [f"{a}Y{H - 1}"]

        def act_names1(a):
            out = []
            for u in range(4):
                out += [f"{a}e0_{h}" for h in range(4 * u, 4 * u + 4)] + [f"{a}e1_{h}" for h in range(4 * u, 4 * u + 4)]
            return out + [f"{a}y"]

        steps("c1_dve", dve_names(0) + dve_names(1), B // 2)
        steps("c1_pe", pe_names1(0) + pe_names1(1), B // 2)
        steps("c1_act", act_names1(0) + act_names1(1), B // 2)

        def c1_pe(eng):
            st, dv, ac = s["c1_pe"], s["c1_dve"], s["c1_act"]
            with eng.Fori(0, B // 2) as i:
                for a in range(2):
                    pk = s[packed1[a]].sem

                    def S(n):
                        u, w = n // 3, n % 3
                        bk = ps[:, n % 4, :]
                        if n == 0:
                            eng.wait_ge(pk, i * 96 + 97)
                        if n >= 4:
                            m = n - 4
                            hl = 4 * (m // 3) + (3 if m % 3 == 0 else 2 * (m % 3) - 1)
                            eng.wait_ge(ac.sem, ac.at(f"{a}e{0 if m % 3 == 0 else 1}_{hl}", i))
                        if w == 0:
                            eng.matmul(bk.rearrange("p (h k) -> p h k", h=4), identb,
                                       causalb.rearrange("p (o k) -> p o k", o=1).broadcast_to([P, 4, P]),
                                       start=True, stop=False, skip_group_check=True)
                            for h in range(4 * u, 4 * u + 4):
                                mm = eng.matmul(bk[:, (h % 4) * P:(h % 4 + 1) * P], qpk[a][:, h, 0:P],
                                                kpk[a][:, h, 0:P], start=False, stop=(h % 4 == 3),
                                                skip_group_check=True)
                        else:
                            h0 = 4 * u + 2 * (w - 1)
                            o2 = bk.rearrange("p (h k) -> p h k", h=2)
                            eng.matmul(o2[:, :, P:SEQ], identb,
                                       causalb.rearrange("p (o k) -> p o k", o=1).broadcast_to([P, 2, P]),
                                       start=True, stop=False, skip_group_check=True)
                            for h in (h0, h0 + 1):
                                mm = eng.matmul(o2[:, h - h0, :], qpk[a][:, h, P:SEQ], kpk[a][:, h, :],
                                                start=False, stop=(h > h0), skip_group_check=True)
                        mm.then_inc(st.sem, 1)

                    def tr(h):
                        u = h // 4
                        eng.wait_ge(ac.sem, ac.at(f"{a}e1_{h}", i))
                        if h >= 2:
                            eng.wait_ge(dv.sem, dv.at(f"{a}c{h - 2}", i))
                        pp0 = p0[u % 2][:, (h % 4) * P:(h % 4 + 1) * P]
                        pp1 = p1[u % 2][:, (h % 4) * SEQ:(h % 4 + 1) * SEQ]
                        bk = ps[:, 4 + h % 2, :]
                        eng.transpose(bk[:, 0:P], pp0, ident)
                        eng.transpose(bk[:, P:2 * P], pp1[:, 0:P], ident)
                        eng.transpose(bk[:, 2 * P:3 * P], pp1[:, P:SEQ], ident).then_inc(st.sem, 1)

                    def pv(h):
                        eng.wait_ge(dv.sem, dv.at(f"{a}c{h}", i))
                        if h == 0 and a == 0:
                            eng.wait_ge(ac.sem, i * ac.per + ac.base)
                        yy = ps[:, 6 + a, 0:SEQ]
                        eng.matmul(yy, vpad[a][0][:, h * P:(h + 1) * P], pT[h % 3][:, 0:SEQ],
                                   start=(h == 0), stop=False, skip_group_check=True)
                        eng.matmul(yy[:, P:SEQ], vpad[a][1][:, h * P:(h + 1) * P], pT[h % 3][:, SEQ:SEQ + P],
                                   start=False, stop=(h == H - 1), skip_group_check=True).then_inc(st.sem, 1)

                    for n in range(3):
                        S(n)
                    for h in range(H):
                        if h < 12 and h % 4 != 1:
                            S(3 * (h // 4 + 1) + (0, None, 1, 2)[h % 4])
                        tr(h)
                        if h:
                            pv(h - 1)
                    pv(H - 1)
            meet("pe", eng)

        def c1_act(eng):
            st, pe, dv = s["c1_act"], s["c1_pe"], s["c1_dve"]
            eng.preload_act_table(ACT.Exp)
            with eng.Fori(0, B // 2) as i:
                for a in range(2):
                    for u in range(4):
                        for h in range(4 * u, 4 * u + 4):
                            n = 3 * u
                            if h == 4 * u:
                                eng.wait_ge(dv.sem, dv.at(f"{a}mx{n}", i))
                                if u >= 2:
                                    eng.wait_ge(pe.sem, pe.at(f"{a}T{4 * u - 5}", i))
                            eng.activation(p0[u % 2][:, (h % 4) * P:(h % 4 + 1) * P],
                                           ps[:, n % 4, (h % 4) * P:(h % 4 + 1) * P], ACT.Exp,
                                           bias=nmx[:, 32 * a + h:32 * a + h + 1],
                                           accum_out=den1[:, 32 * a + h:32 * a + h + 1]).then_inc(st.sem, 1)
                        for h in range(4 * u, 4 * u + 4):
                            n = 3 * u + 1 + (h % 4) // 2
                            if h % 2 == 0:
                                eng.wait_ge(dv.sem, dv.at(f"{a}mx{n}", i))
                            eng.activation(p1[u % 2][:, (h % 4) * SEQ:(h % 4 + 1) * SEQ],
                                           ps[:, n % 4, (h % 2) * SEQ:(h % 2 + 1) * SEQ], ACT.Exp,
                                           bias=nmx[:, 32 * a + 16 + h:32 * a + 17 + h],
                                           accum_out=den1[:, 32 * a + 16 + h:32 * a + 17 + h]).then_inc(st.sem, 1)
                    eng.wait_ge(pe.sem, pe.at(f"{a}Y{H - 1}", i))
                    eng.activation(y1[:, bass.ds((i * 2 + a) * SEQ, SEQ)], ps[:, 6 + a, 0:SEQ], ACT.Copy)\
                       .then_inc(st.sem, 1)
            meet("act", eng)

        def c1_dve(eng):
            st, pe, ac = s["c1_dve"], s["c1_pe"], s["c1_act"]
            eng.wait_ge(v_zeroed, 4)
            with eng.Fori(0, B // 2) as i:
                for a in range(2):
                    b = i * 2 + a
                    for c in range(2):
                        eng.tensor_copy(vpad[a][c].rearrange("p (h c) -> p h c", c=136)[:, :, 0:HD],
                                        v1[:, bass.ds(b * SEQ + c * P, P)].rearrange("p (h c) -> p h c", c=HD))\
                           .then_inc(st.sem, 1)

                    def mx(n):
                        u, w = n // 3, n % 3
                        eng.wait_ge(pe.sem, pe.at(f"{a}S{n}", i))
                        if w == 0:
                            eng.tensor_reduce(nmx[:, 32 * a + 4 * u:32 * a + 4 * u + 4],
                                              ps[:, n % 4, :].rearrange("p (h k) -> p h k", h=4), AX_X, ALU.max,
                                              negate=True).then_inc(st.sem, 1)
                        else:
                            h0 = 32 * a + 16 + 4 * u + 2 * (w - 1)
                            eng.tensor_reduce(nmx[:, h0:h0 + 2], ps[:, n % 4, :].rearrange("p (h k) -> p h k", h=2),
                                              AX_X, ALU.max, negate=True).then_inc(st.sem, 1)

                    for n in range(3):
                        mx(n)
                    for h in range(H):
                        eng.wait_ge(pe.sem, pe.at(f"{a}T{h}", i))
                        if h >= 3:
                            eng.wait_ge(pe.sem, pe.at(f"{a}Y{h - 3}", i))
                        eng.tensor_copy(pT[h % 3], ps[:, 4 + h % 2, 0:3 * P]).then_inc(st.sem, 1)
                        if h < 12 and h % 4 != 1:
                            mx(3 * (h // 4 + 1) + (0, None, 1, 2)[h % 4])
                    eng.wait_ge(ac.sem, ac.at(f"{a}e1_{H - 1}", i))
                    eng.tensor_copy(den_all[:, bass.ds(b * 32, 32)], den1[:, 32 * a:32 * a + 32])\
                       .then_inc(st.sem, 1)
            meet("dve", eng)

        steps("o1_dve0", ["rden", "rT"])
        steps("o1_dve", ["y", "yb"], NT, "o1_dve0")
        steps("o1_dve2", ["x"], NT, "o1_dve")
        steps("o1_pe0", ["rT"])
        steps("o1_pe", ["bc"], NT, "o1_pe0")
        steps("o1_pe2", ["o"], NT, "o1_pe")

        def o1_pe(eng):
            dz = s["o1_dve0"]
            eng.wait_ge(dz.sem, dz.at("rden"))
            for t in range(NTOK):
                mm = eng.transpose(ps[0:16, 4 + t // 4, (t % 4) * P:(t % 4 + 1) * P],
                                   rden_all[:, t * H:(t + 1) * H], ident)
            mm.then_inc(s["o1_pe0"].sem, 1)
            eng.wait_ge(dz.sem, dz.at("rT"))
            with eng.Fori(0, NT) as i:
                eng.matmul(bank(i), tab("sel16", 16), tile(rT, i), start=True, stop=True)\
                   .then_inc(s["o1_pe"].sem, 1)
            with eng.Fori(0, NT) as i:
                q = s["o1_dve"]
                eng.wait_ge(q.sem, q.at("yb", i))
                eng.matmul(bank(i + 4), mat("p1"), tile(y1, i), start=True, stop=True)\
                   .then_inc(s["o1_pe2"].sem, 1)
            meet("pe", eng)

        def o1_dve(eng):
            dz = s["o1_dve0"]
            eng.reciprocal(rden_all, den_all).then_inc(dz.sem, 1)
            q = s["o1_pe0"]
            eng.wait_ge(q.sem, q.at("rT"))
            eng.tensor_copy(rT, ps[0:16, 4:8, :].rearrange("p a t -> p (a t)")).then_inc(dz.sem, 1)
            st = s["o1_dve"]
            with eng.Fori(0, NT) as i:
                q = s["o1_pe"]
                eng.wait_ge(q.sem, q.at("bc", i))
                eng.tensor_tensor(tile(y1, i), tile(y1, i), bank(i), ALU.mult).then_inc(st.sem, 1)
                eng.wait_ge(st.sem, st.at("y", i))
                eng.tensor_scalar(tile(y1, i), tile(y1, i), col("bv"), None, ALU.add).then_inc(st.sem, 1)
            with eng.Fori(0, NT) as i:
                q = s["o1_pe2"]
                eng.wait_ge(q.sem, q.at("o", i))
                eng.scalar_tensor_tensor(out=tile(x, i), in0=bank(i + 4), scalar=col("bp"), in1=tile(x, i),
                                         op0=ALU.add, op1=ALU.add).then_inc(s["o1_dve2"].sem, 1)
            meet("dve", eng)

        ha = [work[:, k * N:(k + 1) * N] for k in range(4)]
        hb = [work[:, (4 + k) * N:(5 + k) * N] for k in range(4)]
        tern = {}
        at = 0
        for nm, n in (("w1", 512), ("w2", 512), ("h1", 2048), ("h2", 2048), ("w3", 512)):
            tern[nm] = wb[:, at:at + n]
            at += n
        sgl = [work[:, 16384 + k * T:16384 + (k + 1) * T] for k in range(2)]
        steps("g1_pe_a", [f"{w}{j}" for j in range(4) for w in "gu"], NT)
        steps("g1_pe_b", [f"o{j}" for j in range(4)], NT, "g1_pe_a")
        steps("g1_pe_c", [f"o{j}" for j in range(4)], NT, "g1_pe_b")
        steps("g1_pe_d", ["y"], NT, "g1_pe_c")
        steps("g1_act_a", [f"s{j}" for j in range(4)], NT)
        steps("g1_act_b", [f"h{j}" for j in range(4)], NT, "g1_act_a")
        steps("g1_act_c", [f"h{j}" for j in range(4)], NT, "g1_act_b")
        steps("g1_dve_a", [f"h{j}" for j in range(4)], NT)
        steps("g1_dve_d", ["x"], NT, "g1_dve_a")

        def g1_pe(eng):
            st, dv = s["g1_pe_a"], s["g1_dve_a"]
            eng.wait_ge(ld_w1, 16)
            with eng.Fori(0, NT) as i:
                for j in range(4):
                    if j >= 2:
                        eng.wait_ge(dv.sem, dv.at(f"h{j - 2}", i))
                    else:
                        eng.wait_ge(dv.sem, i * dv.per + dv.base)
                    eng.matmul(bank(j % 2), tern["w1"][:, j * P:(j + 1) * P], tile(xn, i), start=True, stop=True)\
                       .then_inc(st.sem, 1)
                    eng.matmul(bank(2 + j % 2), tern["w2"][:, j * P:(j + 1) * P], tile(xn, i), start=True, stop=True)\
                       .then_inc(st.sem, 1)
            for nm, src, key, akey in (("h1", ha, "g1_pe_b", "g1_act_b"), ("h2", hb, "g1_pe_c", "g1_act_c")):
                st, ac = s[key], s[akey]
                with eng.Fori(0, NT) as i:
                    if nm == "h1":
                        eng.wait_ge(dv.sem, dv.turn_end(i))
                    else:
                        pa = s["g1_act_b"]
                        eng.wait_ge(pa.sem, pa.turn_end(i))
                    for o in range(4):
                        eng.wait_ge(ac.sem, i * ac.per + (ac.base - ac.per + o + 1))
                        for k in range(4):
                            mm = eng.matmul(bank(4 + o), tern[nm][:, k * 512 + o * P:k * 512 + (o + 1) * P],
                                            tile(src[k], i), start=(k == 0), stop=(k == 3))
                        mm.then_inc(st.sem, 1)
            st, ac, dv = s["g1_pe_d"], s["g1_act_c"], s["g1_dve_d"]
            with eng.Fori(0, NT) as i:
                eng.wait_ge(ac.sem, ac.turn_end(i))
                for k in range(4):
                    mm = eng.matmul(bank(i), tern["w3"][:, k * P:(k + 1) * P], tile(ha[k], i),
                                    start=(k == 0), stop=(k == 3))
                mm.then_inc(st.sem, 1)
            meet("pe", eng)

        def g1_act(eng):
            st, pe, dv = s["g1_act_a"], s["g1_pe_a"], s["g1_dve_a"]
            eng.preload_act_table(ACT.Silu)
            with eng.Fori(0, NT) as i:
                for j in range(4):
                    eng.wait_ge(pe.sem, pe.at(f"g{j}", i))
                    if j >= 2:
                        eng.wait_ge(dv.sem, dv.at(f"h{j - 2}", i))
                    else:
                        eng.wait_ge(dv.sem, i * dv.per + dv.base)
                    eng.activation(sgl[j % 2], bank(j % 2), ACT.Silu, scale=col("w1_s", j)).then_inc(st.sem, 1)
            eng.preload_act_table(ACT.Gelu)
            for key, pkey, dst, sc in (("g1_act_b", "g1_pe_b", hb, "h1_s"), ("g1_act_c", "g1_pe_c", ha, "h2_s")):
                st, pe = s[key], s[pkey]
                with eng.Fori(0, NT) as i:
                    for o in range(4):
                        eng.wait_ge(pe.sem, pe.at(f"o{o}", i))
                        eng.activation(tile(dst[o], i), bank(4 + o), ACT.Gelu, scale=col(sc, o)).then_inc(st.sem, 1)
            meet("act", eng)

        def g1_dve(eng):
            st, pe, ac = s["g1_dve_a"], s["g1_pe_a"], s["g1_act_a"]
            with eng.Fori(0, NT) as i:
                for j in range(4):
                    eng.wait_ge(pe.sem, pe.at(f"u{j}", i))
                    eng.wait_ge(ac.sem, ac.at(f"s{j}", i))
                    eng.scalar_tensor_tensor(out=tile(ha[j], i), in0=bank(2 + j % 2), scalar=col("w2_s", j),
                                             in1=sgl[j % 2], op0=ALU.mult, op1=ALU.mult).then_inc(st.sem, 1)
            st, pe = s["g1_dve_d"], s["g1_pe_d"]
            with eng.Fori(0, NT) as i:
                eng.wait_ge(pe.sem, pe.at("y", i))
                eng.scalar_tensor_tensor(out=tile(x, i), in0=bank(i), scalar=col("w3_s"), in1=tile(x, i),
                                         op0=ALU.mult, op1=ALU.add).then_inc(st.sem, 1)
            meet("dve", eng)

        r2, k2, v2 = [work[:, k * N:(k + 1) * N] for k in range(3)]
        pk2 = [mem[0:PR, :].bitcast(BF16).rearrange("p (m h t) -> p m h t", m=2, h=H)
               for mem in (work[:, 6144:10240], wa[:, 2048:6144])]
        vp2 = [work[:, 10240 + c * VP:10240 + (c + 1) * VP] for c in range(2)]
        decay = work[:, 14592:14592 + 2048]
        aT = [work[:, 16896 + k * 512:16896 + (k + 1) * 512] for k in range(3)]
        kw = wb[:, 0:1024]
        s0 = wb[:, 1024:2048]
        wkt = wb[:, 2048:2064]
        wbt = wb[:, 2064:2192]
        lam = wb[:, 2192:2192 + 16]
        lamc = wb[:, 2208:2209]
        expo = wb[:, 2216:2232]
        g2 = wb[:, 2304:4352]
        steps("t2_act0", ["lam", "lamc", "wk", "wb"] + [f"d{h}" for h in range(H)])
        steps("t2_dve0", ["lamm", "lamcm", "ex"])
        steps("t2_dve1", [f"{w}{h}" for i in range(NT) for w in "mu" for h in range(4 * i, 4 * i + 4)])
        mix = {"r": work[:, 6144:8192], "k": work[:, 8192:10240], "v": work[:, 10240:12288],
               "g": work[:, 12288:14336]}
        xxs = g2
        steps("p2_dve", ["xx", "xx0", "xr", "xk", "xg", "xv"], 1, "t2_dve0")
        steps("p2_dve1", ["r", "k"], NT, "p2_dve")
        steps("p2_dve3", ["kw0", "kw1", "s00", "s01"], 1, "p2_dve1")
        steps("p2_act", ["g"], NT, "t2_act0")
        steps("p2_act_v", ["v"], NT, "p2_act")
        steps("p2_pe", ["r", "k", "g"], NT)
        steps("p2_pe_v", ["v"], NT, "p2_pe")
        steps("p2_pe_k", ["k0", "k1", "s0"], 1, "p2_pe_v")

        def t2_act(eng):
            st, dv = s["t2_act0"], s["t2_dve0"]
            eng.activation(lam, colv("td_bc"), ACT.Exp).then_inc(st.sem, 1)
            eng.activation(lamc, col("td_ch"), ACT.Exp).then_inc(st.sem, 1)
            eng.wait_ge(dv.sem, dv.at("ex"))
            eng.activation(wkt, expo, ACT.Exp).then_inc(st.sem, 1)
            eng.activation(wbt, tab("iota_q"), ACT.Exp, scale=lamc).then_inc(st.sem, 1)
            for h in range(H):
                eng.activation(decay[:, h * P:(h + 1) * P], tab("lag"), ACT.Exp, scale=lam[:, h:h + 1])\
                   .then_inc(st.sem, 1)

        def t2_dve(eng):
            st, ac = s["t2_dve0"], s["t2_act0"]
            eng.wait_ge(ac.sem, ac.at("lamc"))
            eng.tensor_scalar(lam, lam, 1e30, -1.0, ALU.min, ALU.mult).then_inc(st.sem, 1)
            eng.tensor_scalar(lamc, lamc, 1e30, -1.0, ALU.min, ALU.mult).then_inc(st.sem, 1)
            eng.wait_ge(st.sem, st.at("lamm"))
            eng.tensor_scalar(expo, lam, tab("rev_j"), None, ALU.mult).then_inc(st.sem, 1)
            eng.wait_ge(st.sem, st.at("ex"))

        def decays_dve(i, eng):
            st, ac = s["t2_dve1"], s["t2_act0"]
            for h in range(4 * i, 4 * i + 4):
                dh = decay[:, h * P:(h + 1) * P]
                eng.wait_ge(ac.sem, ac.at(f"d{h}"))
                eng.tensor_tensor(dh, dh, tab("before"), ALU.mult).then_inc(st.sem, 1)
            for h in range(4 * i, 4 * i + 4):
                dh = decay[:, h * P:(h + 1) * P]
                eng.wait_ge(st.sem, st.at(f"m{h}"))
                eng.scalar_tensor_tensor(out=dh, in0=ident, scalar=col("u_bc", h), in1=dh, op0=ALU.mult, op1=ALU.add)\
                   .then_inc(st.sem, 1)

        def p2_pe(eng):
            st, dv = s["p2_pe"], s["p2_dve"]
            d1, ac = s["p2_dve1"], s["p2_act"]
            eng.wait_ge(dv.sem, dv.at("xg"))
            with eng.Fori(0, NT) as i:
                eng.wait_ge(d1.sem, i * d1.per + d1.base)
                eng.matmul(bank(0), mat("r2"), tile(mix["r"], i), start=True, stop=True).then_inc(st.sem, 1)
                eng.matmul(bank(1), mat("k2"), tile(mix["k"], i), start=True, stop=True).then_inc(st.sem, 1)
                eng.wait_ge(ac.sem, i * ac.per + ac.base)
                eng.matmul(bank(2), mat("g2"), tile(mix["g"], i), start=True, stop=True).then_inc(st.sem, 1)
            sv = s["p2_pe_v"]
            eng.wait_ge(dv.sem, dv.at("xv"))
            for t in range(NTOK):
                mm = eng.matmul(ps[:, 4 + t // 4, (t % 4) * P:(t % 4 + 1) * P], mix["v"][:, t * P:(t + 1) * P],
                                mat("v2"), start=True, stop=True)
                if t % 4 == 3:
                    mm.then_inc(sv.sem, 1)
            sk = s["p2_pe_k"]
            eng.wait_ge(d1.sem, d1.end)
            for b in range(B):
                mm = eng.matmul(ps[:, b // 4, (b % 4) * P:(b % 4 + 1) * P], mix["k"][:, b * SEQ:b * SEQ + P],
                                mat("k2"), start=True, stop=True)
                if b % 4 == 3:
                    mm.then_inc(sk.sem, 1)
            d3 = s["p2_dve3"]
            eng.wait_ge(ac.sem, s["p2_act_v"].end)
            eng.wait_ge(d3.sem, d3.at("kw1"))
            for b in range(B):
                mm = eng.matmul(ps[:, 2 + b // 4, (b % 4) * P:(b % 4 + 1) * P], kw[:, b * P:(b + 1) * P],
                                v2[:, b * SEQ:b * SEQ + P], start=True, stop=True)
            mm.then_inc(sk.sem, 1)
            meet("pe", eng)

        def p2_act(eng):
            eng.preload_act_table(ACT.Silu)
            st, pe = s["p2_act"], s["p2_pe"]
            dv = s["p2_dve"]
            eng.wait_ge(dv.sem, dv.at("xv"))
            with eng.Fori(0, NT) as i:
                eng.wait_ge(pe.sem, pe.at("g", i))
                eng.activation(tile(g2, i), bank(2), ACT.Silu).then_inc(st.sem, 1)
            pv = s["p2_pe_v"]
            for i in range(NT):
                eng.wait_ge(pv.sem, pv.at("v", i))
                eng.activation(v2[:, i * T:(i + 1) * T], bank(4 + i), ACT.Copy).then_inc(st.sem, 1)
            meet("act", eng)

        def p2_dve(eng):
            st = s["p2_dve"]
            x3 = xn[:, :].rearrange("p (b t) -> p b t", t=SEQ)
            d3 = xxs.rearrange("p (b t) -> p b t", t=SEQ)
            eng.tensor_tensor(d3[:, :, 1:SEQ], x3[:, :, 0:SEQ - 1], x3[:, :, 1:SEQ], ALU.subtract)\
               .then_inc(st.sem, 1)
            eng.tensor_scalar(d3[:, :, 0:1], x3[:, :, 0:1], -1.0, None, ALU.mult).then_inc(st.sem, 1)
            eng.wait_ge(st.sem, st.at("xx0"))
            for k in "rkgv":
                eng.scalar_tensor_tensor(out=mix[k], in0=xxs, scalar=col("maa_" + k), in1=xn[:, :],
                                         op0=ALU.mult, op1=ALU.add).then_inc(st.sem, 1)
            pe, d1 = s["p2_pe"], s["p2_dve1"]
            for i in range(NT):
                eng.wait_ge(pe.sem, pe.at("r", i))
                eng.tensor_copy(tile(r2, i), bank(0)).then_inc(d1.sem, 1)
                eng.wait_ge(pe.sem, pe.at("k", i))
                eng.tensor_copy(tile(k2, i), bank(1)).then_inc(d1.sem, 1)
                decays_dve(i, eng)
            pk, d3s = s["p2_pe_k"], s["p2_dve3"]
            wk = wkt.rearrange("p (o c h) -> p o c h", o=1, c=1).broadcast_to([P, 4, HD, H])
            for n in range(2):
                eng.wait_ge(pk.sem, pk.at(f"k{n}"))
                eng.tensor_tensor(kw[:, n * T:(n + 1) * T].rearrange("p (b c h) -> p b c h", h=H, c=HD),
                                  bank(n).rearrange("p (b c h) -> p b c h", h=H, c=HD), wk, ALU.mult)\
                   .then_inc(d3s.sem, 1)
            eng.wait_ge(pk.sem, pk.at("s0"))
            same = tab("grp").rearrange("p (o c) -> p o c", o=1).broadcast_to([P, 4, P])
            for n in range(2):
                eng.scalar_tensor_tensor(out=s0[:, n * T:(n + 1) * T].rearrange("p (b c) -> p b c", c=P),
                                         in0=bank(2 + n).rearrange("p (b c) -> p b c", c=P), scalar=float(HD),
                                         in1=same, op0=ALU.mult, op1=ALU.mult).then_inc(d3s.sem, 1)
            eng.wait_ge(s["t2_dve1"].sem, s["t2_dve1"].end)
            meet("dve", eng)

        steps("c2_dve0", ["z0", "z1"])
        steps("c2_dve", [f"{a}{n}" for a in range(2) for n in
              ["v0"] + [f"a{n}" for n in range(4)] + ["v1"] + [f"a{n}" for n in range(4, 8)]], B // 2, "c2_dve0")
        steps("c2_act", ["0y", "1y"], B // 2)
        steps("c2_pe", [f"{a}{n}" for a in range(2) for n in [f"S{n}" for n in range(3)] + [x_ for n in range(8)
              for x_ in ([f"S{n + 3}"] if n + 3 < 8 else []) + [f"Y{n}"]]], B // 2)
        for a in range(2):
            steps(f"c2_packed{a}", ["l"])

        def c2_sync(eng):
            pe = s["c2_pe"]

            def pack(b, a):
                for r in range(3):
                    rows = slice(r * 3 * HD, (r + 1) * 3 * HD)
                    for m, src in enumerate((pd2["r"][r:r + 3], pd2["k"][0:3])):
                        eng.dma_start(pk2[a][rows, m], src[:, :, bass.ds(b * SEQ, SEQ)]
                                      .rearrange("j (d h) t -> (j d) h t", h=H)).then_inc(s[f"c2_packed{a}"].sem, 16)

            for n in met:
                eng.wait_ge(met[n], PHASES.index("x2") + 2)
            eng.wait_ge(s["parts2_out"].sem, 48 * B + 49)
            pack(0, 0)
            pack(1, 1)
            with eng.Fori(0, B // 2 - 1) as i:
                for a in range(2):
                    eng.wait_ge(pe.sem, pe.at(f"{a}S7", i))
                    pack(i * 2 + 2 + a, a)

        def c2_pe(eng):
            st, dv, ac = s["c2_pe"], s["c2_dve"], s["c2_act"]
            with eng.Fori(0, B // 2) as i:
                def S(a, n):
                    c, u = n // 4, n % 4
                    if n == 0:
                        eng.wait_ge(s[f"c2_packed{a}"].sem, i * 96 + 97)
                    if n >= 4:
                        eng.wait_ge(dv.sem, dv.at(f"{a}a{n - 4}", i))
                    elif a == 1:
                        eng.wait_ge(dv.sem, dv.at(f"0a{n + 4}", i))
                    else:
                        eng.wait_ge(dv.sem, i * dv.per + dv.base)
                    for h in range(4 * u, 4 * u + 4):
                        mm = eng.matmul(ps[:, n % 4, (h % 4) * P:(h % 4 + 1) * P],
                                        pk2[a][:, 1, h, c * P:(c + 1) * P], pk2[a][:, 0, h, c * P:(c + 1) * P],
                                        start=(h % 4 == 0), stop=(h % 4 == 3), skip_group_check=True)
                    mm.then_inc(st.sem, 1)

                def Y(a, n):
                    c, u = n // 4, n % 4
                    if n == 0:
                        eng.wait_ge(ac.sem, i * ac.per + ac.base)
                    eng.wait_ge(dv.sem, dv.at(f"{a}a{n}", i))
                    for h in range(4 * u, 4 * u + 4):
                        mm = eng.matmul(ps[:, 4 + a, c * P:(c + 1) * P], vp2[c][:, h * P:(h + 1) * P],
                                        aT[n % 3][:, (h % 4) * P:(h % 4 + 1) * P],
                                        start=(h == 0), stop=(h == H - 1), skip_group_check=True)
                    mm.then_inc(st.sem, 1)

                for a in range(2):
                    for n in range(3):
                        S(a, n)
                    for n in range(8):
                        if n + 3 < 8:
                            S(a, n + 3)
                        Y(a, n)
            meet("pe", eng)

        def c2_act(eng):
            st, pe = s["c2_act"], s["c2_pe"]
            with eng.Fori(0, B // 2) as i:
                for a in range(2):
                    eng.wait_ge(pe.sem, pe.at(f"{a}Y7", i))
                    eng.activation(y2q[:, bass.ds((i * 2 + a) * SEQ, SEQ)], ps[:, 4 + a, 0:SEQ], ACT.Copy)\
                       .then_inc(st.sem, 1)
            meet("act", eng)

        def c2_dve(eng):
            z, st, pe = s["c2_dve0"], s["c2_dve"], s["c2_pe"]
            eng.wait_ge(s["parts2_out"].sem, 48 * B + 49)
            for c in range(2):
                eng.memset(vp2[c], 0.0).then_inc(z.sem, 1)
            eng.wait_ge(z.sem, z.end)
            with eng.Fori(0, B // 2) as i:
                for a in range(2):
                    for n in range(8):
                        c, u = n // 4, n % 4
                        if u == 0:
                            if a:
                                eng.wait_ge(pe.sem, pe.at(f"0Y{n + 3}", i))
                            else:
                                eng.wait_ge(pe.sem, i * pe.per + pe.base)
                            eng.tensor_copy(vp2[c][:, 0:H * 129].rearrange("p (h c) -> p h c", c=129)[:, :, 0:P:H],
                                            v2[:, bass.ds((i * 2 + a) * SEQ + c * P, P)]
                                            .rearrange("p (c h) -> p h c", h=H)).then_inc(st.sem, 1)
                        eng.wait_ge(pe.sem, pe.at(f"{a}S{n}", i))
                        if n >= 3:
                            eng.wait_ge(pe.sem, pe.at(f"{a}Y{n - 3}", i))
                        elif a:
                            eng.wait_ge(pe.sem, pe.at(f"0Y{[6, 7, 7][n]}", i))
                        eng.tensor_tensor(aT[n % 3], ps[:, n % 4, :], decay[:, u * 4 * P:(u + 1) * 4 * P], ALU.mult)\
                           .then_inc(st.sem, 1)
            meet("dve", eng)

        y2q = k2
        gn = {"c": work[:, 6144:8192], "q": work[:, 8192:10240], "r": work[:, 10240:12288]}
        rwb = work[:, 12288:13312]
        steps("o2_dve0", ["rw", "x0", "x1"])
        steps("o2_dve1", ["c"], NT, "o2_dve0")
        steps("o2_dve2", ["n", "b", "g"], NT, "o2_dve1")
        steps("o2_dve3", ["x"], NT, "o2_dve2")
        steps("o2_act1", ["sq"], NT)
        steps("o2_act2", ["log"], NT, "o2_act1")
        steps("o2_act3", ["rstd"], NT, "o2_act2")
        steps("o2_pe0", ["x"])
        steps("o2_pe1", ["mean"], NT, "o2_pe0")
        steps("o2_pe2", ["var"], NT, "o2_pe1")
        steps("o2_pe3", ["o"], NT, "o2_pe2")

        def o2_pe(eng):
            dz = s["o2_dve0"]
            eng.wait_ge(dz.sem, dz.at("rw"))
            for b in range(B):
                mm = eng.matmul(ps[:, b // 4, (b % 4) * P:(b % 4 + 1) * P], s0[:, b * P:(b + 1) * P],
                                rwb[:, b * P:(b + 1) * P], start=True, stop=True)
            mm.then_inc(s["o2_pe0"].sem, 1)
            eng.wait_ge(dz.sem, dz.at("x1"))
            with eng.Fori(0, NT) as i:
                eng.matmul(bank(i), tab("grp"), tile(y2q, i), start=True, stop=True).then_inc(s["o2_pe1"].sem, 1)
            with eng.Fori(0, NT) as i:
                q = s["o2_act1"]
                eng.wait_ge(q.sem, q.at("sq", i))
                eng.matmul(bank(i + 4), tab("grp"), tile(gn["q"], i), start=True, stop=True)\
                   .then_inc(s["o2_pe2"].sem, 1)
            with eng.Fori(0, NT) as i:
                q = s["o2_dve2"]
                eng.wait_ge(q.sem, q.at("g", i))
                eng.matmul(bank(i), mat("o2"), tile(gn["c"], i), start=True, stop=True).then_inc(s["o2_pe3"].sem, 1)
            meet("pe", eng)

        def o2_act(eng):
            eng.preload_act_table(ACT.Ln)
            with eng.Fori(0, NT) as i:
                q = s["o2_dve1"]
                eng.wait_ge(q.sem, q.at("c", i))
                eng.activation(tile(gn["q"], i), tile(gn["c"], i), ACT.Square).then_inc(s["o2_act1"].sem, 1)
            with eng.Fori(0, NT) as i:
                q = s["o2_pe2"]
                eng.wait_ge(q.sem, q.at("var", i))
                eng.activation(tile(gn["r"], i), bank(i + 4), ACT.Ln, bias=eps_ap(EPS_GN), scale=DOWN)\
                   .then_inc(s["o2_act2"].sem, 1)
            eng.preload_act_table(ACT.Exp)
            with eng.Fori(0, NT) as i:
                q = s["o2_act2"]
                eng.wait_ge(q.sem, q.at("log", i))
                eng.activation(tile(gn["r"], i), tile(gn["r"], i), ACT.Exp, bias=epst[:, 4:5], scale=-0.5)\
                   .then_inc(s["o2_act3"].sem, 1)
            meet("act", eng)

        def o2_dve(eng):
            st = s["o2_dve0"]
            r3 = r2.rearrange("p (b t) -> p b t", t=SEQ)
            y3 = y2q.rearrange("p (b t) -> p b t", t=SEQ)
            eng.tensor_tensor(rwb.rearrange("p (b q) -> p b q", q=P), r3[:, :, P:SEQ],
                              wbt.rearrange("p (o q) -> p o q", o=1).broadcast_to([P, B, P]), ALU.mult)\
               .then_inc(st.sem, 1)
            q = s["o2_pe0"]
            eng.wait_ge(q.sem, q.at("x"))
            for n in range(2):
                yy = y3[:, 4 * n:4 * n + 4, P:SEQ]
                eng.tensor_tensor(yy, yy, bank(n).rearrange("p (b q) -> p b q", q=P), ALU.add).then_inc(st.sem, 1)
            with eng.Fori(0, NT) as i:
                q = s["o2_pe1"]
                eng.wait_ge(q.sem, q.at("mean", i))
                eng.tensor_tensor(tile(gn["c"], i), tile(y2q, i), bank(i), ALU.subtract)\
                   .then_inc(s["o2_dve1"].sem, 1)
            st = s["o2_dve2"]
            with eng.Fori(0, NT) as i:
                q = s["o2_act3"]
                eng.wait_ge(q.sem, q.at("rstd", i))
                eng.scalar_tensor_tensor(out=tile(gn["c"], i), in0=tile(gn["c"], i), scalar=col("ln_g"),
                                         in1=tile(gn["r"], i), op0=ALU.mult, op1=ALU.mult).then_inc(st.sem, 1)
                eng.wait_ge(st.sem, st.at("n", i))
                eng.tensor_scalar(tile(gn["c"], i), tile(gn["c"], i), col("ln_b"), None, ALU.add)\
                   .then_inc(st.sem, 1)
                eng.wait_ge(st.sem, st.at("b", i))
                eng.tensor_tensor(tile(gn["c"], i), tile(gn["c"], i), tile(g2, i), ALU.mult).then_inc(st.sem, 1)
            with eng.Fori(0, NT) as i:
                q = s["o2_pe3"]
                eng.wait_ge(q.sem, q.at("o", i))
                eng.tensor_tensor(tile(x, i), tile(x, i), bank(i), ALU.add).then_inc(s["o2_dve3"].sem, 1)
            meet("dve", eng)

        q3, k3, v3 = [work[:, k * N:(k + 1) * N] for k in range(3)]
        SC3 = 1.0 / float(P) ** 0.5
        steps("p3_pe", ["q", "k"], NT)
        steps("p3_pe_v", ["v"], NT, "p3_pe")
        steps("p3_dve", ["q", "k"], NT)
        steps("p3_dve_v", ["v"], NT, "p3_dve")

        def p3_pe(eng):
            st, dv = s["p3_pe"], s["p3_dve"]
            with eng.Fori(0, NT) as i:
                eng.wait_ge(dv.sem, i * dv.per + dv.base)
                eng.matmul(bank(0), mat("q3"), tile(xn, i), start=True, stop=True).then_inc(st.sem, 1)
                eng.matmul(bank(1), mat("k3"), tile(xn, i), start=True, stop=True).then_inc(st.sem, 1)
            for t in range(NTOK):
                mm = eng.matmul(ps[:, 4 + t // 4, (t % 4) * P:(t % 4 + 1) * P], xn[:, t * P:(t + 1) * P], mat("v3"),
                                start=True, stop=True)
                if t % 4 == 3:
                    mm.then_inc(s["p3_pe_v"].sem, 1)
            meet("pe", eng)

        def p3_dve(eng):
            st, pe = s["p3_dve"], s["p3_pe"]
            with eng.Fori(0, NT) as i:
                for nm, dst, k in (("q", q3, 0), ("k", k3, 1)):
                    eng.wait_ge(pe.sem, pe.at(nm, i))
                    eng.tensor_copy(tile(dst, i), bank(k)).then_inc(st.sem, 1)
            for i in range(NT):
                q = s["p3_pe_v"]
                eng.wait_ge(q.sem, q.at("v", i))
                eng.tensor_copy(v3[:, i * T:(i + 1) * T], bank(4 + i)).then_inc(s["p3_dve_v"].sem, 1)
            meet("dve", eng)

        c3 = 12000
        pr3 = [work[:, c3 + k * 512:c3 + (k + 1) * 512] for k in range(2)]
        vs3 = [work[:, c3 + 1024 + k * SEQ:c3 + 1024 + (k + 1) * SEQ] for k in range(2)]
        sm3 = [work[:, c3 + 2048 + k * 16:c3 + 2048 + (k + 1) * 16] for k in range(2)]
        TURNS3 = (1, B // 2 - 1)
        for lot in range(2):
            def prev(e):
                return f"c3{lot - 1}_{e}" if lot else None
            steps(f"c3{lot}_pe", ["0S", "1S", "0o", "1o"], TURNS3[lot], prev("pe"))
            steps(f"c3{lot}_act", ["0k", "1k", "0e0", "0e1", "1e0", "1e1"], TURNS3[lot], prev("act"))
            steps(f"c3{lot}_dve", ["0mx", "0nb", "1mx", "1nb", "0rd", "0v0", "0v1", "1rd", "1v0", "1v1", "0x", "1x"],
                  TURNS3[lot], prev("dve"))

        kst3 = [work[:, c3 + 3072 + k * SEQ:c3 + 3072 + (k + 1) * SEQ] for k in range(2)]
        def c3_pe(lot, eng):
            st, dv, ac = s[f"c3{lot}_pe"], s[f"c3{lot}_dve"], s[f"c3{lot}_act"]
            with eng.Fori(0, TURNS3[lot]) as i:
                for a in range(2):
                    b = i * 2 + a + lot * 2 * TURNS3[0]
                    eng.wait_ge(ac.sem, ac.at(f"{a}k", i))
                    eng.wait_ge(dv.sem, i * dv.per + dv.base)
                    for c in range(2):
                        mm = eng.matmul(ps[:, a, c * SEQ:(c + 1) * SEQ], kst3[a][:, c * P:(c + 1) * P],
                                        q3[:, bass.ds(b * SEQ, SEQ)], start=True, stop=True)
                    mm.then_inc(st.sem, 1)
                for a in range(2):
                    eng.wait_ge(dv.sem, dv.at(f"{a}v1", i))
                    for c in range(2):
                        mm = eng.matmul(ps[:, 2 + a, 0:SEQ], vs3[a][:, c * P:(c + 1) * P],
                                        pr3[a][:, c * SEQ:(c + 1) * SEQ], start=(c == 0), stop=(c == 1))
                    mm.then_inc(st.sem, 1)
            meet("pe", eng)

        def c3_act(lot, eng):
            st, dv, pe = s[f"c3{lot}_act"], s[f"c3{lot}_dve"], s[f"c3{lot}_pe"]
            eng.preload_act_table(ACT.Exp)
            with eng.Fori(0, TURNS3[lot]) as i:
                for a in range(2):
                    eng.wait_ge(pe.sem, i * pe.per + pe.base)
                    eng.activation(kst3[a], k3[:, bass.ds((i * 2 + a + lot * 2 * TURNS3[0]) * SEQ, SEQ)], ACT.Copy)\
                       .then_inc(st.sem, 1)
                for a in range(2):
                    eng.wait_ge(dv.sem, dv.at(f"{a}nb", i))
                    for c in range(2):
                        eng.activation(pr3[a][:, c * SEQ:(c + 1) * SEQ], ps[:, a, c * SEQ:(c + 1) * SEQ], ACT.Exp,
                                       bias=sm3[a][:, 2 + c:3 + c], scale=SC3,
                                       accum_out=sm3[a][:, 4 + c:5 + c]).then_inc(st.sem, 1)
            meet("act", eng)

        def c3_dve(lot, eng):
            st, pe, ac = s[f"c3{lot}_dve"], s[f"c3{lot}_pe"], s[f"c3{lot}_act"]
            with eng.Fori(0, TURNS3[lot]) as i:
                for a in range(2):
                    eng.wait_ge(pe.sem, pe.at(f"{a}S", i))
                    eng.tensor_reduce(sm3[a][:, 0:2], ps[:, a, :].rearrange("p (c q) -> p c q", c=2), AX_X, ALU.max)\
                       .then_inc(st.sem, 1)
                    eng.wait_ge(st.sem, st.at(f"{a}mx", i))
                    eng.tensor_scalar(sm3[a][:, 2:4], sm3[a][:, 0:2], -SC3, None, ALU.mult).then_inc(st.sem, 1)
                for a in range(2):
                    b = i * 2 + a + lot * 2 * TURNS3[0]
                    eng.wait_ge(ac.sem, ac.at(f"{a}e1", i))
                    eng.reciprocal(sm3[a][:, 6:8], sm3[a][:, 4:6]).then_inc(st.sem, 1)
                    eng.wait_ge(st.sem, st.at(f"{a}rd", i))
                    for c in range(2):
                        eng.tensor_scalar(vs3[a][:, c * P:(c + 1) * P], v3[:, bass.ds(b * SEQ + c * P, P)],
                                          sm3[a][:, 6 + c:7 + c], None, ALU.mult).then_inc(st.sem, 1)
                for a in range(2):
                    b = i * 2 + a + lot * 2 * TURNS3[0]
                    eng.wait_ge(pe.sem, pe.at(f"{a}o", i))
                    xt = x[:, bass.ds(b * SEQ, SEQ)]
                    eng.tensor_tensor(xt, xt, ps[:, 2 + a, 0:SEQ], ALU.add).then_inc(st.sem, 1)
            meet("dve", eng)

        PHASES = ["ln0", "r0", "sf0", "ef0", "a0", "b0", "ln1", "p1", "c1", "o1", "g1",
                  "ln2", "r2", "p2", "x2", "c2", "o2", "b2",
                  "ln3", "r3", "p3", "c3, two sequences", "x3", "c3, the rest", "b3"]
        WA_FREE = PHASES.index("o1") + 2

        set_up = sem("set_up")
        bft_f32 = work[:, 4096:4096 + 4 * P]

        def clear(L, eng):
            for a in range(0, SLOTS[L], T):
                n = min(T, SLOTS[L] - a)
                eng.dma_start(xg[L][a:a + n, :].rearrange("(a p) d -> p a d", p=P),
                              zeros[:, 0:n].rearrange("p (a d) -> p a d", d=P)).then_inc(zeroed[L], 16)

        block = ctx.enter_context(nc.Block())

        @block.sync
        def _(eng):
            eng.dma_start(x[:, :], d["x"]).then_inc(ld_x, 16)
            eng.dma_start(tabs[:, 0:P], d["tabs"][:, 0:P]).then_inc(ld_x, 16)
            eng.dma_start(cols[:, :], d["cols"]).then_inc(ld_small, 16)
            eng.dma_start(tabs[:, P:], d["tabs"][:, P:]).then_inc(ld_small, 16)
            eng.dma_start(bft_f32, d["bft"]).then_inc(ld_small, 16)
            eng.dma_start(mats[:, :], d["mats"]).then_inc(ld_small, 16)
            eng.wait_ge(zeros_made, 1)
            clear(0, eng)
            eng.dma_start(yg[0][E * CAP:E * CAP + P, :], zeros[:, 0:P]).then_inc(zeroed[0], 16)
            eng.dma_start(wa[:, :], d["w0"]).then_inc(ld_w0, 16)
            eng.dma_start(wb[:, :], d["w1"]).then_inc(ld_w1, 16)
            clear(2, eng)
            clear(3, eng)
            ef0_sync(eng)
            c1_sync(eng)
            for n in met:
                eng.wait_ge(met[n], WA_FREE)
            eng.dma_start(wa[:, :], d["w23"]).then_inc(ld_w23, 16)
            x_sync(2, eng)
            c2_sync(eng)
            x_sync(3, eng)
            last = s["b3_dve"]
            for i in range(NT):
                eng.wait_ge(last.sem, last.at(f"x{i}"))
                eng.dma_start(d["out"][:, i * T:(i + 1) * T], x[:, i * T:(i + 1) * T]).then_inc(stored, 16)
            eng.wait_ge(stored, 16 * NT)

        @block.gpsimd
        def _(eng):
            eng.memset(zeros[:, :], 0.0).then_inc(zeros_made, 1)
            for q in started:
                eng.sem_inc(q, 1)
            eng.sem_inc(s["parts2_out"].sem, 48)
            for k, v in enumerate(EPSV):
                eng.memset(epst[:, k:k + 1], v * DOWN)
            eng.memset(ones16[:, :], 1.0)
            eng.memset(one8[:, :], 1.0)
            eng.memset(epst[:, 4:5], 0.5 * math.log(DOWN)).then_inc(set_up, 1)
            scatter(0, eng)
            gather(0, eng)
            for n in met:
                eng.wait_ge(met[n], PHASES.index("b0") + 2)
            for k in range(2):
                for c in range(2):
                    eng.memset(vpad[k][c], 0.0).then_inc(v_zeroed, 1)
            for L in (2, 3):
                scatter(L, eng)
                gather(L, eng)

        @block.tensor
        def _(eng):
            eng.wait_ge(set_up, 1)
            eng.wait_ge(ld_x, 32)
            meet("pe", eng)
            ln_pe(0, eng)
            eng.wait_ge(ld_small, 64)
            r_pe(0, eng)
            eng.wait_ge(ld_w0, 16)
            sf0_pe(eng)
            ef0_pe(eng)
            a0_pe(eng)
            b_pe(0, eng)
            ln_pe(1, eng)
            p1_pe(eng)
            c1_pe(eng)
            o1_pe(eng)
            g1_pe(eng)
            ln_pe(2, eng)
            r_pe(2, eng)
            p2_pe(eng)
            x_pe(2, eng)
            c2_pe(eng)
            o2_pe(eng)
            b_pe(2, eng)
            ln_pe(3, eng)
            r_pe(3, eng)
            p3_pe(eng)
            c3_pe(0, eng)
            x_pe(3, eng)
            c3_pe(1, eng)
            b_pe(3, eng)

        @block.scalar
        def _(eng):
            eng.wait_ge(set_up, 1)
            meet("act", eng)
            ln_act(0, eng)
            eng.wait_ge(ld_small, 64)
            r_act(0, eng)
            sf0_act(eng)
            ef0_act(eng)
            a0_act(eng)
            b_act(0, eng)
            ln_act(1, eng)
            p1_act(eng)
            c1_act(eng)
            meet("act", eng)
            g1_act(eng)
            ln_act(2, eng)
            r_act(2, eng)
            t2_act(eng)
            p2_act(eng)
            x_act(2, eng)
            c2_act(eng)
            o2_act(eng)
            b_act(2, eng)
            ln_act(3, eng)
            r_act(3, eng)
            meet("act", eng)
            c3_act(0, eng)
            x_act(3, eng)
            c3_act(1, eng)
            b_act(3, eng)

        @block.vector
        def _(eng):
            eng.wait_ge(set_up, 1)
            eng.wait_ge(ld_x, 32)
            meet("dve", eng)
            ln_dve(0, eng)
            eng.wait_ge(ld_small, 64)
            eng.tensor_copy(bft[:, :], bft_f32)
            r_dve(0, eng)
            sf0_dve(eng)
            ef0_dve(eng)
            a0_dve(eng)
            b_dve(0, eng)
            ln_dve(1, eng)
            p1_dve(eng)
            c1_dve(eng)
            o1_dve(eng)
            g1_dve(eng)
            ln_dve(2, eng)
            r_dve(2, eng)
            t2_dve(eng)
            p2_dve(eng)
            x_dve(2, eng)
            c2_dve(eng)
            o2_dve(eng)
            b_dve(2, eng)
            ln_dve(3, eng)
            r_dve(3, eng)
            p3_dve(eng)
            c3_dve(0, eng)
            x_dve(3, eng)
            c3_dve(1, eng)
            b_dve(3, eng)


def tables():
    import numpy as np
    f = np.float64
    t = {}
    t["ones_d"] = np.full((P, P), 1.0 / P)
    t["ident"] = np.eye(P)
    w = np.power(0.001, np.linspace(0.0, 1.0, P))[:, None]
    a = 1e-5
    s = np.arange(SEQ, dtype=f)[None, :]
    t["dec_c"], t["dec_s"] = np.exp(-a * s) * np.cos(w * s), np.exp(-a * s) * np.sin(w * s)
    t["gro_c"], t["gro_s"] = np.exp(a * s) * np.cos(w * s), np.exp(a * s) * np.sin(w * s)
    t["nxt_c"], t["nxt_s"] = np.exp(a * (s + 1)) * np.cos(w * (s + 1)), -np.exp(a * (s + 1)) * np.sin(w * (s + 1))
    keep = np.ones((P, T))
    keep[:, ::SEQ] = 0
    t["keep"] = keep
    th = 1.0 / 10000.0 ** (np.arange(0, HD, 2) / HD)
    p = np.arange(P)
    ang = (p // HD * th[(p % HD) // 2])[:, None]
    sign = np.where(p % 2 == 0, -1.0, 1.0)[:, None]
    t["cosk"], t["sink"] = np.cos(ang), sign * np.sin(ang)
    t["cosq"], t["sinq"] = t["cosk"] / HD ** 0.5, t["sink"] / HD ** 0.5
    for n in ("cosq", "sinq", "cosk", "sink"):
        t[n + "_row"] = np.tile(t[n].T, (P, 1))
    t["code"] = np.tile(E - np.arange(E), (P, 1))
    j, q = p[:, None], p[None, :]
    t["lag"] = np.maximum(q - j - 1, 0)
    t["before"] = j < q
    t["iota_q"] = np.tile(p, (P, 1))
    t["rev_j"] = (P - 1 - p)[:, None]
    t["grp"] = (j % H == q % H) / HD
    t["sel16"] = (j == q // HD)
    t["keep_t"] = np.tile(np.arange(P) % NTOK != 0, (P, 1))
    t["first_slot"] = np.tile(np.arange(E) * CAP - 1, (P, 1))
    t["starts"] = np.tile(P * np.arange(NTOK), (P, 1))
    t["tiles"] = np.tile(np.arange(MAX_TILES), (P, 1))
    t["places"] = np.tile([1, E, E * E], (P, MAX_TILES // 3))
    tabs = np.concatenate([np.asarray(t[n], np.float32).reshape(P, -1) for n, _ in TABS], axis=1)
    bft = [np.eye(P), np.where(q > j, NEG, 0.0), j <= q, np.ones((P, P))]
    return tabs, np.concatenate([np.asarray(b, np.float32) for b in bft], axis=1)


def kernel(**inputs):
    import numpy as _np
    import concourse.bacc as _bacc
    from concourse import mybir as _mybir
    from concourse.bass_utils import run_bass_kernel_spmd as _run

    a = {k: _np.asarray(v) for k, v in inputs.items()}
    cat = _np.concatenate
    swap = _np.arange(P) ^ 1
    wa1, ba1 = a["L1_attn_W_attn"], a["L1_attn_b_attn"]
    wq, wk, wv = wa1[:, 0:P], wa1[:, P:2 * P], wa1[:, 2 * P:]
    bq, bk, bv = ba1[0:P], ba1[P:2 * P], ba1[2 * P:]
    w3 = a["L3_attn_W"]
    by = _np.arange(P).reshape(H, HD).T.reshape(-1)
    m = {"z0": a["L0_attn_Wz"].T, "za0": a["L0_attn_Wza"].T, "y0": a["L0_attn_Wy"].T, "ya0": a["L0_attn_Wya"].T,
         "q1": wq, "qs1": wq[:, swap], "k1": wk, "ks1": wk[:, swap], "v1": wv, "p1": a["L1_attn_W_proj"],
         "r2": a["L2_attn_w_r"].T[:, by], "k2": a["L2_attn_w_k"].T[:, by],
         "v2": a["L2_attn_w_v"].T[:, by], "g2": a["L2_attn_w_g"].T[:, by],
         "o2": a["L2_attn_w_o"].T[by], "q3": w3[:, 0:P], "k3": w3[:, P:2 * P], "v3": w3[:, 2 * P:]}
    mats = cat([m[n] for n in MATS], axis=1)

    def rows(v, n):
        return _np.tile(v[None, :], (P, 1)) if n is None else v.reshape(n, P).T

    def below(v):
        return cat([v, _np.zeros((P - v.shape[0], v.shape[1]), v.dtype)], axis=0)

    eye = _np.eye(P, dtype=_np.float32)
    c = {"bz": rows(a["L0_attn_bz"], 1), "bza": rows(a["L0_attn_bza"], 1), "by": rows(a["L0_attn_by"], 1),
         "bya": rows(a["L0_attn_bya"], 1), "norm_w": rows(a["L0_attn_norm_w"], 1),
         "lc_re": rows(a["L0_attn_lc_re"], 1), "lc_im": rows(a["L0_attn_lc_im"], 1),
         "bq": rows(bq, 1), "bqs": rows(bq[swap], 1), "bk": rows(bk, 1), "bks": rows(bk[swap], 1),
         "bv": rows(bv, 1), "bp": rows(a["L1_attn_b_proj"], 1),
         "w1_s": rows(a["L1_ffn_w1_s"], 4), "w2_s": rows(a["L1_ffn_w2_s"], 4), "h1_s": rows(a["L1_ffn_h1_s"], 4),
         "h2_s": rows(a["L1_ffn_h2_s"], 4), "w3_s": rows(a["L1_ffn_w3_s"], 1),
         "maa_k": rows(a["L2_attn_time_maa_k"], 1), "maa_v": rows(a["L2_attn_time_maa_v"], 1),
         "maa_r": rows(a["L2_attn_time_maa_r"], 1), "maa_g": rows(a["L2_attn_time_maa_g"], 1),
         "td_ch": rows(_np.tile(a["L2_attn_time_decay"], HD), 1), "ln_g": rows(a["L2_attn_ln_g"][by], 1),
         "ln_b": rows(a["L2_attn_ln_b"][by], 1), "td_bc": rows(a["L2_attn_time_decay"], None),
         "u_bc": rows(a["L2_attn_time_faaaa"], None), "b1_2": rows(a["L2_ffn_b1"].reshape(-1), E * 4),
         "ident0": eye, "ident2": eye, "ident3": eye, "gate2": _np.zeros((P, E), _np.float32),
         "router0": a["L0_ffn_router_w"].T, "wgred2": below(a["L2_ffn_wg_red"]), "wg2": below(a["L2_ffn_wg"].T),
         "gate3": a["L3_ffn_w_gate"]}
    cols = cat([c[n] for n, _ in COLS], axis=1)

    def up(w):
        return w.transpose(1, 0, 2).reshape(P, -1)

    def down(w):
        return w.reshape(-1, P, w.shape[-1]).transpose(1, 0, 2).reshape(P, -1)

    w0 = cat([up(a["L0_ffn_rg"]), up(a["L0_ffn_ru"]), down(a["L0_ffn_rd"]), a["L0_ffn_sg"], a["L0_ffn_su"],
              down(a["L0_ffn_sd"])], axis=1)
    w1 = cat([a["L1_ffn_w1_w"].T, a["L1_ffn_w2_w"].T, down(a["L1_ffn_h1_w"].T), down(a["L1_ffn_h2_w"].T),
              down(a["L1_ffn_w3_w"].T)], axis=1)
    w23 = cat([cat([a["L2_ffn_w1"][e], down(a["L2_ffn_w2"][e]), rows(a["L2_ffn_b2"][e], None)], axis=1)
               for e in range(E)]
              + [cat([a["L3_ffn_w1"][e], a["L3_ffn_w3"][e], down(a["L3_ffn_w2"][e])], axis=1) for e in range(E)],
              axis=1)
    tabs, bft = tables()
    arrays = {"x": a["L0_attn_x"].reshape(N, P).T, "mats": mats, "cols": cols, "tabs": tabs, "bft": bft,
              "w0": w0, "w1": w1, "w23": w23}
    arrays = {k: _np.ascontiguousarray(v) for k, v in arrays.items()}

    nc = _bacc.Bacc("TRN2", target_bir_lowering=False, num_devices=1)
    d = {k: nc.dram_tensor(f"in_{k}", v.shape, _mybir.dt.from_np(v.dtype), kind="ExternalInput").ap()
         for k, v in arrays.items()}
    d["out"] = nc.dram_tensor("out", (P, N), F32, kind="ExternalOutput").ap()
    build(nc, d)
    r = _run(nc, [{f"in_{k}": v for k, v in arrays.items()}], core_ids=[0])
    return _np.ascontiguousarray(r.results[0]["out"].T).reshape(B, SEQ, P)
```
